# Optimizing a Trainium2 kernel written in Bass

```python
import numpy as np
import jax
import jax.numpy as jnp

def _softmax(x, axis=-1):
    return jax.nn.softmax(x, axis=axis)

def _gelu(x):
    return jax.nn.gelu(x, approximate=True)

def _silu(x):
    return jax.nn.silu(x)

def _sigmoid(x):
    return jax.nn.sigmoid(x)

def _layernorm(x, axis=-1, eps=1e-05):
    m = jnp.mean(x, axis=axis, keepdims=True)
    v = jnp.var(x, axis=axis, keepdims=True)
    return (x - m) / jnp.sqrt(v + eps)

def _scatter_add(tgt, idx, src, axis=0):
    return tgt.at[idx].add(src)

def _segment_sum(src, seg, n):
    return jax.ops.segment_sum(src, seg, n)
kernel_name = 'mk_adj_ffn_d2_adj_r2_8b69b6'

def setup_inputs(seed: int=0):
    np.random.seed(seed)
    _w = jnp.asarray

    def _rec_inputs():
        import jax
        import jax.numpy as jnp
        _gk = jax.random.key(seed)
        x = -0.0003929 + 0.9999 * jax.random.normal(jax.random.fold_in(_gk, 1), (32, 256, 128), jnp.float32)
        _a = jax.random.bernoulli(jax.random.fold_in(_gk, 2), 0.015625, (256, 256))
        _af = _a.astype(jnp.float32)
        _af = _af / jnp.maximum(_af.sum(-1, keepdims=True), 1.0)
        adj = _af
        return (x, adj)
    x, adj = _rec_inputs()

    def _L0_gnn_setup():
        import jax, jax.numpy as jnp
        import numpy as np
        B, N, D = (128, 256, 128)

        def _make_adj(k):
            a = jax.random.uniform(k, (N, N), dtype=jnp.float32)
            mask = (jax.random.uniform(jax.random.fold_in(k, 1), (N, N)) < 4.0 / N).astype(jnp.float32)
            a = a * mask
            return a / (a.sum(axis=1, keepdims=True) + 1e-08)
        key = jax.random.key(seed)
        ks = jax.random.split(key, 8)
        x = jax.random.normal(ks[0], (B, N, D), dtype=jnp.float32)
        adj_in = _make_adj(ks[1])
        adj_out = _make_adj(ks[2])
        bias_in = jax.random.normal(ks[3], (N, D), dtype=jnp.float32) * 0.02
        bias_out = jax.random.normal(ks[4], (N, D), dtype=jnp.float32) * 0.02
        gate_w_in = jax.random.normal(ks[5], (D, 1), dtype=jnp.float32) * 0.02
        gate_b_in = jnp.zeros((N, 1), dtype=jnp.float32)
        gate_w_out = jax.random.normal(ks[6], (D, 1), dtype=jnp.float32) * 0.02
        gate_b_out = jnp.zeros((N, 1), dtype=jnp.float32)
        loop_gate = jax.random.normal(ks[7], (D, 1), dtype=jnp.float32) * 0.02
        return {'x': x, 'adj_in': adj_in, 'adj_out': adj_out, 'bias_in': bias_in, 'bias_out': bias_out, 'gate_w_in': gate_w_in, 'gate_b_in': gate_b_in, 'gate_w_out': gate_w_out, 'gate_b_out': gate_b_out, 'loop_gate': loop_gate}
    _L0_gnn_all = _L0_gnn_setup()
    _L0_gnn_in = {k: v for k, v in _L0_gnn_all.items() if k in ('bias_in', 'bias_out', 'gate_w_in', 'gate_b_in', 'gate_w_out', 'gate_b_out', 'loop_gate')}
    del _L0_gnn_all

    def _L0_ffn_setup():
        import jax, jax.numpy as jnp
        import numpy as np
        from jax import lax
        key = jax.random.key(seed)
        B, T, I, H = (64, 1024, 128, 128)
        ks = jax.random.split(key, 13)
        s = 1.0 / np.sqrt(H)

        def w(k, shape):
            return jax.random.uniform(k, shape, jnp.float32, -s, s)
        return {'x': jax.random.normal(ks[0], (B, T, I), jnp.float32), 'U_i': w(ks[1], (I, H)), 'V_i': w(ks[2], (H, H)), 'b_i': w(ks[3], (H,)), 'U_f': w(ks[4], (I, H)), 'V_f': w(ks[5], (H, H)), 'b_f': w(ks[6], (H,)), 'U_c': w(ks[7], (I, H)), 'V_c': w(ks[8], (H, H)), 'b_c': w(ks[9], (H,)), 'U_o': w(ks[10], (I, H)), 'V_o': w(ks[11], (H, H)), 'b_o': w(ks[12], (H,))}
    _L0_ffn_all = _L0_ffn_setup()
    _L0_ffn_in = {k: v for k, v in _L0_ffn_all.items() if k in ('U_i', 'V_i', 'b_i', 'U_f', 'V_f', 'b_f', 'U_c', 'V_c', 'b_c', 'U_o', 'V_o', 'b_o')}
    del _L0_ffn_all

    def _L1_gnn_setup():
        import jax, jax.numpy as jnp
        import numpy as np
        EPS = 1e-05

        def _batchnorm(x, gamma, beta):
            mu = jnp.mean(x, axis=0)
            var = jnp.var(x, axis=0)
            return (x - mu) * jax.lax.rsqrt(var + EPS) * gamma + beta
        key = jax.random.key(seed)
        ks = jax.random.split(key, 4)
        b, n, d, h, o = (32, 1024, 128, 256, 128)
        features = jax.random.normal(ks[0], (b, n, d), dtype=jnp.float32)
        A = jax.random.uniform(ks[1], (n, n), dtype=jnp.float32)
        lim1 = float(np.sqrt(6.0 / (d + h)))
        W1 = jax.random.uniform(ks[2], (h, d), minval=-lim1, maxval=lim1, dtype=jnp.float32)
        b1 = jnp.zeros((h,), jnp.float32)
        lim2 = float(np.sqrt(6.0 / (h + o)))
        W2 = jax.random.uniform(ks[3], (o, h), minval=-lim2, maxval=lim2, dtype=jnp.float32)
        b2 = jnp.zeros((o,), jnp.float32)
        g1 = jnp.ones((h,), jnp.float32)
        be1 = jnp.zeros((h,), jnp.float32)
        g2 = jnp.ones((o,), jnp.float32)
        be2 = jnp.zeros((o,), jnp.float32)
        return {'features': features, 'A': A, 'W1': W1, 'b1': b1, 'g1': g1, 'be1': be1, 'W2': W2, 'b2': b2, 'g2': g2, 'be2': be2}
    _L1_gnn_all = _L1_gnn_setup()
    _L1_gnn_in = {k: v for k, v in _L1_gnn_all.items() if k in ('W1', 'b1', 'g1', 'be1', 'W2', 'b2', 'g2', 'be2')}
    del _L1_gnn_all

    def _L1_ffn_setup():
        import jax, jax.numpy as jnp
        import numpy as np
        TOP_K = 2
        key = jax.random.key(seed)
        ks = jax.random.split(key, 4)
        B, L, D, H, E = (8, 2048, 128, 512, 8)
        s = 0.02
        return {'x': jax.random.normal(ks[0], (B, L, D), jnp.float32), 'Wg': jax.random.normal(ks[1], (D, E), jnp.float32) * s, 'bg': jnp.zeros((E,), jnp.float32), 'W1': jax.random.normal(ks[2], (E, D, H), jnp.float32) * s, 'b1': jnp.zeros((E, H), jnp.float32), 'W2': jax.random.normal(ks[3], (E, H, D), jnp.float32) * s, 'b2': jnp.zeros((E, D), jnp.float32)}
    _L1_ffn_all = _L1_ffn_setup()
    _L1_ffn_in = {k: v for k, v in _L1_ffn_all.items() if k in ('Wg', 'bg', 'W1', 'b1', 'W2', 'b2')}
    del _L1_ffn_all
    return {'x': x, 'adj': adj, 'L0_gnn_bias_in': _L0_gnn_in['bias_in'], 'L0_gnn_bias_out': _L0_gnn_in['bias_out'], 'L0_gnn_gate_w_in': _L0_gnn_in['gate_w_in'], 'L0_gnn_gate_b_in': _L0_gnn_in['gate_b_in'], 'L0_gnn_gate_w_out': _L0_gnn_in['gate_w_out'], 'L0_gnn_gate_b_out': _L0_gnn_in['gate_b_out'], 'L0_gnn_loop_gate': _L0_gnn_in['loop_gate'], 'L0_ffn_U_i': _L0_ffn_in['U_i'], 'L0_ffn_V_i': _L0_ffn_in['V_i'], 'L0_ffn_b_i': _L0_ffn_in['b_i'], 'L0_ffn_U_f': _L0_ffn_in['U_f'], 'L0_ffn_V_f': _L0_ffn_in['V_f'], 'L0_ffn_b_f': _L0_ffn_in['b_f'], 'L0_ffn_U_c': _L0_ffn_in['U_c'], 'L0_ffn_V_c': _L0_ffn_in['V_c'], 'L0_ffn_b_c': _L0_ffn_in['b_c'], 'L0_ffn_U_o': _L0_ffn_in['U_o'], 'L0_ffn_V_o': _L0_ffn_in['V_o'], 'L0_ffn_b_o': _L0_ffn_in['b_o'], 'L1_gnn_W1': _L1_gnn_in['W1'], 'L1_gnn_b1': _L1_gnn_in['b1'], 'L1_gnn_g1': _L1_gnn_in['g1'], 'L1_gnn_be1': _L1_gnn_in['be1'], 'L1_gnn_W2': _L1_gnn_in['W2'], 'L1_gnn_b2': _L1_gnn_in['b2'], 'L1_gnn_g2': _L1_gnn_in['g2'], 'L1_gnn_be2': _L1_gnn_in['be2'], 'L1_ffn_Wg': _L1_ffn_in['Wg'], 'L1_ffn_bg': _L1_ffn_in['bg'], 'L1_ffn_W1': _L1_ffn_in['W1'], 'L1_ffn_b1': _L1_ffn_in['b1'], 'L1_ffn_W2': _L1_ffn_in['W2'], 'L1_ffn_b2': _L1_ffn_in['b2']}

def reference(x, adj, L0_gnn_bias_in, L0_gnn_bias_out, L0_gnn_gate_w_in, L0_gnn_gate_b_in, L0_gnn_gate_w_out, L0_gnn_gate_b_out, L0_gnn_loop_gate, L0_ffn_U_i, L0_ffn_V_i, L0_ffn_b_i, L0_ffn_U_f, L0_ffn_V_f, L0_ffn_b_f, L0_ffn_U_c, L0_ffn_V_c, L0_ffn_b_c, L0_ffn_U_o, L0_ffn_V_o, L0_ffn_b_o, L1_gnn_W1, L1_gnn_b1, L1_gnn_g1, L1_gnn_be1, L1_gnn_W2, L1_gnn_b2, L1_gnn_g2, L1_gnn_be2, L1_ffn_Wg, L1_ffn_bg, L1_ffn_W1, L1_ffn_b1, L1_ffn_W2, L1_ffn_b2):
    import jax
    import jax.numpy as jnp

    def _L0_gnn_ref(x, adj_in, adj_out, bias_in, bias_out, gate_w_in, gate_b_in, gate_w_out, gate_b_out, loop_gate):
        import jax, jax.numpy as jnp
        import numpy as np
        B, N, D = (128, 256, 128)

        def _make_adj(k):
            a = jax.random.uniform(k, (N, N), dtype=jnp.float32)
            mask = (jax.random.uniform(jax.random.fold_in(k, 1), (N, N)) < 4.0 / N).astype(jnp.float32)
            a = a * mask
            return a / (a.sum(axis=1, keepdims=True) + 1e-08)
        msg_in = (jnp.einsum('nm,bmd->bnd', adj_in, x) + bias_in) * jax.nn.sigmoid(x @ gate_w_in + gate_b_in)
        msg_out = (jnp.einsum('nm,bmd->bnd', adj_out, x) + bias_out) * jax.nn.sigmoid(x @ gate_w_out + gate_b_out)
        msg_loop = x * jax.nn.sigmoid(x @ loop_gate)
        return jax.nn.relu(msg_in + msg_out + msg_loop)

    def _L0_ffn_ref(x, U_i, V_i, b_i, U_f, V_f, b_f, U_c, V_c, b_c, U_o, V_o, b_o):
        import jax, jax.numpy as jnp
        import numpy as np
        from jax import lax
        B, T, _ = x.shape
        H = U_i.shape[1]
        xt = jnp.swapaxes(x, 0, 1)
        xi = xt @ U_i + b_i
        xf = xt @ U_f + b_f
        xg = xt @ U_c + b_c
        xo = xt @ U_o + b_o
        h0 = jnp.zeros((B, H), x.dtype)
        c0 = jnp.zeros((B, H), x.dtype)

        def step(carry, xs):
            h, c = carry
            xi_t, xf_t, xg_t, xo_t = xs
            i_t = jax.nn.sigmoid(xi_t + h @ V_i)
            f_t = jax.nn.sigmoid(xf_t + h @ V_f)
            g_t = jnp.tanh(xg_t + h @ V_c)
            o_t = jax.nn.sigmoid(xo_t + h @ V_o)
            c_new = h * c + i_t * g_t
            h_new = o_t * jnp.tanh(c_new)
            return ((h_new, c_new), h_new)
        (_, _), hs = lax.scan(step, (h0, c0), (xi, xf, xg, xo))
        return jnp.swapaxes(hs, 0, 1)

    def _L1_gnn_ref(features, A, W1, b1, g1, be1, W2, b2, g2, be2):
        import jax, jax.numpy as jnp
        import numpy as np
        EPS = 1e-05

        def _batchnorm(x, gamma, beta):
            mu = jnp.mean(x, axis=0)
            var = jnp.var(x, axis=0)
            return (x - mu) * jax.lax.rsqrt(var + EPS) * gamma + beta
        b, n, d = features.shape
        A_norm = A + jnp.eye(n, dtype=A.dtype)
        deg = jnp.sum(A_norm, axis=0) + jnp.sum(A_norm, axis=1) - jnp.diagonal(A_norm)
        dinv = jax.lax.rsqrt(deg)
        A_hat = A_norm * dinv[:, None] * dinv[None, :]
        agg = jnp.einsum('nm,bmd->bnd', A_hat, features)
        x = agg.reshape(-1, d)
        h = jax.nn.relu(_batchnorm(x @ W1.T + b1, g1, be1))
        out = h @ W2.T + b2
        out = _batchnorm(out, g2, be2)
        return out.reshape(b, n, -1)

    def _L1_ffn_ref(x, Wg, bg, W1, b1, W2, b2):
        import jax, jax.numpy as jnp
        import numpy as np
        TOP_K = 2
        B, L, D = x.shape
        E = W1.shape[0]
        xf = x.reshape(-1, D)
        gate_logits = xf @ Wg + bg
        top_w, top_i = jax.lax.top_k(gate_logits, TOP_K)
        top_w = jax.nn.softmax(top_w, axis=-1)
        w_dense = jnp.sum(jax.nn.one_hot(top_i, E, dtype=xf.dtype) * top_w[..., None], axis=1)
        out = jnp.zeros_like(xf)
        for e in range(E):
            h = jax.nn.gelu(xf @ W1[e] + b1[e], approximate=False)
            out = out + w_dense[:, e:e + 1] * (h @ W2[e] + b2[e])
        return out.reshape(B, L, D)
    x = x + _L0_gnn_ref(_layernorm(x, axis=-1), adj, adj, L0_gnn_bias_in, L0_gnn_bias_out, L0_gnn_gate_w_in, L0_gnn_gate_b_in, L0_gnn_gate_w_out, L0_gnn_gate_b_out, L0_gnn_loop_gate)
    x = x + _L0_ffn_ref(_layernorm(x, axis=-1), L0_ffn_U_i, L0_ffn_V_i, L0_ffn_b_i, L0_ffn_U_f, L0_ffn_V_f, L0_ffn_b_f, L0_ffn_U_c, L0_ffn_V_c, L0_ffn_b_c, L0_ffn_U_o, L0_ffn_V_o, L0_ffn_b_o)
    x = x + _L1_gnn_ref(_layernorm(x, axis=-1), adj, L1_gnn_W1, L1_gnn_b1, L1_gnn_g1, L1_gnn_be1, L1_gnn_W2, L1_gnn_b2, L1_gnn_g2, L1_gnn_be2)
    x = x + _L1_ffn_ref(_layernorm(x, axis=-1), L1_ffn_Wg, L1_ffn_bg, L1_ffn_W1, L1_ffn_b1, L1_ffn_W2, L1_ffn_b2)
    return x

_drawn_inputs = setup_inputs


def setup_inputs(seed=0):
    import zlib

    import numpy as np

    out = dict(_drawn_inputs(seed))
    spreads = {'L0_gnn_gate_b_in': (0.0, 0.8),
     'L0_gnn_gate_b_out': (0.0, 0.8),
     'L1_gnn_b1': (0.0, 0.8),
     'L1_gnn_g1': (1.0, 0.2),
     'L1_gnn_be1': (0.0, 0.1),
     'L1_gnn_b2': (0.0, 0.8),
     'L1_gnn_g2': (1.0, 0.2),
     'L1_gnn_be2': (0.0, 0.1),
     'L1_ffn_bg': (0.0, 0.1),
     'L1_ffn_b1': (0.0, 0.789),
     'L1_ffn_b2': (0.0, 0.1)}
    factors = {'L0_gnn_bias_in': 8.0,
     'L0_gnn_bias_out': 8.0,
     'L0_gnn_gate_w_in': 2.838,
     'L0_gnn_gate_w_out': 3.128,
     'L0_ffn_V_i': 8.0,
     'L0_ffn_b_i': 8.0,
     'L0_ffn_V_c': 4.572,
     'L0_ffn_b_c': 6.082,
     'L0_ffn_V_o': 8.0,
     'L0_ffn_b_o': 8.0}
    for name, (base, spread) in spreads.items():
        noise = np.random.default_rng([zlib.crc32(name.encode()), seed]).standard_normal(out[name].shape)
        drawn = base * np.exp(spread * noise) if base else spread * noise
        out[name] = jnp.asarray(drawn.astype(out[name].dtype))
    for name, factor in factors.items():
        out[name] = (out[name] * factor).astype(out[name].dtype)
    return out
```

```python
from contextlib import ExitStack

import concourse.bass as bass
from concourse import mybir

F32 = mybir.dt.float32
I32 = mybir.dt.int32
ALU = mybir.AluOpType
ACT = mybir.ActivationFunctionType
AX = mybir.AxisListType

B, N, D = 32, 256, 128
P = 128
C = N // P
TILES = C * B
Q = 4
GROUPS = TILES // Q
BANK = Q * P
H1 = 256
HC = H1 // P
E, F = 8, 512
J = F // P
GATES = 3
STEPS = BANK // B
BLOCKS = N // STEPS
EPS = 1e-5
RSQRT_MAGIC = float(0x5F3759DF)
NEWTON = 3


def peeled(eng, n, body):
    body(0)
    if n > 1:
        with eng.Fori(1, n) as i:
            body(i)


def build(nc, x, adj, bias_in, bias_out, gate_w_in, gate_b_in, gate_w_out, gate_b_out, loop_gate,
          U_i, V_i, b_i, U_c, V_c, b_c, U_o, V_o, b_o, W1, b1, g1, be1, W2, b2, g2, be2,
          Wg, bg, mW1, mb1, mW2, mb2, out):
    x_v = x.rearrange("b (c p) d -> p c b d", p=P)
    out_v = out.rearrange("b (c p) d -> p c b d", p=P)
    ctx = ExitStack()
    with ctx:
        def sb(name, shape, dt=F32):
            return ctx.enter_context(nc.sbuf_tensor(name, shape, dt))

        def sem(name):
            return ctx.enter_context(nc.semaphore(name))

        rows = sb("rows", [P, TILES, D])
        nrm = sb("nrm", [P, TILES, D])
        cols = sb("cols", [P, TILES * P])
        hid = sb("hid", [P, HC * TILES * P])
        hs = hid[:, 0:(N + 1) * B].rearrange("p (t b) -> p t b", b=B)
        h1 = hid[:, :].rearrange("p (c r) -> p c r", c=HC)
        w1e = hid[:, 0:E * F].rearrange("p (e f) -> p e f", e=E)
        w2e = hid[:, E * F:2 * E * F].rearrange("p (e j d) -> p e j d", e=E, j=J)
        b2diag = hid[:, 2 * E * F:2 * E * F + 16 * P].rearrange("p (k d) -> p k d", k=16)
        routeT = hid[:, 2 * E * F + 16 * P:2 * E * F + 20 * P].rearrange("p (k t) -> p k t", k=4)
        hbuf_at = 2 * E * F + 20 * P
        hbuf = hid[:, hbuf_at:hbuf_at + 2 * J * BANK].rearrange("p (u j t) -> p u j t", u=2, j=J)

        ident = sb("ident", [P, P])
        ones = sb("ones", [1, BANK])
        a_rows = sb("a_rows", [P, C, N])
        s_rows = sb("s_rows", [P, C, N])
        a_T = sb("a_T", [P, C, N])
        ah_T = sb("ah_T", [P, C, N])
        bin_sb = sb("bin_sb", [P, C, D])
        bout_sb = sb("bout_sb", [P, C, D])
        gw = sb("gw", [P, 3])
        gb = sb("gb", [P, 2, C])
        gbh = sb("gbh", [P, 2, C])
        gates = sb("gates", [P, 4, TILES])
        U = sb("U", [P, GATES, P])
        V = sb("V", [P, GATES, P])
        bl = sb("bl", [1, GATES * P])
        w_in = sb("w_in", [P, 4, P])
        w_T = sb("w_T", [P, 4, P])
        bn1 = sb("bn1", [P, 3, HC])
        bn2 = sb("bn2", [P, 3])
        mb1_rows = sb("mb1_rows", [E * J, P])
        mb1_T = sb("mb1_T", [P, E * J])
        wg_sb = sb("wg_sb", [P, E])
        bg_sb = sb("bg_sb", [P, E])
        stats = sb("stats", [P, TILES, 6])
        bst = sb("bst", [P, HC + 1, GROUPS, 6])
        tmp = sb("tmp", [P, 4, TILES])
        rstd = sb("rstd", [P, TILES])
        nmr = sb("nmr", [P, TILES])
        small = sb("small", [P, 16])
        mv = sb("mv", [P, HC + 1, 2])
        bsc = sb("bsc", [P, HC + 1])
        bsh = sb("bsh", [P, HC + 1])
        work = sb("work", [P, 2, Q, D])
        T = sb("T", [P, 3, B])
        hc = sb("hc", [P, B])
        ig = sb("ig", [P, B])
        cell = sb("cell", [P, B])
        tc = sb("tc", [P, B])
        logit = sb("logit", [P, TILES, E])
        m1 = sb("m1", [P, TILES])
        m2 = sb("m2", [P, TILES])
        pos = sb("pos", [P, E])
        ps = ctx.enter_context(nc.psum_tensor("ps", [P, 8, BANK], F32))
        route = nrm[:, 0:4, :].rearrange("p a b -> p (a b)").rearrange("p (g e) -> p g e", e=E)
        mk = [nrm[:, 4 + 4 * k:8 + 4 * k, :].rearrange("p a b -> p (a b)").rearrange(
            "p (g e) -> p g e", e=E) for k in range(3)]

        ld_x = [sem(f"ld_x{n}") for n in range(8)]
        ld_adj = sem("ld_adj")
        ld_gnn = sem("ld_gnn")
        ld_lstm = sem("ld_lstm")
        ld_bn = sem("ld_bn")
        ld_small = sem("ld_small")
        ld_moe = sem("ld_moe")
        ld_diag = sem("ld_diag")
        zero_done = sem("zero_done")
        ident_done = sem("ident_done")
        consts = sem("consts")
        dch = sem("dch")
        prep_T = sem("prep_T")
        prep_used = sem("prep_used")
        s_scaled = sem("s_scaled")
        half_bias = sem("half_bias")
        stat_done = [sem(f"stat_done{n}") for n in range(4)]
        nrm_v = [sem(f"nrm_v{n}") for n in range(4)]
        nrm_s = [sem(f"nrm_s{n}") for n in range(4)]
        tp = [sem(f"tp{n}") for n in range(5)]
        tp_v = [sem(f"tp_v{n}") for n in range(5)]
        tp_s = [sem(f"tp_s{n}") for n in range(5)]
        gate_ps = sem("gate_ps")
        gate_th = sem("gate_th")
        gate_done = sem("gate_done")
        agg = sem("agg")
        agg_used = sem("agg_used")
        s1_act = sem("s1_act")
        s1_free = sem("s1_free")
        mixed = sem("mixed")
        mstep = sem("mstep")
        lstm_w = sem("lstm_w")
        first_in = sem("first_in")
        z_ig = sem("z_ig")
        z_o = sem("z_o")
        t_ig = sem("t_ig")
        t_o = sem("t_o")
        t_c = sem("t_c")
        c_done = sem("c_done")
        c_new = sem("c_new")
        h_done = sem("h_done")
        x2_done = sem("x2_done")
        ga_v = sem("ga_v")
        ga_s = sem("ga_s")
        ga = sem("ga")
        hp = sem("hp")
        hp_ev = sem("hp_ev")
        bn1_done = sem("bn1_done")
        relu_done = sem("relu_done")
        op = sem("op")
        op_ev = sem("op_ev")
        bn2_done = sem("bn2_done")
        y_v = sem("y_v")
        y_s = sem("y_s")
        x3_done = sem("x3_done")
        lg = sem("lg")
        lg_exp = sem("lg_exp")
        lg_dif = sem("lg_dif")
        route_done = sem("route_done")
        rT = sem("rT")
        rT_ev = sem("rT_ev")
        b2_ps = sem("b2_ps")
        b2_added = sem("b2_added")
        up = sem("up")
        gelu = sem("gelu")
        down = sem("down")
        accd = sem("accd")
        stored = sem("stored")

        block = ctx.enter_context(nc.Block())

        @block.sync
        def _(sp):
            for n in range(8):
                c, b0 = n // 4, 8 * (n % 4)
                sp.dma_start(rows[:, c * B + b0:c * B + b0 + 8, :],
                             x_v[:, c, b0:b0 + 8, :]).then_inc(ld_x[n], 16)
            sp.wait_ge(op, GROUPS)
            sp.wait_ge(zero_done, 1)
            for e in range(E):
                sp.dma_start(w1e[:, e, :], mW1[e]).then_inc(ld_moe, 16)
            for e in range(E):
                sp.dma_start(w2e[:, e, :, :],
                             mW2[e].rearrange("(j p) d -> p j d", p=P)).then_inc(ld_moe, 16)
            for k in range(16):
                sp.dma_start(b2diag[E * k:E * k + E, k, :], mb2).then_inc(ld_diag, 16)
            for q in range(GROUPS):
                sp.wait_ge(accd, E * (q + 1))
                c, b0 = q // 8, Q * (q % 8)
                sp.dma_start(out_v[:, c, b0:b0 + Q, :],
                             rows[:, Q * q:Q * q + Q, :]).then_inc(stored, 16)
            sp.wait_ge(stored, 16 * GROUPS)

        @block.gpsimd
        def _(pool):
            nc.gpsimd.memset(ident[:, :], 0.0).then_inc(consts, 1)
            nc.gpsimd.memset(ones[:, :], 1.0).then_inc(consts, 1)
            nc.gpsimd.memset(hs[:, 0, :], 0.0).then_inc(consts, 1)
            nc.gpsimd.memset(cell[:, :], 0.0).then_inc(consts, 1)
            nc.gpsimd.iota(pos[:, :], [[-1, E]], base=E, channel_multiplier=0,
                           allow_small_or_imprecise_dtypes=True).then_inc(consts, 1)
            pool.wait_ge(consts, 1)
            nc.gpsimd.affine_select(out=ident[:, :], in_=ident[:, :], compare_op=ALU.not_equal, fill=1.0,
                                    base=0, pattern=[[-1, P]], channel_multiplier=1).then_inc(ident_done, 1)
            pool.wait_ge(op, GROUPS)
            nc.gpsimd.memset(b2diag[:, :, :], 0.0).then_inc(zero_done, 1)

        def cols_view(c, i, by_time):
            if not by_time:
                return cols[:, bass.ds(BANK * i + 8 * c * BANK, BANK)]
            v = cols[:, :].rearrange("p (t b) -> p b t", b=B)
            return v[:, bass.ds(Q * i, Q), c * P:(c + 1) * P]

        @block.scalar
        def _(act):
            act.dma_start(a_rows[:, :, :], adj.rearrange("(c p) m -> p c m", p=P)).then_inc(ld_adj, 16)
            for k, w in enumerate((gate_w_in, gate_w_out, loop_gate)):
                act.dma_start(gw[:, k:k + 1], w).then_inc(ld_gnn, 16)
            for k, w in enumerate((gate_b_in, gate_b_out)):
                act.dma_start(gb[:, k, :], w.rearrange("(c p) a -> p (c a)", p=P),
                              allow_slow_non_contiguous=True).then_inc(ld_gnn, 16)
            act.dma_start(bin_sb[:, :, :], bias_in.rearrange("(c p) d -> p c d", p=P)).then_inc(ld_gnn, 16)
            act.dma_start(bout_sb[:, :, :], bias_out.rearrange("(c p) d -> p c d", p=P)).then_inc(ld_gnn, 16)
            for k, (u, v, b) in enumerate(((U_i, V_i, b_i), (U_c, V_c, b_c), (U_o, V_o, b_o))):
                act.dma_start(U[:, k, :], u).then_inc(ld_lstm, 16)
                act.dma_start(V[:, k, :], v).then_inc(ld_lstm, 16)
                act.dma_start(bl[0:1, k * P:(k + 1) * P],
                              b.rearrange("(a n) -> a n", a=1)).then_inc(ld_lstm, 16)
            act.dma_start(w_in[:, 0:2, :], W1.rearrange("(c p) d -> p c d", p=P)).then_inc(ld_bn, 16)
            act.dma_start(w_in[:, 2:4, :], W2.rearrange("o (c h) -> o c h", h=P)).then_inc(ld_bn, 16)
            act.dma_start(mb1_rows[:, :], mb1.rearrange("e (j p) -> (e j) p", p=P)).then_inc(ld_bn, 16)
            for k, v in enumerate((b1, g1, be1)):
                act.dma_start(bn1[:, k, :], v.rearrange("(c p) -> p c", p=P),
                              allow_slow_non_contiguous=True).then_inc(ld_small, 16)
            for k, v in enumerate((b2, g2, be2)):
                act.dma_start(bn2[:, k:k + 1], v.rearrange("(p a) -> p a", a=1)).then_inc(ld_small, 16)
            act.dma_start(wg_sb[:, :], Wg).then_inc(ld_small, 16)
            act.dma_start(bg_sb[:, :], bg.rearrange("(a n) -> a n", a=1).to_broadcast([P, E])).then_inc(ld_small, 16)

            def normalise(n):
                act.wait_ge(stat_done[n], 1)
                with act.Fori(0, GROUPS // 2) as i:
                    for u in range(Q):
                        g = 2 * Q * i + Q + u
                        last = nc.scalar.activation(
                            nrm[:, bass.ds(g, 1), :], rows[:, bass.ds(g, 1), :], ACT.Identity,
                            bias=nmr[:, bass.ds(g, 1)], scale=rstd[:, bass.ds(g, 1)])
                    last.then_inc(nrm_s[n], 1)

            def copy_out(n, by_time=False):
                for c in range(C):
                    with act.Fori(0, 2) as i:
                        for u in (1, 3):
                            act.wait_ge(tp[n], 8 * c + 4 * i + (u + 1))
                            nc.scalar.copy(cols_view(c, 4 * i + u, by_time), ps[:, 4 + u, :] if not by_time
                                           else ps[:, 4 + u, :].rearrange("p (b t) -> p b t", b=Q)
                                           ).then_inc(tp_s[n], 1)

            normalise(0)
            copy_out(0)
            act.wait_ge(gate_ps, 1)
            act.wait_ge(half_bias, 1)
            lgates = ps[:, 0, 0:3 * TILES].rearrange("p (g k) -> p k g", k=3)
            for k in range(3):
                for c in range(C):
                    last = nc.scalar.activation(
                        gates[:, k, c * B:(c + 1) * B], lgates[:, k, c * B:(c + 1) * B], ACT.Tanh,
                        scale=0.5, bias=gbh[:, k, c:c + 1] if k < 2 else 0.0)
            last.then_inc(gate_th, 1)
            act.wait_ge(gate_done, 1)
            for c in range(C):
                def scaled_bias(i):
                    for u in range(2):
                        if c or not isinstance(i, int):
                            act.wait_ge(s1_free, 8 * c + 2 * i + (u - 1))
                        for t in range(Q):
                            g = c * B + 2 * Q * i + (Q * u + t)
                            last = nc.scalar.activation(work[:, u, t, :], bout_sb[:, c, :], ACT.Identity,
                                                        scale=gates[:, 1, bass.ds(g, 1)])
                        last.then_inc(s1_act, 1)
                peeled(act, 4, scaled_bias)
            normalise(1)
            copy_out(1, by_time=True)

            def steps(i, base=0):
                for s in range(2 * STEPS):
                    bank = 3 * (s // STEPS)
                    col = (s % STEPS) * B
                    t = 2 * STEPS * i + s
                    act.wait_ge(z_ig, t + 1)
                    nc.scalar.activation(T[:, 0:2, :], ps[:, bank:bank + 2, col:col + B],
                                         ACT.Tanh).then_inc(t_ig, 1)
                    act.wait_ge(z_o, t + 1)
                    nc.scalar.activation(T[:, 2, :], ps[:, bank + 2, col:col + B],
                                         ACT.Tanh).then_inc(t_o, 1)
                    act.wait_ge(c_new, t + 1)
                    nc.scalar.activation(tc[:, :], cell[:, :], ACT.Tanh, scale=0.5).then_inc(t_c, 1)
            with act.Fori(0, BLOCKS // 2) as i:
                steps(i)

            normalise(2)
            with act.Fori(0, 4) as i:
                for u in (1, 3):
                    act.wait_ge(ga, 4 * i + (u + 1))
                    nc.scalar.copy(cols[:, bass.ds(BANK * 4 * i + BANK * u, BANK)],
                                   ps[:, 4 + u, :]).then_inc(ga_s, 1)
            act.wait_ge(ld_small, 128)

            def hidden(i):
                for k in range(HC):
                    act.wait_ge(hp, HC * i + (k + 1))
                    nc.scalar.activation(h1[:, k, bass.ds(BANK * i, BANK)], ps[:, k, :], ACT.Identity,
                                         bias=bn1[:, 0, k:k + 1]).then_inc(hp_ev, 1)
            with act.Fori(0, GROUPS) as i:
                hidden(i)
            act.wait_ge(bn1_done, 1)
            with act.Fori(0, GROUPS) as i:
                for k in range(HC):
                    v = h1[:, k, bass.ds(BANK * i, BANK)]
                    nc.scalar.activation(v, v, ACT.Relu, bias=bsh[:, k:k + 1],
                                         scale=bsc[:, k:k + 1]).then_inc(relu_done, 1)
            act.wait_ge(bn2_done, 1)
            with act.Fori(0, GROUPS // 2) as i:
                v = cols[:, bass.ds(2 * BANK * i + BANK, BANK)]
                nc.scalar.activation(v, v, ACT.Identity, bias=bsh[:, HC:HC + 1],
                                     scale=bsc[:, HC:HC + 1]).then_inc(y_s, 1)
            normalise(3)
            copy_out(3)
            act.wait_ge(lg_dif, 1)
            nc.scalar.activation(m2[:, :], m2[:, :], ACT.Exp).then_inc(lg_exp, 1)

            def experts(q):
                for e in range(E):
                    u = e % 2
                    if not (isinstance(q, int) and e < 2):
                        act.wait_ge(down, E * q + (e - 1))
                    for j in range(J):
                        act.wait_ge(up, E * J * q + (J * e + j + 1))
                        nc.scalar.activation(hbuf[:, u, j, :], ps[:, j, :], ACT.Gelu,
                                             bias=mb1_T[:, J * e + j:J * e + j + 1]).then_inc(gelu, 1)
            peeled(act, GROUPS, experts)

        @block.vector
        def _(dve):
            chain = [0]

            def link(ins, times=1):
                chain[0] += times
                ins.then_inc(dch, 1)
                dve.wait_ge(dch, chain[0])

            def rsqrt(y, v, t):
                link(nc.vector.tensor_scalar(t.bitcast(I32), v.bitcast(I32), 1, None,
                                             ALU.logical_shift_right))
                link(nc.vector.tensor_scalar(y.bitcast(I32), t.bitcast(I32), -1.0, RSQRT_MAGIC,
                                             ALU.mult, ALU.add))
                for _ in range(NEWTON):
                    link(nc.vector.scalar_tensor_tensor(out=t, in0=y, scalar=-0.5, in1=y,
                                                        op0=ALU.mult, op1=ALU.mult))
                    link(nc.vector.tensor_tensor(t, t, v, ALU.mult))
                    link(nc.vector.scalar_tensor_tensor(out=y, in0=t, scalar=1.5, in1=y,
                                                        op0=ALU.add, op1=ALU.mult))

            def row_stats(n):
                me, qe = stats[:, :, 1], stats[:, :, 2]
                mo, qo = stats[:, :, 4], stats[:, :, 5]
                link(nc.vector.tensor_tensor(tmp[:, 0, :], me, mo, ALU.subtract))
                link(nc.vector.tensor_tensor(tmp[:, 1, :], qe, qo, ALU.add))
                link(nc.vector.tensor_tensor(tmp[:, 0, :], tmp[:, 0, :], tmp[:, 0, :], ALU.mult))
                link(nc.vector.tensor_scalar(tmp[:, 1, :], tmp[:, 1, :], 1.0 / D, EPS, ALU.mult, ALU.add))
                link(nc.vector.scalar_tensor_tensor(out=tmp[:, 2, :], in0=tmp[:, 0, :], scalar=0.25,
                                                    in1=tmp[:, 1, :], op0=ALU.mult, op1=ALU.add))
                link(nc.vector.tensor_tensor(tmp[:, 3, :], me, mo, ALU.add))
                rsqrt(rstd[:, :], tmp[:, 2, :], tmp[:, 0, :])
                nc.vector.scalar_tensor_tensor(out=nmr[:, :], in0=tmp[:, 3, :], scalar=-0.5,
                                               in1=rstd[:, :], op0=ALU.mult,
                                               op1=ALU.mult).then_inc(stat_done[n], 1)
                dve.wait_ge(stat_done[n], 1)

            def normalise(n):
                with dve.Fori(0, GROUPS // 2) as i:
                    for u in range(Q):
                        g = 2 * Q * i + u
                        last = nc.vector.tensor_scalar(
                            nrm[:, bass.ds(g, 1), :], rows[:, bass.ds(g, 1), :],
                            rstd[:, bass.ds(g, 1)], nmr[:, bass.ds(g, 1)], ALU.mult, ALU.add)
                    last.then_inc(nrm_v[n], 1)

            def copy_out(n, by_time=False):
                for c in range(C):
                    with dve.Fori(0, 2) as i:
                        for u in (0, 2):
                            dve.wait_ge(tp[n], 8 * c + 4 * i + (u + 1))
                            nc.vector.tensor_copy(cols_view(c, 4 * i + u, by_time),
                                                  ps[:, 4 + u, :] if not by_time
                                                  else ps[:, 4 + u, :].rearrange("p (b t) -> p b t", b=Q)
                                                  ).then_inc(tp_v[n], 1)

            def all_tiles_stats():
                with dve.Fori(0, TILES // 8) as i:
                    for u in range(8):
                        last = nc.vector.bn_stats(stats[:, bass.ds(8 * i + u, 1), :].rearrange("p a b -> p (a b)"),
                                                  rows[:, bass.ds(8 * i + u, 1), :].rearrange("p a b -> p (a b)"))
                return last

            for n in range(8):
                dve.wait_ge(ld_x[n], 16)
                for g in range(8 * n, 8 * n + 8):
                    last = nc.vector.bn_stats(stats[:, g, :], rows[:, g, :])
            link(last)
            row_stats(0)
            normalise(0)

            dve.wait_ge(prep_T, 1)
            link(nc.vector.tensor_copy(a_T[:, :, :].rearrange("p c n -> p (c n)"), ps[:, 0, :]))
            dve.wait_ge(prep_T, 2)
            link(nc.vector.tensor_copy(w_T[:, :, :].rearrange("p c n -> p (c n)"), ps[:, 1, :]))
            dve.wait_ge(prep_T, 3)
            nc.vector.tensor_copy(mb1_T[:, :], ps[:, 2, 0:E * J]).then_inc(prep_used, 1)
            dve.wait_ge(ident_done, 1)
            dve.wait_ge(ld_adj, 16)
            link(nc.vector.tensor_copy(s_rows[:, :, :], a_rows[:, :, :]))
            for c in range(C):
                v = s_rows[:, c, c * P:(c + 1) * P]
                link(nc.vector.tensor_tensor(v, v, ident[:, :], ALU.add))
            link(nc.vector.tensor_reduce(small[:, 0:2], s_rows[:, :, :], AX.X, ALU.add))
            link(nc.vector.tensor_reduce(small[:, 2:4], a_T[:, :, :], AX.X, ALU.add))
            for c in range(C):
                link(nc.vector.tensor_tensor(work[:, 0, c, :], a_rows[:, c, c * P:(c + 1) * P],
                                             ident[:, :], ALU.mult))
            link(nc.vector.tensor_reduce(small[:, 4:6], work[:, 0, 0:2, :], AX.X, ALU.add))
            link(nc.vector.tensor_tensor(small[:, 0:2], small[:, 0:2], small[:, 2:4], ALU.add))
            link(nc.vector.tensor_tensor(small[:, 0:2], small[:, 0:2], small[:, 4:6], ALU.subtract))
            rsqrt(small[:, 6:8], small[:, 0:2], small[:, 8:10])
            for c in range(C):
                last = nc.vector.tensor_scalar(s_rows[:, c, :], s_rows[:, c, :], small[:, 6 + c:7 + c],
                                               None, ALU.mult)
            last.then_inc(s_scaled, 1)
            copy_out(0)
            dve.wait_ge(prep_T, 4)
            for c in range(C):
                last = nc.vector.tensor_scalar(ah_T[:, c, :], ps[:, 3, c * N:(c + 1) * N],
                                               small[:, 6 + c:7 + c], None, ALU.mult)
            last.then_inc(prep_used, 1)
            dve.wait_ge(ld_lstm, 16 * 9)
            for k, half in enumerate((0.5, 1.0, 0.5)):
                nc.vector.tensor_scalar(U[:, k, :], U[:, k, :], half, None, ALU.mult)
                nc.vector.tensor_scalar(V[:, k, :], V[:, k, :], 0.5 * half, None, ALU.mult)
                last = nc.vector.tensor_scalar(bl[0:1, k * P:(k + 1) * P], bl[0:1, k * P:(k + 1) * P],
                                               half, None, ALU.mult)
            last.then_inc(lstm_w, 1)
            dve.wait_ge(ld_gnn, 16 * 7)
            nc.vector.tensor_scalar(gbh[:, :, :], gb[:, :, :], 0.5, None, ALU.mult).then_inc(half_bias, 1)
            dve.wait_ge(gate_th, 1)
            link(nc.vector.tensor_scalar(gates[:, 0:3, :], gates[:, 0:3, :], 0.5, 0.5, ALU.mult, ALU.add))
            nc.vector.tensor_tensor(gates[:, 3, :], gates[:, 0, :], gates[:, 1, :],
                                    ALU.add).then_inc(gate_done, 1)
            dve.wait_ge(gate_done, 1)

            for c in range(C):
                def messages(i):
                    for u in range(2):
                        at = 8 * c + 2 * i + u
                        dve.wait_ge(s1_act, at + 1)
                        w = [work[:, u, t, :] for t in range(Q)]
                        gs = [c * B + 2 * Q * i + (Q * u + t) for t in range(Q)]
                        for t in range(Q):
                            last = nc.vector.scalar_tensor_tensor(
                                out=w[t], in0=bin_sb[:, c, :], scalar=gates[:, 0, bass.ds(gs[t], 1)],
                                in1=w[t], op0=ALU.mult, op1=ALU.add)
                        last.then_inc(mstep, 1)
                        dve.wait_ge(mstep, 3 * at + 1)
                        for t in range(Q):
                            last = nc.vector.scalar_tensor_tensor(
                                out=w[t], in0=nrm[:, bass.ds(gs[t], 1), :].rearrange("p a b -> p (a b)"), scalar=gates[:, 2, bass.ds(gs[t], 1)],
                                in1=w[t], op0=ALU.mult, op1=ALU.add)
                        last.then_inc(mstep, 1)
                        dve.wait_ge(mstep, 3 * at + 2)
                        dve.wait_ge(agg, at + 1)
                        for t in range(Q):
                            last = nc.vector.scalar_tensor_tensor(
                                out=w[t], in0=ps[:, u, t * D:(t + 1) * D],
                                scalar=gates[:, 3, bass.ds(gs[t], 1)], in1=w[t], op0=ALU.mult, op1=ALU.add)
                        last.then_inc(mstep, 1)
                        dve.wait_ge(mstep, 3 * at + 3)
                        nc.vector.scalar_tensor_tensor(
                            out=rows[:, bass.ds(gs[0], Q), :], in0=work[:, u, :, :], scalar=0.0,
                            in1=rows[:, bass.ds(gs[0], Q), :], op0=ALU.max, op1=ALU.add).then_inc(s1_free, 1)
                with dve.Fori(0, 4) as i:
                    messages(i)
            dve.wait_ge(s1_free, GROUPS)
            link(all_tiles_stats(), TILES // 8)
            row_stats(1)
            normalise(1)
            copy_out(1, by_time=True)

            dve.wait_ge(consts, 5)

            def steps(i):
                for s in range(2 * STEPS):
                    t = 2 * STEPS * i + s
                    nc.vector.scalar_tensor_tensor(out=hc[:, :], in0=hs[:, bass.ds(t, 1), :].rearrange("p a b -> p (a b)"),
                                                   scalar=0.5, in1=cell[:, :], op0=ALU.mult,
                                                   op1=ALU.mult).then_inc(c_done, 1)
                    dve.wait_ge(t_ig, t + 1)
                    nc.vector.scalar_tensor_tensor(out=ig[:, :], in0=T[:, 0, :], scalar=1.0, in1=T[:, 1, :],
                                                   op0=ALU.add, op1=ALU.mult).then_inc(c_done, 1)
                    dve.wait_ge(c_done, 2 * t + 2)
                    nc.vector.tensor_tensor(cell[:, :], hc[:, :], ig[:, :], ALU.add).then_inc(c_new, 1)
                    dve.wait_ge(t_o, t + 1)
                    dve.wait_ge(t_c, t + 1)
                    nc.vector.scalar_tensor_tensor(out=hs[:, bass.ds(t + 1, 1), :].rearrange("p a b -> p (a b)"), in0=T[:, 2, :],
                                                   scalar=1.0, in1=tc[:, :], op0=ALU.add,
                                                   op1=ALU.mult).then_inc(h_done, 1)
                    dve.wait_ge(h_done, t + 1)
            with dve.Fori(0, BLOCKS // 2) as i:
                steps(i)

            with dve.Fori(0, GROUPS // 4) as i:
                for u in range(4):
                    dve.wait_ge(tp[2], 4 * i + (u + 1))
                    v = rows[:, bass.ds(4 * Q * i + Q * u, Q), :].rearrange("p a b -> p (a b)")
                    nc.vector.scalar_tensor_tensor(out=v, in0=ps[:, 4 + u, :], scalar=0.5, in1=v,
                                                   op0=ALU.mult, op1=ALU.add).then_inc(x2_done, 1)
            dve.wait_ge(x2_done, GROUPS)
            link(all_tiles_stats(), TILES // 8)
            row_stats(2)
            normalise(2)
            with dve.Fori(0, 4) as i:
                for u in (0, 2):
                    dve.wait_ge(ga, 4 * i + (u + 1))
                    nc.vector.tensor_copy(cols[:, bass.ds(BANK * 4 * i + BANK * u, BANK)],
                                          ps[:, 4 + u, :]).then_inc(ga_v, 1)
            with dve.Fori(0, GROUPS) as i:
                for k in range(HC):
                    dve.wait_ge(hp_ev, HC * i + (k + 1))
                    last = nc.vector.bn_stats(bst[:, k, bass.ds(i, 1), :].rearrange("p a b -> p (a b)"),
                                              h1[:, k, bass.ds(BANK * i, BANK)])
            link(last, GROUPS)

            def bn_finish(ks, gamma, beta, done):
                n = len(ks)
                k0 = ks[0]
                for k in ks:
                    last = nc.vector.bn_aggr(mv[:, k, :], bst[:, k, :, :].rearrange("p g s -> p (g s)"))
                link(last)
                link(nc.vector.tensor_scalar(small[:, 0:n], mv[:, k0:k0 + n, 1], EPS, None, ALU.add))
                rsqrt(small[:, 2:2 + n], small[:, 0:n], small[:, 4:4 + n])
                link(nc.vector.tensor_tensor(bsc[:, k0:k0 + n], small[:, 2:2 + n], gamma, ALU.mult))
                link(nc.vector.tensor_tensor(small[:, 0:n], mv[:, k0:k0 + n, 0], bsc[:, k0:k0 + n], ALU.mult))
                nc.vector.tensor_tensor(bsh[:, k0:k0 + n], beta, small[:, 0:n],
                                        ALU.subtract).then_inc(done, 1)
                dve.wait_ge(done, 1)
            dve.wait_ge(ld_small, 128)
            bn_finish([0, 1], bn1[:, 1, :], bn1[:, 2, :], bn1_done)
            with dve.Fori(0, GROUPS // 2) as i:
                for u in range(2):
                    dve.wait_ge(op, 2 * i + (u + 1))
                    v = cols[:, bass.ds(2 * BANK * i + BANK * u, BANK)]
                    nc.vector.tensor_scalar(v, ps[:, 2 + u, :], bn2[:, 0:1], None, ALU.add).then_inc(op_ev, 1)
                    dve.wait_ge(op_ev, 2 * i + (u + 1))
                    last = nc.vector.bn_stats(bst[:, HC, bass.ds(2 * i + u, 1), :].rearrange("p a b -> p (a b)"), v)
            link(last, GROUPS // 2)
            bn_finish([2], bn2[:, 1:2], bn2[:, 2:3], bn2_done)
            with dve.Fori(0, GROUPS // 2) as i:
                v = cols[:, bass.ds(2 * BANK * i, BANK)]
                nc.vector.tensor_scalar(v, v, bsc[:, HC:HC + 1], bsh[:, HC:HC + 1],
                                        ALU.mult, ALU.add).then_inc(y_v, 1)
            with dve.Fori(0, GROUPS // 4) as i:
                for u in range(4):
                    dve.wait_ge(tp[4], 4 * i + (u + 1))
                    v = rows[:, :, :].rearrange("p (c b) d -> p b c d", c=C)[:, bass.ds(8 * i + 2 * u, 2), :, :]
                    s = ps[:, 4 + u, :].rearrange("p (b c d) -> p b c d", b=2, c=C)
                    nc.vector.tensor_tensor(v, v, s, ALU.add).then_inc(x3_done, 1)
            dve.wait_ge(x3_done, GROUPS)
            link(all_tiles_stats(), TILES // 8)
            row_stats(3)
            normalise(3)
            copy_out(3)

            dve.wait_ge(lg, 1)
            lps = ps[:, 0, :].rearrange("p (g e) -> p g e", e=E)

            def over(v):
                return v.unsqueeze(2).to_broadcast([P, TILES, E])

            def each(v):
                return v.unsqueeze(1).to_broadcast([P, TILES, E])

            def first_of(mask, m, scratch):
                link(nc.vector.tensor_tensor(scratch, logit[:, :, :], over(m), ALU.is_equal))
                link(nc.vector.tensor_tensor(scratch, scratch, each(pos[:, :]), ALU.mult))
                link(nc.vector.tensor_reduce(tmp[:, 0, :], scratch, AX.X, ALU.max))
                link(nc.vector.tensor_tensor(mask, scratch, over(tmp[:, 0, :]), ALU.is_equal))
            dve.wait_ge(tp[3], GROUPS)
            link(nc.vector.tensor_tensor(logit[:, :, :], lps, each(bg_sb[:, :]), ALU.add))
            link(nc.vector.tensor_reduce(m1[:, :], logit[:, :, :], AX.X, ALU.max))
            first_of(mk[0], m1[:, :], mk[2])
            link(nc.vector.scalar_tensor_tensor(out=logit[:, :, :], in0=mk[0], scalar=-1e30,
                                                in1=logit[:, :, :], op0=ALU.mult, op1=ALU.add))
            link(nc.vector.tensor_reduce(m2[:, :], logit[:, :, :], AX.X, ALU.max))
            first_of(mk[1], m2[:, :], mk[2])
            nc.vector.tensor_tensor(m2[:, :], m2[:, :], m1[:, :], ALU.subtract).then_inc(lg_dif, 1)
            dve.wait_ge(lg_exp, 1)
            link(nc.vector.tensor_scalar(tmp[:, 0, :], m2[:, :], 1.0, None, ALU.add))
            link(nc.vector.reciprocal(tmp[:, 1, :], tmp[:, 0, :]))
            link(nc.vector.tensor_tensor(tmp[:, 2, :], tmp[:, 1, :], m2[:, :], ALU.mult))
            link(nc.vector.tensor_tensor(mk[0], mk[0], over(tmp[:, 1, :]), ALU.mult))
            link(nc.vector.tensor_tensor(mk[1], mk[1], over(tmp[:, 2, :]), ALU.mult))
            nc.vector.tensor_tensor(route, mk[0], mk[1], ALU.add).then_inc(route_done, 1)
            dve.wait_ge(rT, 1)
            nc.vector.tensor_copy(routeT[:, :, :].rearrange("p k t -> p (k t)"), ps[:, 1, :]).then_inc(rT_ev, 1)
            for q in range(GROUPS):
                dve.wait_ge(b2_ps, q + 1)
                v = rows[:, Q * q:Q * q + Q, :].rearrange("p a b -> p (a b)")
                nc.vector.tensor_tensor(v, v, ps[:, 2 + q % 2, :], ALU.add).then_inc(b2_added, 1)
            dve.wait_ge(b2_added, GROUPS)

            def experts(q):
                for e in range(E):
                    dve.wait_ge(down, E * q + (e + 1))
                    if e:
                        dve.wait_ge(accd, E * q + e)
                    for t in range(Q):
                        v = rows[:, bass.ds(Q * q + t, 1), :].rearrange("p a b -> p (a b)")
                        last = nc.vector.scalar_tensor_tensor(
                            out=v, in0=ps[:, 4 + e % 2, t * D:(t + 1) * D],
                            scalar=route[:, bass.ds(Q * q + t, 1), e:e + 1].rearrange("p a b -> p (a b)"), in1=v, op0=ALU.mult, op1=ALU.add)
                    last.then_inc(accd, 1)
            with dve.Fori(0, GROUPS) as q:
                experts(q)

        @block.tensor
        def _(pe):
            def transposes(n, source, ready):
                for q in range(GROUPS):
                    ready(q)
                    if q >= 4:
                        if q % 2 == 0:
                            pe.wait_ge(tp_v[n], (q - 4) // 2 + 1)
                        else:
                            pe.wait_ge(tp_s[n], (q - 5) // 2 + 1)
                    for t in range(Q):
                        last = nc.tensor.transpose(ps[:, 4 + q % 4, t * P:(t + 1) * P], source(q, t),
                                                   ident[:, :])
                    last.then_inc(tp[n], 1)

            def normalised(n):
                def ready(q):
                    pe.wait_ge(nrm_v[n] if q % 2 == 0 else nrm_s[n], q // 2 + 1)
                return ready

            pe.wait_ge(ident_done, 1)
            pe.wait_ge(ld_adj, 16)
            for cm in range(C):
                for cn in range(C):
                    last = nc.tensor.transpose(ps[:, 0, (cm * C + cn) * P:(cm * C + cn + 1) * P],
                                               a_rows[:, cn, cm * P:(cm + 1) * P], ident[:, :])
            last.then_inc(prep_T, 1)
            pe.wait_ge(ld_bn, 48)
            for k in range(4):
                last = nc.tensor.transpose(ps[:, 1, k * P:(k + 1) * P], w_in[:, k, :], ident[:, :])
            last.then_inc(prep_T, 1)
            nc.tensor.transpose(ps[:, 2, 0:E * J], mb1_rows[:, :], ident[0:E * J, 0:E * J]).then_inc(prep_T, 1)
            transposes(0, lambda q, t: nrm[:, Q * q + t, :], normalised(0))
            pe.wait_ge(s_scaled, 1)
            for cm in range(C):
                for cn in range(C):
                    last = nc.tensor.transpose(ps[:, 3, (cm * C + cn) * P:(cm * C + cn + 1) * P],
                                               s_rows[:, cn, cm * P:(cm + 1) * P], ident[:, :])
            last.then_inc(prep_T, 1)
            pe.wait_ge(ld_gnn, 16 * 7)
            pe.wait_ge(prep_used, 2)
            for g in range(TILES):
                if g % Q == 0:
                    q = g // Q
                    pe.wait_ge(tp_v[0] if q % 2 == 0 else tp_s[0], q // 2 + 1)
                last = nc.tensor.matmul(ps[:, 0, 3 * g:3 * g + 3], cols[:, g * P:(g + 1) * P], gw[:, :],
                                        start=True, stop=True)
            last.then_inc(gate_ps, 1)
            pe.wait_ge(gate_th, 1)
            for c in range(C):
                def aggregate(i):
                    for u in range(2):
                        if c or not isinstance(i, int):
                            pe.wait_ge(mstep, 24 * c + 6 * i + (3 * u - 3))
                        for cm in range(C):
                            last = nc.tensor.matmul(
                                ps[:, u, :], a_T[:, cm, c * P:(c + 1) * P],
                                nrm[:, bass.ds(cm * B + 2 * Q * i + Q * u, Q), :].rearrange("p a b -> p (a b)"),
                                start=(cm == 0), stop=(cm == C - 1))
                        last.then_inc(agg, 1)
                peeled(pe, 4, aggregate)
            transposes(1, lambda q, t: nrm[:, Q * q + t, :], normalised(1))

            def gate_inputs(blk, bank0, k, quarter):
                o = ps[:, bank0 + k, quarter * P:(quarter + 1) * P]
                nc.tensor.matmul(o, bl[0:1, k * P:(k + 1) * P], ones[0:1, 0:P], start=(quarter == 0),
                                 stop=True, skip_group_check=True)
                return nc.tensor.matmul(o, U[:, k, :], cols[:, bass.ds(blk * BANK + quarter * P, P)],
                                        start=False, stop=True, skip_group_check=True)
            pe.wait_ge(lstm_w, 1)
            pe.wait_ge(consts, 5)
            pe.wait_ge(tp_v[1], GROUPS // 2)
            pe.wait_ge(tp_s[1], GROUPS // 2)
            pe.wait_ge(s1_free, GROUPS)
            for k in range(GATES):
                for quarter in range(Q):
                    gate_inputs(0, 0, k, quarter)

            def steps(i, last_round):
                for s in range(2 * STEPS):
                    bank0 = 3 * (s // STEPS)
                    col = (s % STEPS) * B
                    if not (isinstance(i, int) and i == 0 and s == 0):
                        pe.wait_ge(h_done, 2 * STEPS * i + s)
                    h = hs[:, bass.ds(2 * STEPS * i + s, 1), :].rearrange("p a b -> p (a b)")
                    for k in range(GATES):
                        mm = nc.tensor.matmul(ps[:, bank0 + k, col:col + B], V[:, k, :], h,
                                              start=False, stop=True, skip_group_check=True)
                        if k:
                            mm.then_inc(z_ig if k == 1 else z_o, 1)
                    piece = s % STEPS
                    if piece < GATES * Q and not (last_round and s >= STEPS):
                        gate_inputs(2 * i + (s // STEPS + 1), 3 - bank0, piece // Q, piece % Q)
            steps(0, False)
            with pe.Fori(1, BLOCKS // 2 - 1) as i:
                steps(i, False)
            steps(BLOCKS // 2 - 1, True)

            pe.wait_ge(h_done, N)

            def bank_read(q):
                if q >= 4:
                    pe.wait_ge(x2_done, q - 3)
            for q in range(GROUPS):
                bank_read(q)
                for t in range(Q):
                    g = Q * q + t
                    c, b = g // B, g % B
                    last = nc.tensor.transpose(ps[:, 4 + q % 4, t * P:(t + 1) * P],
                                               hs[:, 1 + c * P:1 + (c + 1) * P, b], ident[:, :])
                last.then_inc(tp[2], 1)
            pe.wait_ge(nrm_v[2], GROUPS // 2)
            pe.wait_ge(nrm_s[2], GROUPS // 2)
            for q in range(GROUPS):
                if q >= 4:
                    pe.wait_ge(ga_v if q % 2 == 0 else ga_s, (q - 4) // 2 + 1)
                for t in range(2):
                    b = 2 * q + t
                    for cm in range(C):
                        last = nc.tensor.matmul(ps[:, 4 + q % 4, t * N:(t + 1) * N],
                                                nrm[:, cm * B + b, :], ah_T[:, cm, :],
                                                start=(cm == 0), stop=(cm == C - 1))
                last.then_inc(ga, 1)
            pe.wait_ge(ga_v, GROUPS // 2)
            pe.wait_ge(ga_s, GROUPS // 2)

            def hidden(i):
                for k in range(HC):
                    if not isinstance(i, int):
                        pe.wait_ge(hp_ev, HC * i + (k - 1))
                    nc.tensor.matmul(ps[:, k, :], w_T[:, k, :], cols[:, bass.ds(BANK * i, BANK)],
                                     start=True, stop=True).then_inc(hp, 1)
            peeled(pe, GROUPS, hidden)

            def output_layer(i):
                for u in range(2):
                    if not isinstance(i, int):
                        pe.wait_ge(op_ev, 2 * i + (u - 1))
                    for k in range(HC):
                        pe.wait_ge(relu_done, 4 * i + (2 * u + k + 1))
                        last = nc.tensor.matmul(ps[:, 2 + u, :], w_T[:, 2 + k, :],
                                                h1[:, k, bass.ds(2 * BANK * i + BANK * u, BANK)],
                                                start=(k == 0), stop=(k == HC - 1))
                    last.then_inc(op, 1)
            peeled(pe, GROUPS // 2, output_layer)
            for q in range(GROUPS):
                pe.wait_ge(y_v if q % 2 == 0 else y_s, q // 2 + 1)
                if q >= 4:
                    pe.wait_ge(x3_done, q - 3)
                for t in range(Q):
                    last = nc.tensor.transpose(ps[:, 4 + q % 4, t * P:(t + 1) * P],
                                               cols[:, (Q * q + t) * P:(Q * q + t + 1) * P], ident[:, :])
                last.then_inc(tp[4], 1)
            transposes(3, lambda q, t: nrm[:, Q * q + t, :], normalised(3))
            pe.wait_ge(ld_small, 128)
            for g in range(TILES):
                if g % Q == 0:
                    q = g // Q
                    pe.wait_ge(tp_v[3] if q % 2 == 0 else tp_s[3], q // 2 + 1)
                last = nc.tensor.matmul(ps[:, 0, E * g:E * g + E], cols[:, g * P:(g + 1) * P], wg_sb[:, :],
                                        start=True, stop=True)
            last.then_inc(lg, 1)
            pe.wait_ge(route_done, 1)
            for k in range(4):
                last = nc.tensor.transpose(ps[:, 1, k * P:(k + 1) * P],
                                           route[:, 16 * k:16 * k + 16, :].rearrange("p g e -> p (g e)"),
                                           ident[:, :])
            last.then_inc(rT, 1)
            pe.wait_ge(rT_ev, 1)
            pe.wait_ge(ld_diag, 256)
            for q in range(GROUPS):
                if q >= 2:
                    pe.wait_ge(b2_added, q - 1)
                k, a = q // 4, 4 * (q % 4)
                nc.tensor.matmul(ps[:, 2 + q % 2, :], routeT[:, k, :],
                                 b2diag[:, a:a + 4, :].rearrange("p k d -> p (k d)"),
                                 start=True, stop=True).then_inc(b2_ps, 1)
            pe.wait_ge(ld_moe, 16 * 2 * E)
            pe.wait_ge(b2_added, GROUPS)

            def up_projection(q, e, first):
                for j in range(J):
                    if not (first and e == 0):
                        pe.wait_ge(gelu, E * J * q + (J * e + j - J + 1))
                    nc.tensor.matmul(ps[:, j, :], w1e[:, e, j * P:(j + 1) * P],
                                     cols[:, bass.ds(BANK * q, BANK)], start=True, stop=True).then_inc(up, 1)

            def down_projection(q, e, first):
                pe.wait_ge(gelu, E * J * q + (J * e + J))
                if not (first and e < 2):
                    pe.wait_ge(accd, E * q + (e - 1))
                for t in range(Q):
                    for j in range(J):
                        last = nc.tensor.matmul(ps[:, 4 + e % 2, t * D:(t + 1) * D],
                                                hbuf[:, e % 2, j, t * P:(t + 1) * P], w2e[:, e, j, :],
                                                start=(j == 0), stop=(j == J - 1))
                last.then_inc(down, 1)

            def experts(q):
                first = isinstance(q, int)
                up_projection(q, 0, first)
                for e in range(E):
                    if e + 1 < E:
                        up_projection(q, e + 1, first)
                    down_projection(q, e, first)
            peeled(pe, GROUPS, experts)


_ARGS = {"x": "x", "adj": "adj"}
_ARGS |= {k: "L0_gnn_" + k for k in ("bias_in", "bias_out", "gate_w_in", "gate_b_in", "gate_w_out",
                                    "gate_b_out", "loop_gate")}
_ARGS |= {k: "L0_ffn_" + k for k in ("U_i", "V_i", "b_i", "U_c", "V_c", "b_c", "U_o", "V_o", "b_o")}
_ARGS |= {k: "L1_gnn_" + k for k in ("W1", "b1", "g1", "be1", "W2", "b2", "g2", "be2")}
_ARGS |= {"Wg": "L1_ffn_Wg", "bg": "L1_ffn_bg", "mW1": "L1_ffn_W1", "mb1": "L1_ffn_b1",
          "mW2": "L1_ffn_W2", "mb2": "L1_ffn_b2"}


def kernel(**inputs):
    import numpy as np
    import concourse.bacc as bacc
    from concourse.bass_utils import run_bass_kernel_spmd

    nc = bacc.Bacc("TRN2", target_bir_lowering=False, num_devices=1)
    arrays, args = {}, {}
    for arg, name in _ARGS.items():
        a = np.ascontiguousarray(inputs[name])
        arrays[name] = a
        args[arg] = nc.dram_tensor(name, a.shape, mybir.dt.from_np(a.dtype), kind="ExternalInput").ap()
    out = nc.dram_tensor("out", (B, N, D), F32, kind="ExternalOutput").ap()
    build(nc, out=out, **args)
    r = run_bass_kernel_spmd(nc, [arrays], core_ids=[0])
    return r.results[0]["out"]
```

```python
from contextlib import ExitStack

import concourse.bass as bass
from concourse import mybir

F32 = mybir.dt.float32
BF16 = mybir.dt.bfloat16
F16 = mybir.dt.float16
I32 = mybir.dt.int32
U32 = mybir.dt.uint32
ALU = mybir.AluOpType
ACT = mybir.ActivationFunctionType
AX = mybir.AxisListType

B, N, D = 32, 256, 128
P = 128
C = N // P
TILES = C * B
Q = 4
GROUPS = TILES // Q
BANK = Q * P
H1 = 256
HC = H1 // P
E, F = 8, 512
J = F // P
GATES = 3
STEPS = BANK // B
BLOCKS = N // STEPS
EPS = 1e-5
RSQRT_MAGIC = float(0x5F3759DF)
NEWTON = 3
SB = 4
SBT = TILES // SB
TOP = 2
SLOTS = TOP * SBT + E - 1
U = 3
ITERS = SLOTS // U
PARTS = 3


def staged(eng, body):
    body(0)
    body(1)
    with eng.Fori(2, ITERS - 1) as i:
        body(i)
    body(ITERS - 1)


def peeled(eng, n, body):
    body(0)
    if n > 1:
        with eng.Fori(1, n) as i:
            body(i)


assert SLOTS % U == 0 and ITERS >= 4


def build(nc, x, adj, bias_in, bias_out, gate_w_in, gate_b_in, gate_w_out, gate_b_out, loop_gate,
          U_i, V_i, b_i, U_c, V_c, b_c, U_o, V_o, b_o, W1, b1, g1, be1, W2, b2, g2, be2,
          Wg, bg, mW1, mb1, mW2, mb2, out):
    x_v = x.rearrange("b (c p) d -> p c b d", p=P)
    out_v = out.rearrange("b (c p) d -> p c b d", p=P)
    ctx = ExitStack()
    with ctx:
        def sb(name, shape, dt=F32):
            return ctx.enter_context(nc.sbuf_tensor(name, shape, dt))

        def sem(name):
            return ctx.enter_context(nc.semaphore(name))

        rows = sb("rows", [P, TILES, D])
        nrm = sb("nrm", [P, TILES, D])
        cols = sb("cols", [P, TILES * P])
        hid = sb("hid", [P, HC * TILES * P])
        hs = hid[:, 0:(N + 1) * B].rearrange("p (t b) -> p t b", b=B)
        h1 = hid[:, :].rearrange("p (c r) -> p c r", c=HC)
        at = 0

        def of_hid(n):
            nonlocal at
            at += n
            return hid[:, at - n:at]
        w1e = of_hid(E * F)
        w2e = of_hid(E * F)
        b1e = of_hid(E * F)
        b2e = of_hid(E * D)
        h_pre = of_hid(U * F).rearrange("p (u f) -> p u f", u=U)
        h_T = of_hid(U * F).rearrange("p (u f) -> p u f", u=U)
        zeros = hid[:, (N + 1) * B:(N + 1) * B + SLOTS * D]
        picked = cols[:, :].rearrange("p (s k g d) -> p s k g d", s=2, k=TOP, g=SBT)
        x_slots, y_slots = ([nc.dram_tensor(f"{v}_slots{n}", (SLOTS * P, D), F32, kind="Internal").ap()
                             for n in range(SB)] for v in "xy")

        ident = sb("ident", [P, P])
        a_rows = sb("a_rows", [P, C, N])
        s_rows = sb("s_rows", [P, C, N])
        a_T = sb("a_T", [P, C, N])
        ah_T = sb("ah_T", [P, C, N])
        bin_sb = sb("bin_sb", [P, C, D])
        bout_sb = sb("bout_sb", [P, C, D])
        gw = sb("gw", [P, 3])
        gb = sb("gb", [P, 2, C])
        gbh = sb("gbh", [P, 2, C])
        gates = sb("gates", [P, 4, TILES])
        Ux = sb("Ux", [P, GATES, P])
        Vx = sb("Vx", [P, GATES, P])
        bl = sb("bl", [1, GATES * P])
        Vp = sb("Vp", [P, PARTS, GATES * P], BF16)
        blp = sb("blp", [1, PARTS, GATES * P], BF16)
        bp = sb("bp", [PARTS, GATES * P], BF16)
        res = sb("res", [P, GATES * P])
        ones_bf = sb("ones_bf", [PARTS, P], BF16)
        h_hi = sb("h_hi", [P, B], F16)
        h_lo = sb("h_lo", [P, B], F16)
        h_zero = sb("h_zero", [P, B], F16)
        w_in = sb("w_in", [P, 4, P])
        w_T = sb("w_T", [P, 4, P])
        bn1 = sb("bn1", [P, 3, HC])
        bn2 = sb("bn2", [P, 3])
        wg_sb = sb("wg_sb", [P, E])
        bg_sb = sb("bg_sb", [P, E])
        stats = sb("stats", [P, TILES, 6])
        bst = sb("bst", [P, HC + 1, GROUPS, 6])
        tmp = sb("tmp", [P, 4, TILES])
        rstd = sb("rstd", [P, TILES])
        nmr = sb("nmr", [P, TILES])
        small = sb("small", [P, 16])
        mv = sb("mv", [P, HC + 1, 2])
        bsc = sb("bsc", [P, HC + 1])
        bsh = sb("bsh", [P, HC + 1])
        work = sb("work", [P, 2, Q, D])
        T = sb("T", [P, 3, B])
        hc = sb("hc", [P, B])
        ig = sb("ig", [P, B])
        cell = sb("cell", [P, B])
        tc = sb("tc", [P, B])
        logit = sb("logit", [P, TILES, E])
        m1 = sb("m1", [P, TILES])
        m2 = sb("m2", [P, TILES])
        pos = sb("pos", [P, E])
        x_in = sb("x_in", [P, U, D])
        x_T = sb("x_T", [P, U, D])
        y_out = sb("y_out", [P, U, D])
        before = sb("before", [P, P], BF16)
        all_ones = sb("all_ones", [P, P], BF16)
        mark = sb("mark", [P, TILES * E], BF16)
        ends = sb("ends", [P, 3, SB * E])
        iends = sb("iends", [P, SB * E], I32)
        slot = sb("slot", [P, TOP, TILES], U32)
        tile_no = sb("tile_no", [1, SLOTS])
        expert = sb("expert", [1, SB, SLOTS + 2 * U - 1], I32)
        ps = ctx.enter_context(nc.psum_tensor("ps", [P, 8, BANK], F32))
        mk = [h_T[:, k, :].rearrange("p (g e) -> p g e", e=E) for k in range(3)]
        run = [h_pre[:, 0, :], h_pre[:, 1, :]]

        ld_x = [sem(f"ld_x{n}") for n in range(8)]
        ld_adj = sem("ld_adj")
        ld_gnn = sem("ld_gnn")
        ld_lstm = sem("ld_lstm")
        ld_bn = sem("ld_bn")
        ld_small = sem("ld_small")
        ld_moe = sem("ld_moe")
        zeros_set = sem("zeros_set")
        slots_zeroed = sem("slots_zeroed")
        marked = sem("marked")
        ranked = sem("ranked")
        slots_done = sem("slots_done")
        experts_known = sem("experts_known")
        scattered = [sem(f"scattered{n}") for n in range(SB)]
        x_loaded = [sem(f"x_loaded{n}") for n in range(U)]
        x_turned = sem("x_turned")
        x_copied = sem("x_copied")
        up_done = sem("up_done")
        biased = sem("biased")
        turned = sem("turned")
        gelu_done = sem("gelu_done")
        down_done = sem("down_done")
        y_done = sem("y_done")
        y_stored = [sem(f"y_stored{n}") for n in range(U)]
        picked_done = [sem(f"picked{n}") for n in range(GROUPS)]
        mix_step = sem("mix_step")
        mix_done = sem("mix_done")
        ident_done = sem("ident_done")
        consts = sem("consts")
        dch = sem("dch")
        prep_T = sem("prep_T")
        prep_used = sem("prep_used")
        s_scaled = sem("s_scaled")
        half_bias = sem("half_bias")
        stat_done = [sem(f"stat_done{n}") for n in range(4)]
        nrm_v = [sem(f"nrm_v{n}") for n in range(4)]
        nrm_s = [sem(f"nrm_s{n}") for n in range(4)]
        tp = [sem(f"tp{n}") for n in range(5)]
        tp_v = [sem(f"tp_v{n}") for n in range(5)]
        tp_s = [sem(f"tp_s{n}") for n in range(5)]
        gate_ps = sem("gate_ps")
        gate_th = sem("gate_th")
        gate_done = sem("gate_done")
        agg = sem("agg")
        agg_used = sem("agg_used")
        s1_act = sem("s1_act")
        s1_free = sem("s1_free")
        mixed = sem("mixed")
        mstep = sem("mstep")
        lstm_w = sem("lstm_w")
        bias_parts = sem("bias_parts")
        ld_bp = sem("ld_bp")
        hi_done = sem("hi_done")
        lo_done = sem("lo_done")
        first_in = sem("first_in")
        z_ig = sem("z_ig")
        z_o = sem("z_o")
        t_ig = sem("t_ig")
        t_o = sem("t_o")
        t_c = sem("t_c")
        c_done = sem("c_done")
        c_new = sem("c_new")
        h_done = sem("h_done")
        x2_done = sem("x2_done")
        ga_v = sem("ga_v")
        ga_s = sem("ga_s")
        ga = sem("ga")
        hp = sem("hp")
        hp_ev = sem("hp_ev")
        bn1_done = sem("bn1_done")
        relu_done = sem("relu_done")
        op = sem("op")
        op_ev = sem("op_ev")
        bn2_done = sem("bn2_done")
        y_v = sem("y_v")
        y_s = sem("y_s")
        x3_done = sem("x3_done")
        lg = sem("lg")
        lg_exp = sem("lg_exp")
        lg_dif = sem("lg_dif")
        stored = sem("stored")

        block = ctx.enter_context(nc.Block())

        @block.sync
        def _(sp):
            for n in range(8):
                c, b0 = n // 4, 8 * (n % 4)
                sp.dma_start(rows[:, c * B + b0:c * B + b0 + 8, :],
                             x_v[:, c, b0:b0 + 8, :]).then_inc(ld_x[n], 16)
            sp.wait_ge(bias_parts, 1)
            for k in range(PARTS):
                sp.dma_start(bp[k:k + 1, :], blp[0:1, k, :]).then_inc(ld_bp, 16)
            sp.wait_ge(zeros_set, 1)
            for n in range(SB):
                sp.dma_start(x_slots[n].rearrange("(p t) d -> p (t d)", p=P),
                             zeros).then_inc(slots_zeroed, 16)
            sp.wait_ge(op, GROUPS)
            for e in range(E):
                sp.dma_start(w1e[:, e * F:(e + 1) * F], mW1[e]).then_inc(ld_moe, 16)
            for e in range(E):
                sp.dma_start(w2e[:, e * F:(e + 1) * F].rearrange("p (j d) -> p j d", j=J),
                             mW2[e].rearrange("(j p) d -> p j d", p=P)).then_inc(ld_moe, 16)
            sp.dma_start(b1e, mb1.rearrange("(a e) f -> a (e f)", a=1).to_broadcast([P, E * F])).then_inc(ld_moe, 16)
            sp.dma_start(b2e, mb2.rearrange("(a e) d -> a (e d)", a=1).to_broadcast([P, E * D])).then_inc(ld_moe, 16)

            def load(n, t, u):
                sp.dma_start(x_in[:, u, :], x_slots[n][bass.ds(t * P, P), :]).then_inc(x_loaded[u], 16)

            def store_rows(n):
                for q in range(4 * n, 4 * n + 4):
                    sp.wait_ge(mix_done, q + 1)
                    c, b0 = q // 8, Q * (q % 8)
                    sp.dma_start(out_v[:, c, b0:b0 + Q, :],
                                 rows[:, Q * q:Q * q + Q, :]).then_inc(stored, 16)
            for n in range(SB):
                base = SLOTS * n
                sp.wait_ge(scattered[n], 16 * TOP * SBT)
                for t in range(U):
                    if n:
                        sp.wait_ge(x_turned, base - U + t + 1)
                    load(n, t, t)

                def step(i):
                    for u in range(U):
                        t = U * i + u
                        if not (isinstance(i, int) and i == ITERS - 1):
                            sp.wait_ge(x_turned, base + t + 1)
                            load(n, t + U, u)
                        if not (isinstance(i, int) and t < 2):
                            sp.wait_ge(y_done, base + t - 1)
                            v = (u - 2) % U
                            sp.dma_start(y_slots[n][bass.ds((t - 2) * P, P), :],
                                         y_out[:, v, :]).then_inc(y_stored[v], 16)
                staged(sp, step)
                for t in (SLOTS - 2, SLOTS - 1):
                    sp.wait_ge(y_done, base + t + 1)
                    sp.dma_start(y_slots[n][t * P:(t + 1) * P, :],
                                 y_out[:, t % U, :]).then_inc(y_stored[t % U], 16)
                if n >= 1:
                    store_rows(n - 1)
            store_rows(SB - 1)
            sp.wait_ge(stored, 16 * GROUPS)

        @block.gpsimd
        def _(pool):
            nc.gpsimd.memset(ident[:, :], 0.0).then_inc(consts, 1)
            nc.gpsimd.memset(hs[:, 0, :], 0.0).then_inc(consts, 1)
            nc.gpsimd.memset(ones_bf[:, :], 1.0).then_inc(consts, 1)
            nc.gpsimd.memset(h_zero[:, :], 0.0).then_inc(consts, 1)
            nc.gpsimd.memset(cell[:, :], 0.0).then_inc(consts, 1)
            nc.gpsimd.iota(pos[:, :], [[-1, E]], base=E, channel_multiplier=0,
                           allow_small_or_imprecise_dtypes=True).then_inc(consts, 1)
            pool.wait_ge(consts, 1)
            nc.gpsimd.affine_select(out=ident[:, :], in_=ident[:, :], compare_op=ALU.not_equal, fill=1.0,
                                    base=0, pattern=[[-1, P]], channel_multiplier=1).then_inc(ident_done, 1)
            nc.gpsimd.memset(zeros, 0.0).then_inc(zeros_set, 1)
            nc.gpsimd.memset(before[:, :], 0.0).then_inc(consts, 1)
            nc.gpsimd.memset(all_ones[:, :], 1.0).then_inc(consts, 1)
            nc.gpsimd.memset(expert[:, :, :], 0).then_inc(consts, 1)
            nc.gpsimd.iota(tile_no[:, :], [[1, SLOTS]], base=0, channel_multiplier=0,
                           allow_small_or_imprecise_dtypes=True).then_inc(consts, 1)
            pool.wait_ge(consts, 8)
            nc.gpsimd.affine_select(out=before[:, :], in_=before[:, :], compare_op=ALU.is_ge, fill=1.0,
                                    base=0, pattern=[[-1, P]], channel_multiplier=1).then_inc(consts, 1)

            pool.wait_ge(slots_done, TOP)
            pool.wait_ge(slots_zeroed, 16 * SB)
            pool.wait_ge(nrm_s[3], GROUPS // 2)
            for n in range(SB):
                for g in range(SBT * n, SBT * n + SBT):
                    for k in range(TOP):
                        nc.gpsimd.indirect_dma_start(
                            x_slots[n], bass.IndirectOffsetOnAxis(ap=slot[:, k, g:g + 1], axis=0),
                            nrm[:, g, :], None).then_inc(scattered[n], 16)
            pool.wait_ge(lg, 1)
            for n in range(SB):
                if n >= 2:
                    pool.wait_ge(mix_done, 4 * (n - 1))
                for u in range(U):
                    pool.wait_ge(y_stored[u], 16 * ITERS * (n + 1))
                for g in range(SBT):
                    for k in range(TOP):
                        nc.gpsimd.indirect_dma_start(
                            picked[:, n % 2, k, g, :], None, y_slots[n],
                            bass.IndirectOffsetOnAxis(ap=slot[:, k, SBT * n + g:SBT * n + g + 1], axis=0)
                        ).then_inc(picked_done[(SBT * n + g) // Q], 16)

        def cols_view(c, i, by_time):
            if not by_time:
                return cols[:, bass.ds(BANK * i + 8 * c * BANK, BANK)]
            v = cols[:, :].rearrange("p (t b) -> p b t", b=B)
            return v[:, bass.ds(Q * i, Q), c * P:(c + 1) * P]

        def load_experts(eng, regs, n, i):
            eng.load(regs, expert[0:1, n, bass.ds(U * i, 2 * U - 1)])
            return [eng.snap(r, min_val=0, max_val=E - 1) for r in regs]

        @block.scalar
        def _(act):
            act.dma_start(a_rows[:, :, :], adj.rearrange("(c p) m -> p c m", p=P)).then_inc(ld_adj, 16)
            for k, w in enumerate((gate_w_in, gate_w_out, loop_gate)):
                act.dma_start(gw[:, k:k + 1], w).then_inc(ld_gnn, 16)
            for k, w in enumerate((gate_b_in, gate_b_out)):
                act.dma_start(gb[:, k, :], w.rearrange("(c p) a -> p (c a)", p=P),
                              allow_slow_non_contiguous=True).then_inc(ld_gnn, 16)
            act.dma_start(bin_sb[:, :, :], bias_in.rearrange("(c p) d -> p c d", p=P)).then_inc(ld_gnn, 16)
            act.dma_start(bout_sb[:, :, :], bias_out.rearrange("(c p) d -> p c d", p=P)).then_inc(ld_gnn, 16)
            for k, (u, v, b) in enumerate(((U_i, V_i, b_i), (U_c, V_c, b_c), (U_o, V_o, b_o))):
                act.dma_start(Ux[:, k, :], u).then_inc(ld_lstm, 16)
                act.dma_start(Vx[:, k, :], v).then_inc(ld_lstm, 16)
                act.dma_start(bl[0:1, k * P:(k + 1) * P],
                              b.rearrange("(a n) -> a n", a=1)).then_inc(ld_lstm, 16)
            act.dma_start(w_in[:, 0:2, :], W1.rearrange("(c p) d -> p c d", p=P)).then_inc(ld_bn, 16)
            act.dma_start(w_in[:, 2:4, :], W2.rearrange("o (c h) -> o c h", h=P)).then_inc(ld_bn, 16)
            for k, v in enumerate((b1, g1, be1)):
                act.dma_start(bn1[:, k, :], v.rearrange("(c p) -> p c", p=P),
                              allow_slow_non_contiguous=True).then_inc(ld_small, 16)
            for k, v in enumerate((b2, g2, be2)):
                act.dma_start(bn2[:, k:k + 1], v.rearrange("(p a) -> p a", a=1)).then_inc(ld_small, 16)
            act.dma_start(wg_sb[:, :], Wg).then_inc(ld_small, 16)
            act.dma_start(bg_sb[:, :], bg.rearrange("(a n) -> a n", a=1).to_broadcast([P, E])).then_inc(ld_small, 16)

            def normalise(n):
                act.wait_ge(stat_done[n], 1)
                with act.Fori(0, GROUPS // 2) as i:
                    for u in range(Q):
                        g = 2 * Q * i + Q + u
                        last = nc.scalar.activation(
                            nrm[:, bass.ds(g, 1), :], rows[:, bass.ds(g, 1), :], ACT.Identity,
                            bias=nmr[:, bass.ds(g, 1)], scale=rstd[:, bass.ds(g, 1)])
                    last.then_inc(nrm_s[n], 1)

            def copy_out(n, by_time=False):
                for c in range(C):
                    with act.Fori(0, 2) as i:
                        for u in (1, 3):
                            act.wait_ge(tp[n], 8 * c + 4 * i + (u + 1))
                            nc.scalar.copy(cols_view(c, 4 * i + u, by_time), ps[:, 4 + u, :] if not by_time
                                           else ps[:, 4 + u, :].rearrange("p (b t) -> p b t", b=Q)
                                           ).then_inc(tp_s[n], 1)

            normalise(0)
            copy_out(0)
            act.wait_ge(gate_ps, 1)
            act.wait_ge(half_bias, 1)
            lgates = ps[:, 0, 0:3 * TILES].rearrange("p (g k) -> p k g", k=3)
            for k in range(3):
                for c in range(C):
                    last = nc.scalar.activation(
                        gates[:, k, c * B:(c + 1) * B], lgates[:, k, c * B:(c + 1) * B], ACT.Tanh,
                        scale=0.5, bias=gbh[:, k, c:c + 1] if k < 2 else 0.0)
            last.then_inc(gate_th, 1)
            act.wait_ge(gate_done, 1)
            for c in range(C):
                def scaled_bias(i):
                    for u in range(2):
                        if c or not isinstance(i, int):
                            act.wait_ge(s1_free, 8 * c + 2 * i + (u - 1))
                        for t in range(Q):
                            g = c * B + 2 * Q * i + (Q * u + t)
                            last = nc.scalar.activation(work[:, u, t, :], bout_sb[:, c, :], ACT.Identity,
                                                        scale=gates[:, 1, bass.ds(g, 1)])
                        last.then_inc(s1_act, 1)
                peeled(act, 4, scaled_bias)
            normalise(1)
            copy_out(1, by_time=True)

            def steps(i, base=0):
                for s in range(2 * STEPS):
                    bank = 3 * (s // STEPS)
                    col = (s % STEPS) * B
                    t = 2 * STEPS * i + s
                    act.wait_ge(z_ig, t + 1)
                    nc.scalar.activation(T[:, 0:2, :], ps[:, bank:bank + 2, col:col + B],
                                         ACT.Tanh).then_inc(t_ig, 1)
                    act.wait_ge(z_o, t + 1)
                    nc.scalar.activation(T[:, 2, :], ps[:, bank + 2, col:col + B],
                                         ACT.Tanh).then_inc(t_o, 1)
                    act.wait_ge(c_new, t + 1)
                    nc.scalar.activation(tc[:, :], cell[:, :], ACT.Tanh, scale=0.5).then_inc(t_c, 1)
            for i in range(BLOCKS // 2):
                steps(i)

            normalise(2)
            with act.Fori(0, 4) as i:
                for u in (1, 3):
                    act.wait_ge(ga, 4 * i + (u + 1))
                    nc.scalar.copy(cols[:, bass.ds(BANK * 4 * i + BANK * u, BANK)],
                                   ps[:, 4 + u, :]).then_inc(ga_s, 1)
            act.wait_ge(ld_small, 128)
            act.wait_ge(slots_zeroed, 16 * SB)

            def hidden(i):
                for k in range(HC):
                    act.wait_ge(hp, HC * i + (k + 1))
                    nc.scalar.activation(h1[:, k, bass.ds(BANK * i, BANK)], ps[:, k, :], ACT.Identity,
                                         bias=bn1[:, 0, k:k + 1]).then_inc(hp_ev, 1)
            with act.Fori(0, GROUPS) as i:
                hidden(i)
            act.wait_ge(bn1_done, 1)
            with act.Fori(0, GROUPS) as i:
                for k in range(HC):
                    v = h1[:, k, bass.ds(BANK * i, BANK)]
                    nc.scalar.activation(v, v, ACT.Relu, bias=bsh[:, k:k + 1],
                                         scale=bsc[:, k:k + 1]).then_inc(relu_done, 1)
            act.wait_ge(bn2_done, 1)
            with act.Fori(0, GROUPS // 2) as i:
                v = cols[:, bass.ds(2 * BANK * i + BANK, BANK)]
                nc.scalar.activation(v, v, ACT.Identity, bias=bsh[:, HC:HC + 1],
                                     scale=bsc[:, HC:HC + 1]).then_inc(y_s, 1)
            normalise(3)
            copy_out(3)
            act.wait_ge(lg_dif, 1)
            nc.scalar.activation(m2[:, :], m2[:, :], ACT.Exp).then_inc(lg_exp, 1)

            def copy_x(tg, v, first):
                act.wait_ge(x_turned, tg + 1)
                if not first:
                    act.wait_ge(up_done, tg - 2)
                nc.scalar.copy(x_T[:, v, :], ps[:, 7, 0:D]).then_inc(x_copied, 1)

            def gelu_of(tg, v, first):
                act.wait_ge(turned, tg + 1)
                if not first:
                    act.wait_ge(down_done, tg - 2)
                nc.scalar.activation(h_T[:, v, :], ps[:, 3 + v, :], ACT.Gelu).then_inc(gelu_done, 1)
            for n in range(SB):
                base = SLOTS * n
                copy_x(base, 0, n == 0)

                def step(i):
                    for u in range(U):
                        t = U * i + u
                        peel = isinstance(i, int)
                        if not (peel and t == SLOTS - 1):
                            copy_x(base + t + 1, (u + 1) % U, peel and n == 0 and t < 2)
                        if not (peel and t == 0):
                            gelu_of(base + t - 1, (u - 1) % U, peel and n == 0 and t < 4)
                staged(act, step)
                gelu_of(base + SLOTS - 1, (SLOTS - 1) % U, False)

        @block.vector
        def _(dve):
            chain = [0]

            def link(ins, times=1):
                chain[0] += times
                ins.then_inc(dch, 1)
                dve.wait_ge(dch, chain[0])

            def rsqrt(y, v, t):
                link(nc.vector.tensor_scalar(t.bitcast(I32), v.bitcast(I32), 1, None,
                                             ALU.logical_shift_right))
                link(nc.vector.tensor_scalar(y.bitcast(I32), t.bitcast(I32), -1.0, RSQRT_MAGIC,
                                             ALU.mult, ALU.add))
                for _ in range(NEWTON):
                    link(nc.vector.scalar_tensor_tensor(out=t, in0=y, scalar=-0.5, in1=y,
                                                        op0=ALU.mult, op1=ALU.mult))
                    link(nc.vector.tensor_tensor(t, t, v, ALU.mult))
                    link(nc.vector.scalar_tensor_tensor(out=y, in0=t, scalar=1.5, in1=y,
                                                        op0=ALU.add, op1=ALU.mult))

            def row_stats(n):
                me, qe = stats[:, :, 1], stats[:, :, 2]
                mo, qo = stats[:, :, 4], stats[:, :, 5]
                link(nc.vector.tensor_tensor(tmp[:, 0, :], me, mo, ALU.subtract))
                link(nc.vector.tensor_tensor(tmp[:, 1, :], qe, qo, ALU.add))
                link(nc.vector.tensor_tensor(tmp[:, 0, :], tmp[:, 0, :], tmp[:, 0, :], ALU.mult))
                link(nc.vector.tensor_scalar(tmp[:, 1, :], tmp[:, 1, :], 1.0 / D, EPS, ALU.mult, ALU.add))
                link(nc.vector.scalar_tensor_tensor(out=tmp[:, 2, :], in0=tmp[:, 0, :], scalar=0.25,
                                                    in1=tmp[:, 1, :], op0=ALU.mult, op1=ALU.add))
                link(nc.vector.tensor_tensor(tmp[:, 3, :], me, mo, ALU.add))
                rsqrt(rstd[:, :], tmp[:, 2, :], tmp[:, 0, :])
                nc.vector.scalar_tensor_tensor(out=nmr[:, :], in0=tmp[:, 3, :], scalar=-0.5,
                                               in1=rstd[:, :], op0=ALU.mult,
                                               op1=ALU.mult).then_inc(stat_done[n], 1)
                dve.wait_ge(stat_done[n], 1)

            def normalise(n):
                with dve.Fori(0, GROUPS // 2) as i:
                    for u in range(Q):
                        g = 2 * Q * i + u
                        last = nc.vector.tensor_scalar(
                            nrm[:, bass.ds(g, 1), :], rows[:, bass.ds(g, 1), :],
                            rstd[:, bass.ds(g, 1)], nmr[:, bass.ds(g, 1)], ALU.mult, ALU.add)
                    last.then_inc(nrm_v[n], 1)

            def copy_out(n, by_time=False):
                for c in range(C):
                    with dve.Fori(0, 2) as i:
                        for u in (0, 2):
                            dve.wait_ge(tp[n], 8 * c + 4 * i + (u + 1))
                            nc.vector.tensor_copy(cols_view(c, 4 * i + u, by_time),
                                                  ps[:, 4 + u, :] if not by_time
                                                  else ps[:, 4 + u, :].rearrange("p (b t) -> p b t", b=Q)
                                                  ).then_inc(tp_v[n], 1)

            def all_tiles_stats():
                with dve.Fori(0, TILES // 8) as i:
                    for u in range(8):
                        last = nc.vector.bn_stats(stats[:, bass.ds(8 * i + u, 1), :].rearrange("p a b -> p (a b)"),
                                                  rows[:, bass.ds(8 * i + u, 1), :].rearrange("p a b -> p (a b)"))
                return last

            for n in range(8):
                dve.wait_ge(ld_x[n], 16)
                for g in range(8 * n, 8 * n + 8):
                    last = nc.vector.bn_stats(stats[:, g, :], rows[:, g, :])
            link(last)
            row_stats(0)
            normalise(0)

            dve.wait_ge(prep_T, 1)
            link(nc.vector.tensor_copy(a_T[:, :, :].rearrange("p c n -> p (c n)"), ps[:, 0, :]))
            dve.wait_ge(prep_T, 2)
            nc.vector.tensor_copy(w_T[:, :, :].rearrange("p c n -> p (c n)"), ps[:, 1, :]).then_inc(prep_used, 1)
            dve.wait_ge(ident_done, 1)
            dve.wait_ge(ld_adj, 16)
            link(nc.vector.tensor_copy(s_rows[:, :, :], a_rows[:, :, :]))
            for c in range(C):
                v = s_rows[:, c, c * P:(c + 1) * P]
                link(nc.vector.tensor_tensor(v, v, ident[:, :], ALU.add))
            link(nc.vector.tensor_reduce(small[:, 0:2], s_rows[:, :, :], AX.X, ALU.add))
            link(nc.vector.tensor_reduce(small[:, 2:4], a_T[:, :, :], AX.X, ALU.add))
            for c in range(C):
                link(nc.vector.tensor_tensor(work[:, 0, c, :], a_rows[:, c, c * P:(c + 1) * P],
                                             ident[:, :], ALU.mult))
            link(nc.vector.tensor_reduce(small[:, 4:6], work[:, 0, 0:2, :], AX.X, ALU.add))
            link(nc.vector.tensor_tensor(small[:, 0:2], small[:, 0:2], small[:, 2:4], ALU.add))
            link(nc.vector.tensor_tensor(small[:, 0:2], small[:, 0:2], small[:, 4:6], ALU.subtract))
            rsqrt(small[:, 6:8], small[:, 0:2], small[:, 8:10])
            for c in range(C):
                last = nc.vector.tensor_scalar(s_rows[:, c, :], s_rows[:, c, :], small[:, 6 + c:7 + c],
                                               None, ALU.mult)
            last.then_inc(s_scaled, 1)
            copy_out(0)
            dve.wait_ge(prep_T, 3)
            for c in range(C):
                last = nc.vector.tensor_scalar(ah_T[:, c, :], ps[:, 3, c * N:(c + 1) * N],
                                               small[:, 6 + c:7 + c], None, ALU.mult)
            last.then_inc(prep_used, 1)
            dve.wait_ge(ld_lstm, 16 * 9)
            for k, half in enumerate((0.5, 1.0, 0.5)):
                nc.vector.tensor_scalar(Ux[:, k, :], Ux[:, k, :], half, None, ALU.mult)
                nc.vector.tensor_scalar(Vx[:, k, :], Vx[:, k, :], 0.5 * half, None, ALU.mult)
                last = nc.vector.tensor_scalar(bl[0:1, k * P:(k + 1) * P], bl[0:1, k * P:(k + 1) * P],
                                               half, None, ALU.mult)
            link(last)

            def split(parts, whole, rest):
                link(nc.vector.tensor_copy(parts[0], whole))
                link(nc.vector.tensor_tensor(rest, whole, parts[0], ALU.subtract))
                link(nc.vector.tensor_copy(parts[1], rest))
                link(nc.vector.tensor_tensor(rest, rest, parts[1], ALU.subtract))
                return nc.vector.tensor_copy(parts[2], rest)
            split([blp[0:1, k, :] for k in range(PARTS)], bl[0:1, :], res[0:1, :]).then_inc(bias_parts, 1)
            dve.wait_ge(bias_parts, 1)
            split([Vp[:, k, :] for k in range(PARTS)], Vx[:, :, :].rearrange("p k h -> p (k h)"),
                  res[:, :]).then_inc(lstm_w, 1)
            dve.wait_ge(ld_gnn, 16 * 7)
            nc.vector.tensor_scalar(gbh[:, :, :], gb[:, :, :], 0.5, None, ALU.mult).then_inc(half_bias, 1)
            dve.wait_ge(gate_th, 1)
            link(nc.vector.tensor_scalar(gates[:, 0:3, :], gates[:, 0:3, :], 0.5, 0.5, ALU.mult, ALU.add))
            nc.vector.tensor_tensor(gates[:, 3, :], gates[:, 0, :], gates[:, 1, :],
                                    ALU.add).then_inc(gate_done, 1)
            dve.wait_ge(gate_done, 1)

            for c in range(C):
                def messages(i):
                    for u in range(2):
                        at = 8 * c + 2 * i + u
                        dve.wait_ge(s1_act, at + 1)
                        w = [work[:, u, t, :] for t in range(Q)]
                        gs = [c * B + 2 * Q * i + (Q * u + t) for t in range(Q)]
                        for t in range(Q):
                            last = nc.vector.scalar_tensor_tensor(
                                out=w[t], in0=bin_sb[:, c, :], scalar=gates[:, 0, bass.ds(gs[t], 1)],
                                in1=w[t], op0=ALU.mult, op1=ALU.add)
                        last.then_inc(mstep, 1)
                        dve.wait_ge(mstep, 3 * at + 1)
                        for t in range(Q):
                            last = nc.vector.scalar_tensor_tensor(
                                out=w[t], in0=nrm[:, bass.ds(gs[t], 1), :].rearrange("p a b -> p (a b)"), scalar=gates[:, 2, bass.ds(gs[t], 1)],
                                in1=w[t], op0=ALU.mult, op1=ALU.add)
                        last.then_inc(mstep, 1)
                        dve.wait_ge(mstep, 3 * at + 2)
                        dve.wait_ge(agg, at + 1)
                        for t in range(Q):
                            last = nc.vector.scalar_tensor_tensor(
                                out=w[t], in0=ps[:, u, t * D:(t + 1) * D],
                                scalar=gates[:, 3, bass.ds(gs[t], 1)], in1=w[t], op0=ALU.mult, op1=ALU.add)
                        last.then_inc(mstep, 1)
                        dve.wait_ge(mstep, 3 * at + 3)
                        nc.vector.scalar_tensor_tensor(
                            out=rows[:, bass.ds(gs[0], Q), :], in0=work[:, u, :, :], scalar=0.0,
                            in1=rows[:, bass.ds(gs[0], Q), :], op0=ALU.max, op1=ALU.add).then_inc(s1_free, 1)
                with dve.Fori(0, 4) as i:
                    messages(i)
            dve.wait_ge(s1_free, GROUPS)
            link(all_tiles_stats(), TILES // 8)
            row_stats(1)
            normalise(1)
            copy_out(1, by_time=True)

            dve.wait_ge(consts, 6)

            def steps(i):
                for s in range(2 * STEPS):
                    t = 2 * STEPS * i + s
                    nc.vector.scalar_tensor_tensor(out=hc[:, :], in0=hs[:, bass.ds(t, 1), :].rearrange("p a b -> p (a b)"),
                                                   scalar=0.5, in1=cell[:, :], op0=ALU.mult,
                                                   op1=ALU.mult).then_inc(c_done, 1)
                    dve.wait_ge(t_ig, t + 1)
                    nc.vector.scalar_tensor_tensor(out=ig[:, :], in0=T[:, 0, :], scalar=1.0, in1=T[:, 1, :],
                                                   op0=ALU.add, op1=ALU.mult).then_inc(c_done, 1)
                    dve.wait_ge(c_done, 2 * t + 2)
                    nc.vector.tensor_tensor(cell[:, :], hc[:, :], ig[:, :], ALU.add).then_inc(c_new, 1)
                    dve.wait_ge(t_o, t + 1)
                    dve.wait_ge(t_c, t + 1)
                    nc.vector.scalar_tensor_tensor(out=h_hi[:, :], in0=T[:, 2, :],
                                                   scalar=1.0, in1=tc[:, :], op0=ALU.add,
                                                   op1=ALU.mult).then_inc(hi_done, 1)
                    nc.vector.scalar_tensor_tensor(out=hs[:, t + 1, :], in0=T[:, 2, :],
                                                   scalar=1.0, in1=tc[:, :], op0=ALU.add,
                                                   op1=ALU.mult).then_inc(h_done, 1)
                    dve.wait_ge(h_done, t + 1)
                    nc.vector.tensor_tensor(h_lo[:, :], hs[:, t + 1, :], h_hi[:, :],
                                            ALU.subtract).then_inc(lo_done, 1)
            for i in range(BLOCKS // 2):
                steps(i)

            with dve.Fori(0, GROUPS // 4) as i:
                for u in range(4):
                    dve.wait_ge(tp[2], 4 * i + (u + 1))
                    v = rows[:, bass.ds(4 * Q * i + Q * u, Q), :].rearrange("p a b -> p (a b)")
                    nc.vector.scalar_tensor_tensor(out=v, in0=ps[:, 4 + u, :], scalar=0.5, in1=v,
                                                   op0=ALU.mult, op1=ALU.add).then_inc(x2_done, 1)
            dve.wait_ge(x2_done, GROUPS)
            link(all_tiles_stats(), TILES // 8)
            row_stats(2)
            normalise(2)
            with dve.Fori(0, 4) as i:
                for u in (0, 2):
                    dve.wait_ge(ga, 4 * i + (u + 1))
                    nc.vector.tensor_copy(cols[:, bass.ds(BANK * 4 * i + BANK * u, BANK)],
                                          ps[:, 4 + u, :]).then_inc(ga_v, 1)
            with dve.Fori(0, GROUPS) as i:
                for k in range(HC):
                    dve.wait_ge(hp_ev, HC * i + (k + 1))
                    last = nc.vector.bn_stats(bst[:, k, bass.ds(i, 1), :].rearrange("p a b -> p (a b)"),
                                              h1[:, k, bass.ds(BANK * i, BANK)])
            link(last, GROUPS)

            def bn_finish(ks, gamma, beta, done):
                n = len(ks)
                k0 = ks[0]
                for k in ks:
                    last = nc.vector.bn_aggr(mv[:, k, :], bst[:, k, :, :].rearrange("p g s -> p (g s)"))
                link(last)
                link(nc.vector.tensor_scalar(small[:, 0:n], mv[:, k0:k0 + n, 1], EPS, None, ALU.add))
                rsqrt(small[:, 2:2 + n], small[:, 0:n], small[:, 4:4 + n])
                link(nc.vector.tensor_tensor(bsc[:, k0:k0 + n], small[:, 2:2 + n], gamma, ALU.mult))
                link(nc.vector.tensor_tensor(small[:, 0:n], mv[:, k0:k0 + n, 0], bsc[:, k0:k0 + n], ALU.mult))
                nc.vector.tensor_tensor(bsh[:, k0:k0 + n], beta, small[:, 0:n],
                                        ALU.subtract).then_inc(done, 1)
                dve.wait_ge(done, 1)
            dve.wait_ge(ld_small, 128)
            bn_finish([0, 1], bn1[:, 1, :], bn1[:, 2, :], bn1_done)
            with dve.Fori(0, GROUPS // 2) as i:
                for u in range(2):
                    dve.wait_ge(op, 2 * i + (u + 1))
                    v = cols[:, bass.ds(2 * BANK * i + BANK * u, BANK)]
                    nc.vector.tensor_scalar(v, ps[:, 2 + u, :], bn2[:, 0:1], None, ALU.add).then_inc(op_ev, 1)
                    dve.wait_ge(op_ev, 2 * i + (u + 1))
                    last = nc.vector.bn_stats(bst[:, HC, bass.ds(2 * i + u, 1), :].rearrange("p a b -> p (a b)"), v)
            link(last, GROUPS // 2)
            bn_finish([2], bn2[:, 1:2], bn2[:, 2:3], bn2_done)
            with dve.Fori(0, GROUPS // 2) as i:
                v = cols[:, bass.ds(2 * BANK * i, BANK)]
                nc.vector.tensor_scalar(v, v, bsc[:, HC:HC + 1], bsh[:, HC:HC + 1],
                                        ALU.mult, ALU.add).then_inc(y_v, 1)
            with dve.Fori(0, GROUPS // 4) as i:
                for u in range(4):
                    dve.wait_ge(tp[4], 4 * i + (u + 1))
                    v = rows[:, :, :].rearrange("p (c b) d -> p b c d", c=C)[:, bass.ds(8 * i + 2 * u, 2), :, :]
                    s = ps[:, 4 + u, :].rearrange("p (b c d) -> p b c d", b=2, c=C)
                    nc.vector.tensor_tensor(v, v, s, ALU.add).then_inc(x3_done, 1)
            dve.wait_ge(x3_done, GROUPS)
            link(all_tiles_stats(), TILES // 8)
            row_stats(3)
            normalise(3)
            copy_out(3)

            dve.wait_ge(lg, 1)
            lps = ps[:, 0, :].rearrange("p (g e) -> p g e", e=E)

            def over(v):
                return v.unsqueeze(2).to_broadcast([P, TILES, E])

            def each(v):
                return v.unsqueeze(1).to_broadcast([P, TILES, E])

            def first_of(mask, m, scratch):
                link(nc.vector.tensor_tensor(scratch, logit[:, :, :], over(m), ALU.is_equal))
                link(nc.vector.tensor_tensor(scratch, scratch, each(pos[:, :]), ALU.mult))
                link(nc.vector.tensor_reduce(tmp[:, 0, :], scratch, AX.X, ALU.max))
                link(nc.vector.tensor_tensor(mask, scratch, over(tmp[:, 0, :]), ALU.is_equal))
            link(nc.vector.tensor_tensor(logit[:, :, :], lps, each(bg_sb[:, :]), ALU.add))
            link(nc.vector.tensor_reduce(m1[:, :], logit[:, :, :], AX.X, ALU.max))
            first_of(mk[0], m1[:, :], mk[2])
            link(nc.vector.scalar_tensor_tensor(out=logit[:, :, :], in0=mk[0], scalar=-1e30,
                                                in1=logit[:, :, :], op0=ALU.mult, op1=ALU.add))
            link(nc.vector.tensor_reduce(m2[:, :], logit[:, :, :], AX.X, ALU.max))
            first_of(mk[1], m2[:, :], mk[2])
            nc.vector.tensor_tensor(m2[:, :], m2[:, :], m1[:, :], ALU.subtract).then_inc(lg_dif, 1)
            dve.wait_ge(lg_exp, 1)
            link(nc.vector.tensor_scalar(tmp[:, 0, :], m2[:, :], 1.0, None, ALU.add))
            link(nc.vector.reciprocal(tmp[:, 1, :], tmp[:, 0, :]))
            link(nc.vector.tensor_tensor(tmp[:, 2, :], tmp[:, 1, :], m2[:, :], ALU.mult))
            weight = [tmp[:, 1, :], tmp[:, 2, :]]
            flat = [v[:, :, :].rearrange("p g e -> p (g e)") for v in mk]
            nc.vector.tensor_tensor(mark[:, :], flat[0], flat[1], ALU.add).then_inc(marked, 1)
            dve.wait_ge(ranked, 1)
            tot = logit[:, :, :].rearrange("p g e -> p (g e)")
            rank = flat[2]
            link(nc.vector.tensor_copy(rank, ps[:, 1, :]))
            link(nc.vector.tensor_copy(tot, ps[:, 2, :]))
            link(nc.vector.tensor_copy(run[0], tot))

            def blocks(v):
                return v.rearrange("p (s r) -> p s r", s=SB)
            src, dst, step = 0, 1, 1
            while step < SBT:
                a, b = blocks(run[src]), blocks(run[dst])
                nc.vector.tensor_copy(b[:, :, 0:step * E], a[:, :, 0:step * E])
                link(nc.vector.tensor_tensor(b[:, :, step * E:], a[:, :, step * E:],
                                             a[:, :, :SBT * E - step * E], ALU.add))
                src, dst, step = dst, src, 2 * step
            count = blocks(run[src])[:, :, (SBT - 1) * E:]
            link(nc.vector.tensor_scalar(iends[:, :].rearrange("p (s e) -> p s e", s=SB), count,
                                         float(P - 1), None, ALU.add))
            link(nc.vector.tensor_scalar(iends[:, :], iends[:, :], 7, None, ALU.arith_shift_right))
            link(nc.vector.tensor_copy(ends[:, 0, :], iends[:, :]))
            link(nc.vector.tensor_copy(ends[:, 1, :], ends[:, 0, :]))
            at_, to, step = 1, 2, 1
            while step < E:
                a = ends[:, at_, :].rearrange("p (s e) -> p s e", s=SB)
                b = ends[:, to, :].rearrange("p (s e) -> p s e", s=SB)
                nc.vector.tensor_copy(b[:, :, 0:step], a[:, :, 0:step])
                link(nc.vector.tensor_tensor(b[:, :, step:], a[:, :, step:], a[:, :, :E - step], ALU.add))
                at_, to, step = to, at_, 2 * step
            end = ends[:, at_, :]
            link(nc.vector.tensor_tensor(ends[:, 0, :], end, ends[:, 0, :], ALU.subtract))
            link(nc.vector.tensor_scalar(ends[:, 0, :], ends[:, 0, :], float(P), None, ALU.mult))
            link(nc.vector.tensor_tensor(rank, rank, run[src], ALU.add))
            link(nc.vector.tensor_tensor(rank, rank, tot, ALU.subtract))
            for n in range(SB):
                v = mk[2][:, n * SBT:(n + 1) * SBT, :]
                last = nc.vector.tensor_tensor(
                    v, v, ends[:, 0, n * E:(n + 1) * E].unsqueeze(1).to_broadcast([P, SBT, E]), ALU.add)
            link(last)
            for k in range(TOP):
                link(nc.vector.tensor_tensor(mk[k][:, :, :], mk[k][:, :, :], mk[2][:, :, :], ALU.mult))
                link(nc.vector.tensor_reduce(m1[:, :], mk[k][:, :, :], AX.X, ALU.add))
                nc.vector.tensor_copy(slot[:, k, :], m1[:, :]).then_inc(slots_done, 1)
            for n in range(SB):
                v = logit[0:1, 0:SLOTS, :]
                link(nc.vector.tensor_tensor(
                    v, tile_no[:, :].unsqueeze(2).to_broadcast([1, SLOTS, E]),
                    end[0:1, n * E:(n + 1) * E].unsqueeze(1).to_broadcast([1, SLOTS, E]), ALU.is_ge))
                link(nc.vector.tensor_reduce(m2[0:1, 0:SLOTS], v, AX.X, ALU.add))
                nc.vector.tensor_scalar(expert[0:1, n, U - 1:U - 1 + SLOTS], m2[0:1, 0:SLOTS],
                                        float(E - 1), None, ALU.min).then_inc(experts_known, 1)
            dve.wait_ge(experts_known, SB)
            dve.wait_ge(ld_moe, 16 * (2 * E + 2))

            e_regs = [dve.alloc_register(f"dve_e{n}") for n in range(2 * U - 1)]

            def add_bias(tg, v, e, first):
                dve.wait_ge(up_done, tg + 1)
                if not first:
                    dve.wait_ge(turned, tg - 2)
                nc.vector.tensor_tensor(h_pre[:, v, :], ps[:, v, :], b1e[:, bass.ds(e * F, F)],
                                        ALU.add).then_inc(biased, 1)

            def finish_rows(tg, rounds, v, e, first):
                dve.wait_ge(down_done, tg + 1)
                if not first:
                    dve.wait_ge(y_stored[v], 16 * rounds)
                nc.vector.tensor_tensor(y_out[:, v, :], ps[:, 6, 0:D], b2e[:, bass.ds(e * D, D)],
                                        ALU.add).then_inc(y_done, 1)

            def mix(n):
                for q in range(4 * n, 4 * n + 4):
                    dve.wait_ge(picked_done[q], 16 * TOP * Q)
                    for k in range(TOP):
                        for g in range(Q * q, Q * q + Q):
                            last = nc.vector.scalar_tensor_tensor(
                                out=rows[:, g, :], in0=picked[:, n % 2, k, g - SBT * n, :],
                                scalar=weight[k][:, g:g + 1], in1=rows[:, g, :], op0=ALU.mult, op1=ALU.add)
                        last.then_inc((mix_step, mix_done)[k], 1)
                        if k == 0:
                            dve.wait_ge(mix_step, q + 1)
            for n in range(SB):
                base = SLOTS * n

                def step(i):
                    es = load_experts(dve, e_regs, n, i)
                    for u in range(U):
                        t = U * i + u
                        peel = isinstance(i, int)
                        add_bias(base + t, u, es[u + 2], peel and n == 0 and t < 3)
                        if not (peel and t < 2):
                            r = i + (n * ITERS) + (1 if u == 2 else 0) - 1
                            finish_rows(base + t - 2, r, (u - 2) % U, es[u], peel and n == 0 and t < 5)
                staged(dve, step)
                es = load_experts(dve, e_regs, n, ITERS)
                for t in (SLOTS - 2, SLOTS - 1):
                    finish_rows(base + t, ITERS * (n + 1) - 1, t % U, es[t - SLOTS + 2], False)
                if n >= 1:
                    mix(n - 1)
            mix(SB - 1)

        @block.tensor
        def _(pe):
            def transposes(n, source, ready):
                for q in range(GROUPS):
                    ready(q)
                    if q >= 4:
                        if q % 2 == 0:
                            pe.wait_ge(tp_v[n], (q - 4) // 2 + 1)
                        else:
                            pe.wait_ge(tp_s[n], (q - 5) // 2 + 1)
                    for t in range(Q):
                        last = nc.tensor.transpose(ps[:, 4 + q % 4, t * P:(t + 1) * P], source(q, t),
                                                   ident[:, :])
                    last.then_inc(tp[n], 1)

            def normalised(n):
                def ready(q):
                    pe.wait_ge(nrm_v[n] if q % 2 == 0 else nrm_s[n], q // 2 + 1)
                return ready

            pe.wait_ge(ident_done, 1)
            pe.wait_ge(ld_adj, 16)
            for cm in range(C):
                for cn in range(C):
                    last = nc.tensor.transpose(ps[:, 0, (cm * C + cn) * P:(cm * C + cn + 1) * P],
                                               a_rows[:, cn, cm * P:(cm + 1) * P], ident[:, :])
            last.then_inc(prep_T, 1)
            pe.wait_ge(ld_bn, 32)
            for k in range(4):
                last = nc.tensor.transpose(ps[:, 1, k * P:(k + 1) * P], w_in[:, k, :], ident[:, :])
            last.then_inc(prep_T, 1)
            transposes(0, lambda q, t: nrm[:, Q * q + t, :], normalised(0))
            pe.wait_ge(s_scaled, 1)
            for cm in range(C):
                for cn in range(C):
                    last = nc.tensor.transpose(ps[:, 3, (cm * C + cn) * P:(cm * C + cn + 1) * P],
                                               s_rows[:, cn, cm * P:(cm + 1) * P], ident[:, :])
            last.then_inc(prep_T, 1)
            pe.wait_ge(ld_gnn, 16 * 7)
            pe.wait_ge(prep_used, 2)
            for g in range(TILES):
                if g % Q == 0:
                    q = g // Q
                    pe.wait_ge(tp_v[0] if q % 2 == 0 else tp_s[0], q // 2 + 1)
                last = nc.tensor.matmul(ps[:, 0, 3 * g:3 * g + 3], cols[:, g * P:(g + 1) * P], gw[:, :],
                                        start=True, stop=True)
            last.then_inc(gate_ps, 1)
            pe.wait_ge(gate_th, 1)
            for c in range(C):
                def aggregate(i):
                    for u in range(2):
                        if c or not isinstance(i, int):
                            pe.wait_ge(mstep, 24 * c + 6 * i + (3 * u - 3))
                        for cm in range(C):
                            last = nc.tensor.matmul(
                                ps[:, u, :], a_T[:, cm, c * P:(c + 1) * P],
                                nrm[:, bass.ds(cm * B + 2 * Q * i + Q * u, Q), :].rearrange("p a b -> p (a b)"),
                                start=(cm == 0), stop=(cm == C - 1))
                        last.then_inc(agg, 1)
                peeled(pe, 4, aggregate)
            transposes(1, lambda q, t: nrm[:, Q * q + t, :], normalised(1))

            def gate_inputs(blk, bank0, k, quarter):
                o = ps[:, bank0 + k, quarter * P:(quarter + 1) * P]
                nc.tensor.matmul(o, bp[:, k * P:(k + 1) * P], ones_bf[:, :], start=(quarter == 0),
                                 stop=True, skip_group_check=True)
                return nc.tensor.matmul(o, Ux[:, k, :], cols[:, bass.ds(blk * BANK + quarter * P, P)],
                                        start=False, stop=True, skip_group_check=True)
            pe.wait_ge(lstm_w, 1)
            pe.wait_ge(ld_bp, 16 * PARTS)
            pe.wait_ge(consts, 6)
            pe.wait_ge(tp_v[1], GROUPS // 2)
            pe.wait_ge(tp_s[1], GROUPS // 2)
            pe.wait_ge(s1_free, GROUPS)
            for k in range(GATES):
                for quarter in range(Q):
                    gate_inputs(0, 0, k, quarter)

            def steps(i, last_round):
                for s in range(2 * STEPS):
                    bank0 = 3 * (s // STEPS)
                    col = (s % STEPS) * B
                    t = 2 * STEPS * i + s

                    def product(k, h, last=None):
                        for part in range(PARTS):
                            mm = nc.tensor.matmul(ps[:, bank0 + k, col:col + B],
                                                  Vp[:, part, k * P:(k + 1) * P], h[:, :],
                                                  start=False, stop=True, skip_group_check=True)
                        if last is not None:
                            mm.then_inc(last, 1)
                    if t:
                        pe.wait_ge(hi_done, t)
                        for k in range(GATES):
                            product(k, h_hi)
                        pe.wait_ge(lo_done, t)
                    for k in range(GATES):
                        product(k, h_lo if t else h_zero, (None, z_ig, z_o)[k])
                    piece = s % STEPS
                    if piece < GATES * Q and not (last_round and s >= STEPS):
                        gate_inputs(2 * i + (s // STEPS + 1), 3 - bank0, piece // Q, piece % Q)
            steps(0, False)
            for i in range(1, BLOCKS // 2 - 1):
                steps(i, False)
            steps(BLOCKS // 2 - 1, True)

            pe.wait_ge(h_done, N)

            def bank_read(q):
                if q >= 4:
                    pe.wait_ge(x2_done, q - 3)
            for q in range(GROUPS):
                bank_read(q)
                for t in range(Q):
                    g = Q * q + t
                    c, b = g // B, g % B
                    last = nc.tensor.transpose(ps[:, 4 + q % 4, t * P:(t + 1) * P],
                                               hs[:, 1 + c * P:1 + (c + 1) * P, b], ident[:, :])
                last.then_inc(tp[2], 1)
            pe.wait_ge(nrm_v[2], GROUPS // 2)
            pe.wait_ge(nrm_s[2], GROUPS // 2)
            for q in range(GROUPS):
                if q >= 4:
                    pe.wait_ge(ga_v if q % 2 == 0 else ga_s, (q - 4) // 2 + 1)
                for t in range(2):
                    b = 2 * q + t
                    for cm in range(C):
                        last = nc.tensor.matmul(ps[:, 4 + q % 4, t * N:(t + 1) * N],
                                                nrm[:, cm * B + b, :], ah_T[:, cm, :],
                                                start=(cm == 0), stop=(cm == C - 1))
                last.then_inc(ga, 1)
            pe.wait_ge(ga_v, GROUPS // 2)
            pe.wait_ge(ga_s, GROUPS // 2)

            def hidden(i):
                for k in range(HC):
                    if not isinstance(i, int):
                        pe.wait_ge(hp_ev, HC * i + (k - 1))
                    nc.tensor.matmul(ps[:, k, :], w_T[:, k, :], cols[:, bass.ds(BANK * i, BANK)],
                                     start=True, stop=True).then_inc(hp, 1)
            peeled(pe, GROUPS, hidden)

            def output_layer(i):
                for u in range(2):
                    if not isinstance(i, int):
                        pe.wait_ge(op_ev, 2 * i + (u - 1))
                    for k in range(HC):
                        pe.wait_ge(relu_done, 4 * i + (2 * u + k + 1))
                        last = nc.tensor.matmul(ps[:, 2 + u, :], w_T[:, 2 + k, :],
                                                h1[:, k, bass.ds(2 * BANK * i + BANK * u, BANK)],
                                                start=(k == 0), stop=(k == HC - 1))
                    last.then_inc(op, 1)
            peeled(pe, GROUPS // 2, output_layer)
            for q in range(GROUPS):
                pe.wait_ge(y_v if q % 2 == 0 else y_s, q // 2 + 1)
                if q >= 4:
                    pe.wait_ge(x3_done, q - 3)
                for t in range(Q):
                    last = nc.tensor.transpose(ps[:, 4 + q % 4, t * P:(t + 1) * P],
                                               cols[:, (Q * q + t) * P:(Q * q + t + 1) * P], ident[:, :])
                last.then_inc(tp[4], 1)
            transposes(3, lambda q, t: nrm[:, Q * q + t, :], normalised(3))
            pe.wait_ge(ld_small, 128)
            for g in range(TILES):
                if g % Q == 0:
                    q = g // Q
                    pe.wait_ge(tp_v[3] if q % 2 == 0 else tp_s[3], q // 2 + 1)
                last = nc.tensor.matmul(ps[:, 0, E * g:E * g + E], cols[:, g * P:(g + 1) * P], wg_sb[:, :],
                                        start=True, stop=True)
            last.then_inc(lg, 1)
            pe.wait_ge(marked, 1)
            pe.wait_ge(consts, 11)
            nc.tensor.matmul(ps[:, 1, :], before[:, :], mark[:, :], start=True, stop=True)
            nc.tensor.matmul(ps[:, 2, :], all_ones[:, :], mark[:, :], start=True, stop=True).then_inc(ranked, 1)
            pe.wait_ge(ld_moe, 16 * (2 * E + 2))
            pe.wait_ge(experts_known, SB)
            e_regs = [pe.alloc_register(f"pe_e{n}") for n in range(2 * U - 1)]

            def turn_x(tg, rounds, v, first):
                pe.wait_ge(x_loaded[v], 16 * rounds)
                if not first:
                    pe.wait_ge(x_copied, tg)
                nc.tensor.transpose(ps[:, 7, 0:P], x_in[:, v, :], ident[:, :]).then_inc(x_turned, 1)

            def up(tg, v, e, first):
                pe.wait_ge(x_copied, tg + 1)
                if not first:
                    pe.wait_ge(biased, tg - 2)
                nc.tensor.matmul(ps[:, v, :], x_T[:, v, :], w1e[:, bass.ds(e * F, F)],
                                 start=True, stop=True).then_inc(up_done, 1)

            def turn_h(tg, v, first):
                pe.wait_ge(biased, tg + 1)
                if not first:
                    pe.wait_ge(gelu_done, tg - 2)
                for j in range(J):
                    last = nc.tensor.transpose(ps[:, 3 + v, j * P:(j + 1) * P],
                                               h_pre[:, v, j * P:(j + 1) * P], ident[:, :])
                last.then_inc(turned, 1)

            def down(tg, v, e, first):
                pe.wait_ge(gelu_done, tg + 1)
                if not first:
                    pe.wait_ge(y_done, tg)
                for j in range(J):
                    last = nc.tensor.matmul(ps[:, 6, 0:D], h_T[:, v, j * P:(j + 1) * P],
                                            w2e[:, bass.ds(e * F + j * D, D)],
                                            start=(j == 0), stop=(j == J - 1))
                last.then_inc(down_done, 1)
            for n in range(SB):
                base = SLOTS * n
                turn_x(base, n * ITERS + 1, 0, n == 0)

                def step(i):
                    es = load_experts(pe, e_regs, n, i)
                    for u in range(U):
                        t = U * i + u
                        peel = isinstance(i, int)
                        if not (peel and t == SLOTS - 1):
                            turn_x(base + t + 1, i + (n * ITERS + 1 + (u == U - 1)), (u + 1) % U, False)
                        up(base + t, u, es[u + 2], peel and n == 0 and t < 3)
                        if not (peel and t < 1):
                            turn_h(base + t - 1, (u - 1) % U, peel and n == 0 and t < 4)
                        if not (peel and t < 2):
                            down(base + t - 2, (u - 2) % U, es[u], peel and n == 0 and t < 3)
                staged(pe, step)
                es = load_experts(pe, e_regs, n, ITERS)
                turn_h(base + SLOTS - 1, (SLOTS - 1) % U, False)
                for t in (SLOTS - 2, SLOTS - 1):
                    down(base + t, t % U, es[t - SLOTS + 2], False)


_ARGS = {"x": "x", "adj": "adj"}
_ARGS |= {k: "L0_gnn_" + k for k in ("bias_in", "bias_out", "gate_w_in", "gate_b_in", "gate_w_out",
                                    "gate_b_out", "loop_gate")}
_ARGS |= {k: "L0_ffn_" + k for k in ("U_i", "V_i", "b_i", "U_c", "V_c", "b_c", "U_o", "V_o", "b_o")}
_ARGS |= {k: "L1_gnn_" + k for k in ("W1", "b1", "g1", "be1", "W2", "b2", "g2", "be2")}
_ARGS |= {"Wg": "L1_ffn_Wg", "bg": "L1_ffn_bg", "mW1": "L1_ffn_W1", "mb1": "L1_ffn_b1",
          "mW2": "L1_ffn_W2", "mb2": "L1_ffn_b2"}


def kernel(**inputs):
    import numpy as np
    import concourse.bacc as bacc
    from concourse.bass_utils import run_bass_kernel_spmd

    nc = bacc.Bacc("TRN2", target_bir_lowering=False, num_devices=1)
    arrays, args = {}, {}
    for arg, name in _ARGS.items():
        a = np.ascontiguousarray(inputs[name])
        arrays[name] = a
        args[arg] = nc.dram_tensor(name, a.shape, mybir.dt.from_np(a.dtype), kind="ExternalInput").ap()
    out = nc.dram_tensor("out", (B, N, D), F32, kind="ExternalOutput").ap()
    build(nc, out=out, **args)
    r = run_bass_kernel_spmd(nc, [arrays], core_ids=[0])
    return r.results[0]["out"]
```

```python
from contextlib import ExitStack

import concourse.bass as bass
from concourse import mybir

F32 = mybir.dt.float32
BF16 = mybir.dt.bfloat16
F16 = mybir.dt.float16
I32 = mybir.dt.int32
U32 = mybir.dt.uint32
ALU = mybir.AluOpType
ACT = mybir.ActivationFunctionType
AX = mybir.AxisListType

B, N, D = 32, 256, 128
P = 128
C = N // P
TILES = C * B
Q = 4
GROUPS = TILES // Q
BANK = Q * P
H1 = 256
HC = H1 // P
E, F = 8, 512
J = F // P
GATES = 3
STEPS = BANK // B
BLOCKS = N // STEPS
EPS = 1e-5
RSQRT_MAGIC = float(0x5F3759DF)
NEWTON = 3
TOP = 2
PREP = (6, 8, 10, 6)
LAG = 4
SIZES = (7, 25, 25, 7)
SB = len(SIZES)
EARLY = -(-SIZES[0] // Q)
ROUTE_1, ROUTE_2 = 11, 15
COPY_1 = EARLY + 5
TURN_1, RANK_1 = 4, 7
FIRST = [sum(SIZES[:n]) for n in range(SB + 1)]
SLOTS = [TOP * n + E - 1 for n in SIZES]
STORED_EARLY = 6
ZERO_TILES = 21
ZERO_DMAS = sum(-(-n // ZERO_TILES) for n in SLOTS)
U = 3
ROUNDS = [n // U for n in SLOTS]
PER_LOAD = 4
TABLE = max(SLOTS) + 2 * U - 1
AGG_1 = 0
CHAIN = 6 + 2 + 3 * NEWTON + 1
FINISH_1 = AGG_1 + 2 * B + 3
NORM_1 = FINISH_1 + CHAIN + 1
X2_2 = N // C + 2
FINISH_2 = X2_2 + B + 3
NORM_2 = FINISH_2 + CHAIN + 1
DEGREES = 12 + 2 + 3 * NEWTON
ADJ = FINISH_2 + CHAIN + 1
assert ADJ + DEGREES + 2 * C < N
assert NORM_1 + B // 2 + 2 <= N // C - STEPS and NORM_2 + B // 2 < N
PARTS = 3


def staged(eng, rounds, body):
    body(0)
    body(1)
    with eng.Fori(2, rounds - 1) as i:
        body(i)
    body(rounds - 1)


def peeled(eng, n, body):
    body(0)
    if n > 1:
        with eng.Fori(1, n) as i:
            body(i)


assert E * GROUPS == P and E * (2 * GROUPS - 1) <= BANK
assert FIRST[SB] == TILES and all(n % U == 0 and (n // U - 3) % PER_LOAD == 0 and n // U > 3 for n in SLOTS)


def build(nc, x, adj, bias_in, bias_out, gate_w_in, gate_b_in, gate_w_out, gate_b_out, loop_gate,
          U_i, V_i, b_i, U_c, V_c, b_c, U_o, V_o, b_o, W1, b1, g1, be1, W2, b2, g2, be2,
          Wg, bg, mW1, mb1, mW2, mb2, out):
    x_v = x.rearrange("b (c p) d -> p c b d", p=P)
    out_v = out.rearrange("b (c p) d -> p c b d", p=P)
    ctx = ExitStack()
    with ctx:
        def sb(name, shape, dt=F32):
            return ctx.enter_context(nc.sbuf_tensor(name, shape, dt))

        def sem(name):
            return ctx.enter_context(nc.semaphore(name))

        rows = sb("rows", [P, TILES, D])
        nrm = sb("nrm", [P, TILES, D])
        cols = sb("cols", [P, TILES * P])
        hid = sb("hid", [P, HC * TILES * P])
        hs = hid[:, 0:(N + 1) * B].rearrange("p (t b) -> p t b", b=B)
        h1 = hid[:, :].rearrange("p (c r) -> p c r", c=HC)
        at = 0

        def of_hid(n):
            nonlocal at
            at += n
            return hid[:, at - n:at]
        w1e = of_hid(E * F)
        w2e = of_hid(E * F)
        b1e = of_hid(E * F)
        b2e = of_hid(E * D)
        h_pre = of_hid(U * F).rearrange("p (u f) -> p u f", u=U)
        h_T = of_hid(U * F).rearrange("p (u f) -> p u f", u=U)
        zeros = hid[:, (N + 1) * B:(N + 1) * B + ZERO_TILES * D]
        at = (N + 1) * B + ZERO_TILES * D
        msg = hid[:, at:at + B * D].rearrange("p (b d) -> p b d", b=B)
        nrm_1 = hid[:, (N // C + 1) * B:(N + 1) * B].rearrange("p (b d) -> p b d", b=B)
        sums = nrm_1
        msg2 = hid[:, at + B * D:at + B * D + 1024].rearrange("p (b d) -> p b d", d=D)
        picked = [cols[:, :].rearrange("p (g d) -> p g d", d=D), nrm]
        x_slots, y_slots = ([nc.dram_tensor(f"{v}_slots{n}", (SLOTS[n] * P, D), F32, kind="Internal").ap()
                             for n in range(SB)] for v in "xy")

        ident = sb("ident", [P, P])
        a_rows = sb("a_rows", [P, C, N])
        s_rows = sb("s_rows", [P, C, N])
        a_T = sb("a_T", [P, C, N])
        ah_T = sb("ah_T", [P, C, N])
        bin_sb = sb("bin_sb", [P, C, D])
        bout_sb = sb("bout_sb", [P, C, D])
        gw = sb("gw", [P, 3])
        CG = GROUPS // C
        gw_wide = sb("gw_wide", [P, 3 * (2 * CG - 1)])
        gb = sb("gb", [P, 2, C])
        gbh = sb("gbh", [P, 2, C])
        gates = sb("gates", [P, 4, TILES])
        Ux = sb("Ux", [P, GATES, P])
        Vx = sb("Vx", [P, GATES, P])
        bl = sb("bl", [1, GATES * P])
        Vp = sb("Vp", [P, PARTS, GATES * P], BF16)
        blp = sb("blp", [1, PARTS, GATES * P], BF16)
        bp = sb("bp", [PARTS, GATES * P], BF16)
        res = sb("res", [P, GATES * P])
        ones_bf = sb("ones_bf", [PARTS, P], BF16)
        h_hi = sb("h_hi", [P, B], F16)
        h_lo = sb("h_lo", [P, B], F16)
        h_zero = sb("h_zero", [P, B], F16)
        w_in = sb("w_in", [P, 4, P])
        w_T = sb("w_T", [P, 4, P])
        bn1 = sb("bn1", [P, 3, HC])
        bn2 = sb("bn2", [P, 3])
        wg_sb = sb("wg_sb", [P, E])
        bg_sb = sb("bg_sb", [P, E])
        stats = sb("stats", [P, TILES, 6])
        bst = sb("bst", [P, HC + 1, GROUPS, 6])
        tmp = sb("tmp", [P, 4, TILES])
        rstd = sb("rstd", [P, TILES])
        nmr = sb("nmr", [P, TILES])
        small = sb("small", [P, 16])
        mv = sb("mv", [P, HC + 1, 2])
        bsc = sb("bsc", [P, HC + 1])
        bsh = sb("bsh", [P, HC + 1])
        work = sb("work", [P, 2, Q, D])
        gates_T = work[0:3 * CG, 1, :, :].rearrange("p q d -> p (q d)")
        wg_wide = work[:, 1, :, :].rearrange("p q d -> p (q d)")[:, 0:(2 * GROUPS - 1) * E]
        logits_T = work[:, 0, :, :].rearrange("p q d -> p (q d)")
        T = sb("T", [P, 3, B])
        hc = sb("hc", [P, B])
        ig = sb("ig", [P, B])
        logit = sb("logit", [P, TILES, E])
        m1 = sb("m1", [P, TILES])
        m2 = sb("m2", [P, TILES])
        pos = sb("pos", [P, E])
        x_in = sb("x_in", [P, U, D])
        x_T = sb("x_T", [P, U, D])
        y_out = sb("y_out", [P, U, D])
        before = sb("before", [P, P], BF16)
        all_ones = sb("all_ones", [P, P], BF16)
        mark = sb("mark", [P, TILES * E], BF16)
        ends = sb("ends", [P, 3, SB * E])
        iends = sb("iends", [P, SB * E], I32)
        slot = sb("slot", [P, TOP, TILES], U32)
        tile_no = sb("tile_no", [1, max(SLOTS)])
        expert = sb("expert", [1, SB, TABLE], I32)
        ps = ctx.enter_context(nc.psum_tensor("ps", [P, 8, BANK], F32))
        cell, tc = ps[:, 7, 0:B], ps[:, 7, 2 * B:3 * B]
        mk = [h_T[:, k, :].rearrange("p (g e) -> p g e", e=E) for k in range(3)]
        run = [h_pre[:, 0, :], h_pre[:, 1, :]]
        run_table = h_pre[:, 2, :].rearrange("p (t e) -> p t e", e=E)

        ld_x = [sem(f"ld_x{n}") for n in range(8)]
        ld_adj = sem("ld_adj")
        ld_gnn = sem("ld_gnn")
        ld_lstm = sem("ld_lstm")
        ld_bn = sem("ld_bn")
        ld_small = sem("ld_small")
        ld_moe = sem("ld_moe")
        zeros_set = sem("zeros_set")
        slots_zeroed = sem("slots_zeroed")
        marked = sem("marked")
        ranked = sem("ranked")
        slots_done = sem("slots_done")
        experts_known = sem("experts_known")
        scattered = [sem(f"scattered{n}") for n in range(SB)]
        x_loaded = [sem(f"x_loaded{n}") for n in range(U)]
        x_turned = sem("x_turned")
        x_copied = sem("x_copied")
        up_done = sem("up_done")
        biased = sem("biased")
        turned = sem("turned")
        gelu_done = sem("gelu_done")
        down_done = sem("down_done")
        y_done = sem("y_done")
        y_stored = [sem(f"y_stored{n}") for n in range(U)]
        picked_done = [sem(f"picked{n}") for n in range(SB)]
        mix_step = sem("mix_step")
        mix_done = sem("mix_done")
        ident_done = sem("ident_done")
        consts = sem("consts")
        dch = sem("dch")
        prep_T = sem("prep_T")
        prep_used = sem("prep_used")
        fill_adj = sem("fill_adj")
        fill_adj_T = sem("fill_adj_T")
        ah_done = sem("ah_done")
        half_bias = sem("half_bias")
        stat_done = [sem(f"stat_done{n}") for n in range(6)]
        nrm_v = [sem(f"nrm_v{n}") for n in range(4)]
        nrm_s = [sem(f"nrm_s{n}") for n in range(4)]
        tp = [sem(f"tp{n}") for n in range(5)]
        tp_v = [sem(f"tp_v{n}") for n in range(5)]
        tp_s = [sem(f"tp_s{n}") for n in range(5)]
        tp_c1 = sem("tp_c1")
        cp_c1 = sem("cp_c1")
        gw_ready = sem("gw_ready")
        gate_acc = sem("gate_acc")
        gate_copied = sem("gate_copied")
        gate_ps = sem("gate_ps")
        gate_th = sem("gate_th")
        gate_done = sem("gate_done")
        agg = sem("agg")
        agg_used = sem("agg_used")
        s1_act = sem("s1_act")
        s1_free = sem("s1_free")
        msg_step = sem("msg_step")
        fill_agg = sem("fill_agg")
        fill_msg = sem("fill_msg")
        fill_x = sem("fill_x")
        fill_st = sem("fill_st")
        fill_chain = sem("fill_chain")
        fill_nrm = sem("fill_nrm")
        fill_T = sem("fill_T")
        fill_cols = sem("fill_cols")
        late_T = sem("late_T")
        late_x = sem("late_x")
        late_nrm = sem("late_nrm")
        mstep = sem("mstep")
        lstm_w = sem("lstm_w")
        bias_parts = sem("bias_parts")
        ld_bp = sem("ld_bp")
        hi_done = sem("hi_done")
        lo_done = sem("lo_done")
        first_in = sem("first_in")
        z_ig = sem("z_ig")
        z_o = sem("z_o")
        t_ig = sem("t_ig")
        t_o = sem("t_o")
        t_c = sem("t_c")
        c_done = sem("c_done")
        c_new = sem("c_new")
        h_done = sem("h_done")
        x2_done = sem("x2_done")
        ga_s = sem("ga_s")
        ga = sem("ga")
        hp = sem("hp")
        hp_ev = sem("hp_ev")
        bn1_done = sem("bn1_done")
        relu_done = sem("relu_done")
        op = sem("op")
        op_ev = sem("op_ev")
        bn2_done = sem("bn2_done")
        y_v = sem("y_v")
        y_s = sem("y_s")
        x3_done = sem("x3_done")
        wg_ready = sem("wg_ready")
        lg_T = sem("lg_T")
        lg_copied = sem("lg_copied")
        lg = sem("lg")
        lg_exp = sem("lg_exp")
        lg_dif = sem("lg_dif")
        stored = sem("stored")

        block = ctx.enter_context(nc.Block())

        def store_rows(eng, q):
            eng.wait_ge(mix_done, Q * (q + 1))
            c, b0 = q // 8, Q * (q % 8)
            eng.dma_start(out_v[:, c, b0:b0 + Q, :],
                          rows[:, Q * q:Q * q + Q, :]).then_inc(stored, 16)

        @block.sync
        def _(sp):
            for n in range(8):
                c, b0 = n // 4, 8 * (n % 4)
                sp.dma_start(rows[:, c * B + b0:c * B + b0 + 8, :],
                             x_v[:, c, b0:b0 + 8, :]).then_inc(ld_x[n], 16)
            sp.wait_ge(bias_parts, 1)
            for k in range(PARTS):
                sp.dma_start(bp[k:k + 1, :], blp[0:1, k, :]).then_inc(ld_bp, 16)
            sp.wait_ge(zeros_set, 1)
            sp.wait_ge(hi_done, 1)
            for n in range(SB):
                v = x_slots[n].rearrange("(p t) d -> p (t d)", p=P)
                for a in range(0, SLOTS[n], ZERO_TILES):
                    m = min(ZERO_TILES, SLOTS[n] - a) * D
                    sp.dma_start(v[:, a * D:a * D + m], zeros[:, 0:m]).then_inc(slots_zeroed, 16)
            sp.wait_ge(op, GROUPS)
            for e in range(E):
                sp.dma_start(w1e[:, e * F:(e + 1) * F], mW1[e]).then_inc(ld_moe, 16)
            for e in range(E):
                sp.dma_start(w2e[:, e * F:(e + 1) * F].rearrange("p (j d) -> p j d", j=J),
                             mW2[e].rearrange("(j p) d -> p j d", p=P)).then_inc(ld_moe, 16)
            sp.dma_start(b1e, mb1.rearrange("(a e) f -> a (e f)", a=1).to_broadcast([P, E * F])).then_inc(ld_moe, 16)
            sp.dma_start(b2e, mb2.rearrange("(a e) d -> a (e d)", a=1).to_broadcast([P, E * D])).then_inc(ld_moe, 16)

            def load(n, t, u):
                sp.dma_start(x_in[:, u, :], x_slots[n][bass.ds(t * P, P), :]).then_inc(x_loaded[u], 16)

            def first_loads(n):
                sp.wait_ge(scattered[n], 16 * TOP * SIZES[n])
                for t in range(U):
                    if n:
                        sp.wait_ge(x_turned, sum(SLOTS[:n]) - U + t + 1)
                    load(n, t, t)
            first_loads(0)
            base = 0
            for n in range(SB):
                def step(i):
                    for u in range(U):
                        t = U * i + u
                        if not (isinstance(i, int) and i == ROUNDS[n] - 1):
                            sp.wait_ge(x_turned, base + t + 1)
                            load(n, t + U, u)
                        if not (isinstance(i, int) and t < 2):
                            sp.wait_ge(y_done, base + t - 1)
                            v = (u - 2) % U
                            sp.dma_start(y_slots[n][bass.ds((t - 2) * P, P), :],
                                         y_out[:, v, :]).then_inc(y_stored[v], 16)
                staged(sp, ROUNDS[n], step)
                if n + 1 < SB:
                    first_loads(n + 1)
                for t in (SLOTS[n] - 2, SLOTS[n] - 1):
                    sp.wait_ge(y_done, base + t + 1)
                    sp.dma_start(y_slots[n][t * P:(t + 1) * P, :],
                                 y_out[:, t % U, :]).then_inc(y_stored[t % U], 16)
                base += SLOTS[n]
            for q in range(STORED_EARLY, GROUPS):
                store_rows(sp, q)
            sp.wait_ge(stored, 16 * GROUPS)

        @block.gpsimd
        def _(pool):
            nc.gpsimd.memset(ident[:, :], 0.0).then_inc(consts, 1)
            nc.gpsimd.memset(hs[:, 0, :], 0.0).then_inc(consts, 1)
            nc.gpsimd.memset(ones_bf[:, :], 1.0).then_inc(consts, 1)
            nc.gpsimd.memset(h_zero[:, :], 0.0).then_inc(consts, 1)
            nc.gpsimd.iota(pos[:, :], [[-1, E]], base=E, channel_multiplier=0,
                           allow_small_or_imprecise_dtypes=True).then_inc(consts, 1)
            pool.wait_ge(consts, 1)
            nc.gpsimd.affine_select(out=ident[:, :], in_=ident[:, :], compare_op=ALU.not_equal, fill=1.0,
                                    base=0, pattern=[[-1, P]], channel_multiplier=1).then_inc(ident_done, 1)
            nc.gpsimd.memset(zeros, 0.0).then_inc(zeros_set, 1)
            nc.gpsimd.memset(before[:, :], 0.0).then_inc(consts, 1)
            nc.gpsimd.memset(all_ones[:, :], 1.0).then_inc(consts, 1)
            nc.gpsimd.memset(expert[:, :, :], 0).then_inc(consts, 1)
            nc.gpsimd.iota(tile_no[:, :], [[1, max(SLOTS)]], base=0, channel_multiplier=0,
                           allow_small_or_imprecise_dtypes=True).then_inc(consts, 1)
            pool.wait_ge(consts, 7)
            nc.gpsimd.affine_select(out=before[:, :], in_=before[:, :], compare_op=ALU.is_ge, fill=1.0,
                                    base=0, pattern=[[-1, P]], channel_multiplier=1).then_inc(consts, 1)

            pool.wait_ge(gate_done, 2)
            pool.wait_ge(nrm_s[0], GROUPS // 2)
            pool.wait_ge(nrm_v[0], GROUPS // 2)
            steps_ = 0
            for b in range(0, B, 8):
                w, w2 = msg[:, b:b + 8, :], msg2[:, :, :]

                def gate(k):
                    return gates[:, k, B + b:B + b + 8].unsqueeze(2).to_broadcast([P, 8, D])

                def bias(v):
                    return v[:, 1, :].unsqueeze(1).to_broadcast([P, 8, D])
                for out_, a, g in ((w, bias(bout_sb), gate(1)), (w2, bias(bin_sb), gate(0)), (w, w, w2),
                                   (w2, nrm[:, B + b:B + b + 8, :], gate(2)), (w, w, w2)):
                    nc.gpsimd.tensor_tensor(out_, a, g, ALU.add if a is w else ALU.mult).then_inc(msg_step, 1)
                    steps_ += 1
                    pool.wait_ge(msg_step, steps_)

            pool.wait_ge(slots_zeroed, 16 * ZERO_DMAS)
            pool.wait_ge(nrm_s[3], GROUPS // 2)
            for n in range(SB):
                if FIRST[n + 1] > B:
                    pool.wait_ge(nrm_v[3], GROUPS // 2)
                pool.wait_ge(slots_done, TOP * min(n + 1, 2))
                for g in range(FIRST[n], FIRST[n + 1]):
                    for k in range(TOP):
                        nc.gpsimd.indirect_dma_start(
                            x_slots[n], bass.IndirectOffsetOnAxis(ap=slot[:, k, g:g + 1], axis=0),
                            nrm[:, g, :], None).then_inc(scattered[n], 16)
            pool.wait_ge(lg, 2)
            for n in range(SB):
                pool.wait_ge(scattered[n], 16 * TOP * SIZES[n])
            for n in range(SB):
                for u in range(U):
                    pool.wait_ge(y_stored[u], 16 * sum(ROUNDS[:n + 1]))
                for g in range(SIZES[n]):
                    for k in range(TOP):
                        nc.gpsimd.indirect_dma_start(
                            picked[k][:, FIRST[n] + g, :], None, y_slots[n],
                            bass.IndirectOffsetOnAxis(ap=slot[:, k, FIRST[n] + g:FIRST[n] + g + 1], axis=0)
                        ).then_inc(picked_done[n], 16)

        def cols_view(c, i, by_time):
            if not by_time:
                return cols[:, BANK * (i + 8 * c):BANK * (i + 8 * c + 1)]
            v = cols[:, :].rearrange("p (t b) -> p b t", b=B)
            return v[:, Q * i:Q * (i + 1), c * P:(c + 1) * P]

        def rank_banks(n):
            return (ps[:, 0, 0:BANK // 2], ps[:, 0, BANK // 2:]) if n == 1 else (ps[:, 0, :], ps[:, 1, :])

        def load_experts(eng, regs, n, i):
            eng.load(regs, expert[0:1, n, bass.ds(U * i, len(regs))])
            return [eng.snap(r, min_val=0, max_val=E - 1) for r in regs]

        @block.scalar
        def _(act):
            act.dma_start(a_rows[:, :, :], adj.rearrange("(c p) m -> p c m", p=P)).then_inc(ld_adj, 16)
            for k, w in enumerate((gate_w_in, gate_w_out, loop_gate)):
                act.dma_start(gw[:, k:k + 1], w).then_inc(ld_gnn, 16)
            for k, w in enumerate((gate_b_in, gate_b_out)):
                act.dma_start(gb[:, k, :], w.rearrange("(c p) a -> p (c a)", p=P),
                              allow_slow_non_contiguous=True).then_inc(ld_gnn, 16)
            act.dma_start(bin_sb[:, :, :], bias_in.rearrange("(c p) d -> p c d", p=P)).then_inc(ld_gnn, 16)
            act.dma_start(bout_sb[:, :, :], bias_out.rearrange("(c p) d -> p c d", p=P)).then_inc(ld_gnn, 16)
            for k, (u, v, b) in enumerate(((U_i, V_i, b_i), (U_c, V_c, b_c), (U_o, V_o, b_o))):
                act.dma_start(Ux[:, k, :], u).then_inc(ld_lstm, 16)
                act.dma_start(Vx[:, k, :], v).then_inc(ld_lstm, 16)
                act.dma_start(bl[0:1, k * P:(k + 1) * P],
                              b.rearrange("(a n) -> a n", a=1)).then_inc(ld_lstm, 16)
            act.dma_start(w_in[:, 0:2, :], W1.rearrange("(c p) d -> p c d", p=P)).then_inc(ld_bn, 16)
            act.dma_start(w_in[:, 2:4, :], W2.rearrange("o (c h) -> o c h", h=P)).then_inc(ld_bn, 16)
            for k, v in enumerate((b1, g1, be1)):
                act.dma_start(bn1[:, k, :], v.rearrange("(c p) -> p c", p=P),
                              allow_slow_non_contiguous=True).then_inc(ld_small, 16)
            for k, v in enumerate((b2, g2, be2)):
                act.dma_start(bn2[:, k:k + 1], v.rearrange("(p a) -> p a", a=1)).then_inc(ld_small, 16)
            act.dma_start(wg_sb[:, :], Wg).then_inc(ld_small, 16)
            act.dma_start(bg_sb[:, :], bg.rearrange("(a n) -> a n", a=1).to_broadcast([P, E])).then_inc(ld_small, 16)

            def normalise_group(n, q):
                for g in range(Q * q, Q * (q + 1)):
                    last = nc.scalar.activation(
                        (nrm_1 if n == 1 else nrm)[:, g, :], rows[:, g, :], ACT.Identity,
                        bias=nmr[:, g:g + 1], scale=rstd[:, g:g + 1])
                last.then_inc(nrm_s[n], 1)

            def normalise(n, first=0, groups=GROUPS, copied=0, by_time=False):
                act.wait_ge(stat_done[n], 1)
                for q in range(first + 1, max(first + groups, copied + 4 if copied else 0), 2):
                    if q < first + groups:
                        normalise_group(n, q)
                    if 4 <= q < copied + 4:
                        act.wait_ge(tp[n], q - 3)
                        o, v = cols_view(0, q - 4, by_time), ps[:, 4 + (q - 4) % 4, :]
                        nc.scalar.copy(o, v.rearrange("p (b t) -> p b t", b=Q) if by_time else v
                                       ).then_inc(tp_s[n], 1)

            normalise(0, copied=GROUPS // 2)
            def gate_tanh(c):
                act.wait_ge(gate_acc, c + 1)
                nc.scalar.copy(gates_T, ps[0:3 * CG, 2, :]).then_inc(gate_copied, 1)
                act.wait_ge(gate_ps, c + 1)
                lgates = ps[:, 3, 0:3 * B].rearrange("p (t q k) -> p k q t", t=Q, k=3)
                for k in range(3):
                    last = nc.scalar.activation(
                        gates[:, k, c * B:(c + 1) * B].rearrange("p (q t) -> p q t", t=Q), lgates[:, k, :, :],
                        ACT.Tanh,
                        scale=0.5, bias=gbh[:, k, c:c + 1] if k < 2 else 0.0)
                last.then_inc(gate_th, 1)
            act.wait_ge(half_bias, 1)
            gate_tanh(0)
            act.wait_ge(gate_done, 1)
            with act.Fori(0, GROUPS // 4) as i:
                for u in range(2):
                    for t in range(Q):
                        g = bass.ds(2 * Q * i + (Q * u + t), 1)
                        last = nc.scalar.activation(sums[:, g, :].rearrange("p a b -> p (a b)"), bout_sb[:, 0, :],
                                                    ACT.Identity, scale=gates[:, 1, g])
                    last.then_inc(s1_act, 1)
            for q in range(GROUPS // 2):
                act.wait_ge(tp_c1, q + 1)
                nc.scalar.copy(cols_view(1, q, False), ps[:, 6 + q % 2, :]).then_inc(cp_c1, 1)
            gate_tanh(1)
            normalise(1, groups=GROUPS // 2, copied=GROUPS // 2, by_time=True)

            def between(t):
                for start, base, ready, done in ((NORM_1, B, stat_done[4], fill_nrm),
                                                 (NORM_2, 0, stat_done[5], late_nrm)):
                    if start <= t < start + B // 2:
                        if t == start:
                            act.wait_ge(ready, 1)
                        for g in range(base + 2 * (t - start), base + 2 * (t - start) + 2):
                            last = nc.scalar.activation(nrm[:, g, :], rows[:, g, :], ACT.Identity,
                                                        bias=nmr[:, g:g + 1], scale=rstd[:, g:g + 1])
                        last.then_inc(done, 1)

            def steps(i, base=0):
                for s in range(2 * STEPS):
                    bank = 3 * (s // STEPS)
                    col = (s % STEPS) * B
                    t = 2 * STEPS * i + s
                    act.wait_ge(z_ig, t + 1)
                    nc.scalar.activation(T[:, 0:2, :], ps[:, bank:bank + 2, col:col + B],
                                         ACT.Tanh).then_inc(t_ig, 1)
                    act.wait_ge(z_o, t + 1)
                    nc.scalar.activation(T[:, 2, :], ps[:, bank + 2, col:col + B],
                                         ACT.Tanh).then_inc(t_o, 1)
                    act.wait_ge(c_new, t + 1)
                    nc.scalar.activation(tc[:, :], cell[:, :], ACT.Tanh, scale=0.5).then_inc(t_c, 1)
                    between(t)
            for i in range(BLOCKS // 2):
                steps(i)

            act.wait_ge(stat_done[2], 1)
            for q in range(GROUPS // 2, 3 * GROUPS // 4):
                normalise_group(2, q)
            act.wait_ge(ld_small, 128)
            act.wait_ge(slots_zeroed, 16 * ZERO_DMAS)
            for q in range(-2, GROUPS):
                if q + 2 < GROUPS:
                    act.wait_ge(ga, q + 3)
                    nc.scalar.copy(cols[:, BANK * (q + 2):BANK * (q + 3)], ps[:, 4 + (q + 2) % 4, :]).then_inc(ga_s, 1)
                for k in range(HC if q >= 0 else 0):
                    act.wait_ge(hp, HC * q + (k + 1))
                    nc.scalar.activation(h1[:, k, BANK * q:BANK * (q + 1)], ps[:, 2 * (q % 2) + k, :], ACT.Identity,
                                         bias=bn1[:, 0, k:k + 1]).then_inc(hp_ev, 1)
            act.wait_ge(bn1_done, 1)
            with act.Fori(0, GROUPS) as i:
                for k in range(HC):
                    v = h1[:, k, bass.ds(BANK * i, BANK)]
                    nc.scalar.activation(v, v, ACT.Relu, bias=bsh[:, k:k + 1],
                                         scale=bsc[:, k:k + 1]).then_inc(relu_done, 1)
            act.wait_ge(bn2_done, 1)
            with act.Fori(0, GROUPS // 2) as i:
                v = cols[:, bass.ds(2 * BANK * i + BANK, BANK)]
                nc.scalar.activation(v, v, ACT.Identity, bias=bsh[:, HC:HC + 1],
                                     scale=bsc[:, HC:HC + 1]).then_inc(y_s, 1)
            act.wait_ge(stat_done[3], 1)
            for q in range(GROUPS + 2):
                if q < GROUPS // 2:
                    normalise_group(3, q)
                if q >= 2:
                    act.wait_ge(tp[3], q - 1)
                    nc.scalar.copy(cols_view(0, q - 2, False), ps[:, 4 + (q - 2) % 4, :]).then_inc(tp_s[3], 1)
                if q in (COPY_1, GROUPS + 1):
                    n = q != COPY_1
                    act.wait_ge(lg_T, n + 1)
                    if n:
                        act.wait_ge(lg, 1)
                    nc.scalar.copy(logits_T, ps[:, n, :]).then_inc(lg_copied, 1)
            act.wait_ge(lg_dif, 1)
            nc.scalar.activation(m2[:, :], m2[:, :], ACT.Exp).then_inc(lg_exp, 1)

            def copy_x(tg, v, first):
                act.wait_ge(x_turned, tg + 1)
                if not first:
                    act.wait_ge(up_done, tg - 2)
                nc.scalar.copy(x_T[:, v, :], ps[:, 7, 0:D]).then_inc(x_copied, 1)

            def gelu_of(tg, v, first):
                act.wait_ge(turned, tg + 1)
                if not first:
                    act.wait_ge(down_done, tg - 2)
                nc.scalar.activation(h_T[:, v, :], ps[:, 3 + v, :], ACT.Gelu).then_inc(gelu_done, 1)
            base = 0
            for n in range(SB):
                copy_x(base, 0, n == 0)

                def step(i):
                    for u in range(U):
                        t = U * i + u
                        peel = isinstance(i, int)
                        if not (peel and t == SLOTS[n] - 1):
                            copy_x(base + t + 1, (u + 1) % U, peel and n == 0 and t < 2)
                        if not (peel and t == 0):
                            gelu_of(base + t - 1, (u - 1) % U, peel and n == 0 and t < 4)
                if n < SB - 1:
                    staged(act, ROUNDS[n], step)
                else:
                    for i in range(ROUNDS[n]):
                        step(i)
                        if 0 < i <= STORED_EARLY:
                            store_rows(act, i - 1)
                gelu_of(base + SLOTS[n] - 1, (SLOTS[n] - 1) % U, False)
                base += SLOTS[n]

        @block.vector
        def _(dve):
            chain = [0]

            def link(ins, times=1):
                chain[0] += times
                ins.then_inc(dch, 1)
                dve.wait_ge(dch, chain[0])

            def rsqrt_step(k, y, v, t):
                if k == 0:
                    return nc.vector.tensor_scalar(t.bitcast(I32), v.bitcast(I32), 1, None,
                                                   ALU.logical_shift_right)
                if k == 1:
                    return nc.vector.tensor_scalar(y.bitcast(I32), t.bitcast(I32), -1.0, RSQRT_MAGIC,
                                                   ALU.mult, ALU.add)
                if k % 3 == 2:
                    return nc.vector.scalar_tensor_tensor(out=t, in0=y, scalar=-0.5, in1=y,
                                                          op0=ALU.mult, op1=ALU.mult)
                if k % 3 == 0:
                    return nc.vector.tensor_tensor(t, t, v, ALU.mult)
                return nc.vector.scalar_tensor_tensor(out=y, in0=t, scalar=1.5, in1=y,
                                                      op0=ALU.add, op1=ALU.mult)

            def rsqrt(y, v, t):
                for k in range(2 + 3 * NEWTON):
                    link(rsqrt_step(k, y, v, t))

            def row_stats_step(k, g0, g1):
                me, qe = stats[:, g0:g1, 1], stats[:, g0:g1, 2]
                mo, qo = stats[:, g0:g1, 4], stats[:, g0:g1, 5]
                a, b, v, m = (tmp[:, n, g0:g1] for n in range(4))
                if k == 0:
                    return nc.vector.tensor_tensor(a, me, mo, ALU.subtract)
                if k == 1:
                    return nc.vector.tensor_tensor(b, qe, qo, ALU.add)
                if k == 2:
                    return nc.vector.tensor_tensor(a, a, a, ALU.mult)
                if k == 3:
                    return nc.vector.tensor_scalar(b, b, 1.0 / D, EPS, ALU.mult, ALU.add)
                if k == 4:
                    return nc.vector.scalar_tensor_tensor(out=v, in0=a, scalar=0.25, in1=b,
                                                          op0=ALU.mult, op1=ALU.add)
                if k == 5:
                    return nc.vector.tensor_tensor(m, me, mo, ALU.add)
                if k < CHAIN - 1:
                    return rsqrt_step(k - 6, rstd[:, g0:g1], v, a)
                return nc.vector.scalar_tensor_tensor(out=nmr[:, g0:g1], in0=m, scalar=-0.5,
                                                      in1=rstd[:, g0:g1], op0=ALU.mult, op1=ALU.mult)

            def degrees_step(k):
                rowsum, colsum, diag = small[:, 0:2], small[:, 2:4], small[:, 4:6]
                if k == 0:
                    return nc.vector.tensor_copy(s_rows[:, :, :], a_rows[:, :, :])
                if k in (1, 2):
                    v = s_rows[:, k - 1, (k - 1) * P:k * P]
                    return nc.vector.tensor_tensor(v, v, ident[:, :], ALU.add)
                if k == 3:
                    return nc.vector.tensor_reduce(rowsum, s_rows[:, :, :], AX.X, ALU.add)
                if k == 4:
                    return nc.vector.tensor_reduce(colsum, a_T[:, :, :], AX.X, ALU.add)
                if k in (5, 6):
                    return nc.vector.tensor_tensor(work[:, 0, k - 5, :], a_rows[:, k - 5, (k - 5) * P:(k - 4) * P],
                                                   ident[:, :], ALU.mult)
                if k == 7:
                    return nc.vector.tensor_reduce(diag, work[:, 0, 0:2, :], AX.X, ALU.add)
                if k == 8:
                    return nc.vector.tensor_tensor(rowsum, rowsum, colsum, ALU.add)
                if k == 9:
                    return nc.vector.tensor_tensor(rowsum, rowsum, diag, ALU.subtract)
                if k < DEGREES - C:
                    return rsqrt_step(k - 10, small[:, 6:8], rowsum, small[:, 8:10])
                c = k - (DEGREES - C)
                return nc.vector.tensor_scalar(s_rows[:, c, :], s_rows[:, c, :], small[:, 6 + c:7 + c],
                                               None, ALU.mult)

            def row_stats(n, g0=0, g1=TILES, times=1):
                for k in range(CHAIN - 1):
                    link(row_stats_step(k, g0, g1))
                row_stats_step(CHAIN - 1, g0, g1).then_inc(stat_done[n], 1)
                dve.wait_ge(stat_done[n], times)

            def normalise_group(n, q):
                for g in range(Q * q, Q * (q + 1)):
                    last = nc.vector.tensor_scalar(
                        (nrm_1 if n == 1 else nrm)[:, g, :], rows[:, g, :], rstd[:, g:g + 1],
                        nmr[:, g:g + 1], ALU.mult, ALU.add)
                last.then_inc(nrm_v[n], 1)

            def normalise(n, first=0, groups=GROUPS, copied=0, by_time=False, beside=None):
                for q in range(first, max(first + groups, copied + 4 if copied else 0), 2):
                    if q < first + groups:
                        normalise_group(n, q)
                    if 4 <= q < copied + 4:
                        dve.wait_ge(tp[n], q - 3)
                        o, v = cols_view(0, q - 4, by_time), ps[:, 4 + (q - 4) % 4, :]
                        nc.vector.tensor_copy(o, v.rearrange("p (b t) -> p b t", b=Q) if by_time else v
                                              ).then_inc(tp_v[n], 1)
                    if beside is not None:
                        beside(q)

            def tiles_stats(g0=0, g1=TILES):
                for g in range(g0, g1):
                    last = nc.vector.bn_stats(stats[:, g, :], rows[:, g, :])
                link(last)

            for n in range(8):
                dve.wait_ge(ld_x[n], 16)
                for g in range(8 * n, 8 * n + 8):
                    last = nc.vector.bn_stats(stats[:, g, :], rows[:, g, :])
            link(last)
            row_stats(0)
            dve.wait_ge(ld_gnn, 16 * 7)
            nc.vector.tensor_scalar(gbh[:, :, :], gb[:, :, :], 0.5, None, ALU.mult).then_inc(half_bias, 1)
            link(nc.vector.memset(gw_wide[:, :], 0.0))
            nc.vector.tensor_copy(gw_wide[:, 3 * (CG - 1):3 * CG], gw[:, :]).then_inc(gw_ready, 1)
            def split(parts, whole, rest):
                link(nc.vector.tensor_copy(parts[0], whole))
                link(nc.vector.tensor_tensor(rest, whole, parts[0], ALU.subtract))
                link(nc.vector.tensor_copy(parts[1], rest))
                link(nc.vector.tensor_tensor(rest, rest, parts[1], ALU.subtract))
                return nc.vector.tensor_copy(parts[2], rest)

            def prepare(q):
                if q == PREP[0]:
                    dve.wait_ge(ld_lstm, 16 * 9)
                    for k, half in enumerate((0.5, 1.0, 0.5)):
                        nc.vector.tensor_scalar(Ux[:, k, :], Ux[:, k, :], half, None, ALU.mult)
                        nc.vector.tensor_scalar(Vx[:, k, :], Vx[:, k, :], 0.5 * half, None, ALU.mult)
                        last = nc.vector.tensor_scalar(bl[0:1, k * P:(k + 1) * P], bl[0:1, k * P:(k + 1) * P],
                                                       half, None, ALU.mult)
                    link(last)

                if q == PREP[1]:
                    split([blp[0:1, k, :] for k in range(PARTS)], bl[0:1, :], res[0:1, :]).then_inc(bias_parts, 1)
                if q == PREP[2]:
                    dve.wait_ge(bias_parts, 1)
                    split([Vp[:, k, :] for k in range(PARTS)], Vx[:, :, :].rearrange("p k h -> p (k h)"),
                          res[:, :]).then_inc(lstm_w, 1)
                if q == PREP[3]:
                    dve.wait_ge(prep_T, 1)
                    link(nc.vector.tensor_copy(a_T[:, :, :].rearrange("p c n -> p (c n)"), ps[:, 0, :]))
                    dve.wait_ge(prep_T, 2)
                    nc.vector.tensor_copy(w_T[:, :, :].rearrange("p c n -> p (c n)"), ps[:, 1, :]).then_inc(prep_used, 1)
            normalise(0, copied=GROUPS // 2, beside=prepare)
            def finish_gates(c):
                g = gates[:, :, c * B:(c + 1) * B]
                dve.wait_ge(gate_th, c + 1)
                link(nc.vector.tensor_scalar(g[:, 0:3, :], g[:, 0:3, :], 0.5, 0.5, ALU.mult, ALU.add))
                nc.vector.tensor_tensor(g[:, 3, :], g[:, 0, :], g[:, 1, :], ALU.add).then_inc(gate_done, 1)
            finish_gates(0)
            dve.wait_ge(gate_done, 1)

            def messages(i, v):
                gs = [bass.ds(2 * Q * i + t, 1) for t in range(2 * Q)]
                w = [sums[:, g, :].rearrange("p a b -> p (a b)") for g in gs]
                dve.wait_ge(s1_act, 2 * i + 2)
                for t in range(2 * Q):
                    last = nc.vector.scalar_tensor_tensor(out=w[t], in0=bin_sb[:, 0, :], scalar=gates[:, 0, gs[t]],
                                                          in1=w[t], op0=ALU.mult, op1=ALU.add)
                last.then_inc(mstep, 1)
                dve.wait_ge(mstep, 3 * i + 1)
                for t in range(2 * Q):
                    last = nc.vector.scalar_tensor_tensor(
                        out=w[t], in0=nrm[:, gs[t], :].rearrange("p a b -> p (a b)"),
                        scalar=gates[:, 2, gs[t]], in1=w[t], op0=ALU.mult, op1=ALU.add)
                last.then_inc(mstep, 1)
                dve.wait_ge(mstep, 3 * i + 2)
                dve.wait_ge(agg, 2 * i + 2)
                for t in range(2 * Q):
                    last = nc.vector.scalar_tensor_tensor(
                        out=w[t], in0=ps[:, 4 * v + t // Q, (t % Q) * D:(t % Q + 1) * D],
                        scalar=gates[:, 3, gs[t]], in1=w[t], op0=ALU.mult, op1=ALU.add)
                last.then_inc(mstep, 1)
                dve.wait_ge(mstep, 3 * i + 3)
                for u in range(2):
                    g = bass.ds(2 * Q * i + Q * u, Q)
                    nc.vector.scalar_tensor_tensor(out=rows[:, g, :], in0=sums[:, g, :], scalar=0.0,
                                                   in1=rows[:, g, :], op0=ALU.max,
                                                   op1=ALU.add).then_inc(s1_free, 1)
            for i in range(GROUPS // 4):
                messages(i, i % 2)
                if i == 2:
                    finish_gates(1)
            dve.wait_ge(s1_free, GROUPS // C)
            tiles_stats(0, B)
            row_stats(1, 0, B)
            normalise(1, groups=GROUPS // 2, copied=GROUPS // 2, by_time=True)

            dve.wait_ge(tp_s[1], GROUPS // 4)
            link(nc.vector.memset(cell, 0.0))
            dve.wait_ge(consts, 5)

            def between(t):
                j = (t - AGG_1 - 2) // 2
                even = (t - AGG_1) % 2 == 0
                if even and 0 <= j < B:
                    if j % 8 == 0:
                        dve.wait_ge(msg_step, 5 * (j // 8 + 1))
                    dve.wait_ge(fill_agg, j + 1)
                    nc.vector.scalar_tensor_tensor(out=msg[:, j, :], in0=ps[:, 6, 0:D],
                                                   scalar=gates[:, 3, B + j:B + j + 1], in1=msg[:, j, :],
                                                   op0=ALU.mult, op1=ALU.add).then_inc(fill_msg, 1)
                if even and 1 <= j <= B:
                    dve.wait_ge(fill_x, j)
                    last = nc.vector.bn_stats(stats[:, B + j - 1, :], rows[:, B + j - 1, :])
                    if j == B:
                        last.then_inc(fill_chain, 1)
                if not even and 0 <= j < B:
                    dve.wait_ge(fill_msg, j + 1)
                    nc.vector.scalar_tensor_tensor(out=rows[:, B + j, :], in0=msg[:, j, :], scalar=0.0,
                                                   in1=rows[:, B + j, :], op0=ALU.max,
                                                   op1=ALU.add).then_inc(fill_x, 1)
                for start, g0, done, links in ((FINISH_1, B, stat_done[4], 0),
                                               (FINISH_2, 0, stat_done[5], CHAIN)):
                    k = t - start
                    if 0 <= k < CHAIN:
                        dve.wait_ge(fill_chain, links + k + 1)
                        row_stats_step(k, g0, g0 + B).then_inc(done if k == CHAIN - 1 else fill_chain, 1)
                k = t - ADJ
                if 0 <= k < DEGREES:
                    if k:
                        dve.wait_ge(fill_adj, k)
                    degrees_step(k).then_inc(fill_adj, 1)
                c = k - DEGREES - 1
                if 0 <= c < C:
                    dve.wait_ge(fill_adj_T, c + 1)
                    nc.vector.tensor_scalar(ah_T[:, c, :], ps[:, 6, 0:N], small[:, 6 + c:7 + c], None,
                                            ALU.mult).then_inc(ah_done, 1)
                j = t - NORM_1 - 2
                if 0 <= j < B // 2:
                    dve.wait_ge(fill_T, j + 1)
                    v = cols[:, :].rearrange("p (t b) -> p b t", b=B)
                    nc.vector.tensor_copy(v[:, 2 * j:2 * j + 2, P:2 * P],
                                          ps[:, 6, 0:2 * P].rearrange("p (b t) -> p b t", b=2)
                                          ).then_inc(fill_cols, 1)
                j = t - X2_2 - 1
                if 0 <= j < B:
                    dve.wait_ge(late_T, j + 1)
                    nc.vector.scalar_tensor_tensor(out=rows[:, j, :], in0=ps[:, 6, 0:D], scalar=0.5,
                                                   in1=rows[:, j, :], op0=ALU.mult,
                                                   op1=ALU.add).then_inc(late_x, 1)
                if 1 <= j <= B:
                    dve.wait_ge(late_x, j)
                    last = nc.vector.bn_stats(stats[:, j - 1, :], rows[:, j - 1, :])
                    if j == B:
                        last.then_inc(fill_chain, 1)

            def steps(i):
                for s in range(2 * STEPS):
                    t = 2 * STEPS * i + s
                    nc.vector.scalar_tensor_tensor(out=hc[:, :], in0=hs[:, bass.ds(t, 1), :].rearrange("p a b -> p (a b)"),
                                                   scalar=0.5, in1=cell[:, :], op0=ALU.mult,
                                                   op1=ALU.mult).then_inc(c_done, 1)
                    between(t)
                    dve.wait_ge(t_ig, t + 1)
                    nc.vector.scalar_tensor_tensor(out=ig[:, :], in0=T[:, 0, :], scalar=1.0, in1=T[:, 1, :],
                                                   op0=ALU.add, op1=ALU.mult).then_inc(c_done, 1)
                    dve.wait_ge(c_done, 2 * t + 2)
                    nc.vector.tensor_tensor(cell[:, :], hc[:, :], ig[:, :], ALU.add).then_inc(c_new, 1)
                    dve.wait_ge(t_o, t + 1)
                    dve.wait_ge(t_c, t + 1)
                    nc.vector.scalar_tensor_tensor(out=h_hi[:, :], in0=T[:, 2, :],
                                                   scalar=1.0, in1=tc[:, :], op0=ALU.add,
                                                   op1=ALU.mult).then_inc(hi_done, 1)
                    nc.vector.scalar_tensor_tensor(out=hs[:, t + 1, :], in0=T[:, 2, :],
                                                   scalar=1.0, in1=tc[:, :], op0=ALU.add,
                                                   op1=ALU.mult).then_inc(h_done, 1)
                    dve.wait_ge(h_done, t + 1)
                    nc.vector.tensor_tensor(h_lo[:, :], hs[:, t + 1, :], h_hi[:, :],
                                            ALU.subtract).then_inc(lo_done, 1)
            for i in range(BLOCKS // 2):
                steps(i)

            dve.wait_ge(ld_small, 128)
            link(nc.vector.memset(wg_wide, 0.0))
            nc.vector.tensor_copy(wg_wide[:, E * (GROUPS - 1):E * GROUPS], wg_sb[:, :]).then_inc(wg_ready, 1)
            for half in range(2):
                q0 = half * GROUPS // 4
                for q in range(q0, q0 + GROUPS // 4):
                    dve.wait_ge(tp[2], q + 1)
                    v = rows[:, B + Q * q:B + Q * (q + 1), :].rearrange("p a b -> p (a b)")
                    nc.vector.scalar_tensor_tensor(out=v, in0=ps[:, (4 + q) % 8, :], scalar=0.5, in1=v,
                                                   op0=ALU.mult, op1=ALU.add).then_inc(x2_done, 1)
                g0, g1 = B + Q * q0, B + Q * (q0 + GROUPS // 4)
                dve.wait_ge(x2_done, q0 + GROUPS // 4)
                tiles_stats(g0, g1)
                row_stats(2, g0, g1, half + 1)
            for q in range(3 * GROUPS // 4, GROUPS):
                normalise_group(2, q)
            for q in range(GROUPS):
                for k in range(HC):
                    dve.wait_ge(hp_ev, HC * q + (k + 1))
                    last = nc.vector.bn_stats(bst[:, k, q, :], h1[:, k, BANK * q:BANK * (q + 1)])
            link(last)

            def bn_finish(ks, gamma, beta, done):
                n = len(ks)
                k0 = ks[0]
                for k in ks:
                    last = nc.vector.bn_aggr(mv[:, k, :], bst[:, k, :, :].rearrange("p g s -> p (g s)"))
                link(last)
                link(nc.vector.tensor_scalar(small[:, 0:n], mv[:, k0:k0 + n, 1], EPS, None, ALU.add))
                rsqrt(small[:, 2:2 + n], small[:, 0:n], small[:, 4:4 + n])
                link(nc.vector.tensor_tensor(bsc[:, k0:k0 + n], small[:, 2:2 + n], gamma, ALU.mult))
                link(nc.vector.tensor_tensor(small[:, 0:n], mv[:, k0:k0 + n, 0], bsc[:, k0:k0 + n], ALU.mult))
                nc.vector.tensor_tensor(bsh[:, k0:k0 + n], beta, small[:, 0:n],
                                        ALU.subtract).then_inc(done, 1)
                dve.wait_ge(done, 1)
            dve.wait_ge(ld_small, 128)
            bn_finish([0, 1], bn1[:, 1, :], bn1[:, 2, :], bn1_done)
            with dve.Fori(0, GROUPS // 2) as i:
                for u in range(2):
                    dve.wait_ge(op, 2 * i + (u + 1))
                    v = cols[:, bass.ds(2 * BANK * i + BANK * u, BANK)]
                    nc.vector.tensor_scalar(v, ps[:, 2 + u, :], bn2[:, 0:1], None, ALU.add).then_inc(op_ev, 1)
                    dve.wait_ge(op_ev, 2 * i + (u + 1))
                    last = nc.vector.bn_stats(bst[:, HC, bass.ds(2 * i + u, 1), :].rearrange("p a b -> p (a b)"), v)
            link(last, GROUPS // 2)
            bn_finish([2], bn2[:, 1:2], bn2[:, 2:3], bn2_done)
            with dve.Fori(0, GROUPS // 2) as i:
                v = cols[:, bass.ds(2 * BANK * i, BANK)]
                nc.vector.tensor_scalar(v, v, bsc[:, HC:HC + 1], bsh[:, HC:HC + 1],
                                        ALU.mult, ALU.add).then_inc(y_v, 1)
            with dve.Fori(0, GROUPS // 4) as i:
                for u in range(4):
                    dve.wait_ge(tp[4], 4 * i + (u + 1))
                    v = rows[:, :, :].rearrange("p (c b) d -> p b c d", c=C)[:, bass.ds(8 * i + 2 * u, 2), :, :]
                    s = ps[:, 4 + u, :].rearrange("p (b c d) -> p b c d", b=2, c=C)
                    nc.vector.tensor_tensor(v, v, s, ALU.add).then_inc(x3_done, 1)
            dve.wait_ge(x3_done, GROUPS)
            tiles_stats(0, B)
            row_stats(3, 0, B)
            tiles_stats(B, TILES)
            row_stats(3, B, TILES, 2)
            def take_logits(n, q0, q1):
                dve.wait_ge(lg, n + 1)
                link(nc.vector.tensor_tensor(
                    logit[:, Q * q0:Q * q1, :].rearrange("p (q t) e -> p q t e", t=Q),
                    ps[:, 2 + n, :].rearrange("p (t q e) -> p q t e", t=Q, e=E)[:, q0:q1, :, :],
                    bg_sb[:, :].unsqueeze(1).unsqueeze(1).to_broadcast([P, q1 - q0, Q, E]), ALU.add))

            def pick_experts(g0, g1):
                n = g1 - g0
                lo = logit[:, g0:g1, :]
                first, second, scratch = (v[:, g0:g1, :] for v in mk)

                def over(v):
                    return v.unsqueeze(2).to_broadcast([P, n, E])

                def each(v):
                    return v.unsqueeze(1).to_broadcast([P, n, E])

                def first_of(mask, m):
                    link(nc.vector.tensor_tensor(scratch, lo, over(m), ALU.is_equal))
                    link(nc.vector.tensor_tensor(scratch, scratch, each(pos[:, :]), ALU.mult))
                    link(nc.vector.tensor_reduce(tmp[:, 0, g0:g1], scratch, AX.X, ALU.max))
                    link(nc.vector.tensor_tensor(mask, scratch, over(tmp[:, 0, g0:g1]), ALU.is_equal))
                link(nc.vector.tensor_reduce(m1[:, g0:g1], lo, AX.X, ALU.max))
                first_of(first, m1[:, g0:g1])
                link(nc.vector.scalar_tensor_tensor(out=lo, in0=first, scalar=-1e30, in1=lo,
                                                    op0=ALU.mult, op1=ALU.add))
                link(nc.vector.tensor_reduce(m2[:, g0:g1], lo, AX.X, ALU.max))
                first_of(second, m2[:, g0:g1])

            def mark_experts(g0, g1):
                first, second = (v[:, g0:g1, :].rearrange("p g e -> p (g e)") for v in mk[0:2])
                nc.vector.tensor_tensor(mark[:, g0 * E:g1 * E], first, second, ALU.add).then_inc(marked, 1)

            def place(n0, n1, done):
                g0, g1 = FIRST[n0], FIRST[n1]
                tiles, blocks = g1 - g0, n1 - n0
                rank, tot = (v[:, g0:g1, :].rearrange("p g e -> p (g e)") for v in (mk[2], logit))
                rs = [v[:, 0:tiles * E] for v in run]
                dve.wait_ge(ranked, done)
                within, whole = rank_banks(done)
                nc.vector.tensor_copy(rank, within[:, 0:tiles * E])
                link(nc.vector.tensor_copy(tot, whole[:, 0:tiles * E]))
                link(nc.vector.tensor_copy(rs[0], tot))
                src, dst, step = 0, 1, 1
                while step < tiles:
                    nc.vector.tensor_copy(rs[dst][:, 0:step * E], rs[src][:, 0:step * E])
                    link(nc.vector.tensor_tensor(rs[dst][:, step * E:], rs[src][:, step * E:],
                                                 rs[src][:, :(tiles - step) * E], ALU.add))
                    src, dst, step = dst, src, 2 * step
                upto = [rs[src][:, (FIRST[n + 1] - g0 - 1) * E:(FIRST[n + 1] - g0) * E] for n in range(n0, n1)]
                w = blocks * E
                count, sum_a, sum_b = (ends[:, k, 0:w] for k in range(3))
                last = nc.vector.tensor_copy(ends[:, 0, 0:E], upto[0])
                for n in range(1, blocks):
                    last = nc.vector.tensor_tensor(ends[:, 0, n * E:(n + 1) * E], upto[n], upto[n - 1],
                                                   ALU.subtract)
                link(last)
                link(nc.vector.tensor_scalar(iends[:, 0:w], count, float(P - 1), None, ALU.add))
                link(nc.vector.tensor_scalar(iends[:, 0:w], iends[:, 0:w], 7, None, ALU.arith_shift_right))
                nc.vector.tensor_copy(count, iends[:, 0:w])
                link(nc.vector.tensor_copy(sum_a, iends[:, 0:w]))
                a, b, step = sum_a, sum_b, 1
                while step < E:
                    va, vb = (v.rearrange("p (s e) -> p s e", s=blocks) for v in (a, b))
                    nc.vector.tensor_copy(vb[:, :, 0:step], va[:, :, 0:step])
                    link(nc.vector.tensor_tensor(vb[:, :, step:], va[:, :, step:], va[:, :, :E - step], ALU.add))
                    a, b, step = b, a, 2 * step
                end = a
                link(nc.vector.tensor_tensor(count, end, count, ALU.subtract))
                link(nc.vector.tensor_scalar(count, count, float(P), None, ALU.mult))
                if blocks > 1:
                    for n in range(1, blocks):
                        v = ends[:, 0, n * E:(n + 1) * E]
                        last = nc.vector.tensor_tensor(v, v, upto[n - 1], ALU.subtract)
                    link(last)
                link(nc.vector.tensor_tensor(rank, rank, rs[src], ALU.add))
                link(nc.vector.tensor_tensor(rank, rank, tot, ALU.subtract))
                for n in range(n0, n1):
                    v = mk[2][:, FIRST[n]:FIRST[n + 1], :]
                    first = ends[:, 0, (n - n0) * E:(n - n0 + 1) * E]
                    last = nc.vector.tensor_tensor(
                        v, v, first.unsqueeze(1).to_broadcast([P, SIZES[n], E]), ALU.add)
                link(last)
                for k in range(TOP):
                    link(nc.vector.tensor_tensor(mk[k][:, g0:g1, :], mk[k][:, g0:g1, :],
                                                 mk[2][:, g0:g1, :], ALU.mult))
                    link(nc.vector.tensor_reduce(tmp[:, 3, g0:g1], mk[k][:, g0:g1, :], AX.X, ALU.add))
                    nc.vector.tensor_copy(slot[:, k, g0:g1], tmp[:, 3, g0:g1]).then_inc(slots_done, 1)
                    dve.wait_ge(slots_done, TOP * (done - 1) + k + 1)
                for n in range(n0, n1):
                    ts = SLOTS[n]
                    v = run_table[0:1, 0:ts, :]
                    link(nc.vector.tensor_tensor(
                        v, tile_no[:, 0:ts].unsqueeze(2).to_broadcast([1, ts, E]),
                        end[0:1, (n - n0) * E:(n - n0 + 1) * E].unsqueeze(1).to_broadcast([1, ts, E]),
                        ALU.is_ge))
                    link(nc.vector.tensor_reduce(tmp[0:1, 3, 0:ts], v, AX.X, ALU.add))
                    nc.vector.tensor_scalar(expert[0:1, n, U - 1:U - 1 + ts], tmp[0:1, 3, 0:ts],
                                            float(E - 1), None, ALU.min).then_inc(experts_known, 1)
                    dve.wait_ge(experts_known, n + 1)

            def route_early(q):
                if q == ROUTE_1:
                    take_logits(0, 0, EARLY)
                    pick_experts(0, FIRST[1])
                    mark_experts(0, FIRST[1])
                if q == ROUTE_2:
                    place(0, 1, 1)
            for q in range(GROUPS // 2, GROUPS):
                normalise_group(3, q)
                route_early(q)
            take_logits(1, EARLY, GROUPS)
            pick_experts(FIRST[1], TILES)
            mark_experts(FIRST[1], TILES)
            nc.vector.tensor_tensor(m2[:, :], m2[:, :], m1[:, :], ALU.subtract).then_inc(lg_dif, 1)
            place(1, SB, 2)
            dve.wait_ge(lg_exp, 1)
            link(nc.vector.tensor_scalar(tmp[:, 0, :], m2[:, :], 1.0, None, ALU.add))
            link(nc.vector.reciprocal(tmp[:, 1, :], tmp[:, 0, :]))
            link(nc.vector.tensor_tensor(tmp[:, 2, :], tmp[:, 1, :], m2[:, :], ALU.mult))
            weight = [tmp[:, 1, :], tmp[:, 2, :]]
            dve.wait_ge(ld_moe, 16 * (2 * E + 2))

            e_regs = [dve.alloc_register(f"dve_e{n}") for n in range(2 * U - 1)]

            def add_bias(tg, v, e, first):
                dve.wait_ge(up_done, tg + 1)
                if not first:
                    dve.wait_ge(turned, tg - 2)
                nc.vector.tensor_tensor(h_pre[:, v, :], ps[:, v, :], b1e[:, bass.ds(e * F, F)],
                                        ALU.add).then_inc(biased, 1)

            def finish_rows(tg, rounds, v, e, first):
                dve.wait_ge(down_done, tg + 1)
                if not first:
                    dve.wait_ge(y_stored[v], 16 * rounds)
                nc.vector.tensor_tensor(y_out[:, v, :], ps[:, 6, 0:D], b2e[:, bass.ds(e * D, D)],
                                        ALU.add).then_inc(y_done, 1)

            def mix(n, g, m):
                for k in range(TOP):
                    for a in range(m):
                        at = bass.ds(FIRST[n] + a + g, 1)
                        r = rows[:, at, :].rearrange("p a d -> p (a d)")
                        nc.vector.scalar_tensor_tensor(
                            out=r, in0=picked[k][:, at, :].rearrange("p a d -> p (a d)"),
                            scalar=weight[k][:, at], in1=r,
                            op0=ALU.mult, op1=ALU.add).then_inc((mix_step, mix_done)[k], 1)
                    if k == 0:
                        dve.wait_ge(mix_step, FIRST[n] + m + g)
            base = 0
            for n in range(SB):
                def step(i, beside=None):
                    es = load_experts(dve, e_regs, n, i)
                    for u in range(U):
                        t = U * i + u
                        peel = isinstance(i, int)
                        add_bias(base + t, u, es[u + 2], peel and n == 0 and t < 3)
                        if not (peel and t < 2):
                            r = i + sum(ROUNDS[:n]) + (1 if u == 2 else 0) - 1
                            finish_rows(base + t - 2, r, (u - 2) % U, es[u], peel and n == 0 and t < 5)
                        if beside is not None:
                            beside(u)
                if n != 2:
                    staged(dve, ROUNDS[n], step)
                else:
                    step(0)
                    step(1)
                    dve.wait_ge(picked_done[0], 16 * TOP * SIZES[0])
                    with dve.Fori(2, 2 + SIZES[0]) as i:
                        step(i)
                        mix(0, i - 2, 1)
                    start = 2 + SIZES[0]
                    step(start)
                    start += 1
                    dve.wait_ge(picked_done[1], 16 * TOP * SIZES[1])
                    with dve.Fori(start, ROUNDS[n] - 1) as i:
                        step(i, lambda u: mix(1, U * i + (u - U * start), 1))
                    step(ROUNDS[n] - 1)
                    mixed_tiles = U * (ROUNDS[n] - 1 - start)
                    mix(1, mixed_tiles, SIZES[1] - mixed_tiles)
                es = load_experts(dve, e_regs, n, ROUNDS[n])
                for t in (SLOTS[n] - 2, SLOTS[n] - 1):
                    finish_rows(base + t, sum(ROUNDS[:n + 1]) - 1, t % U, es[t - SLOTS[n] + 2], False)
                base += SLOTS[n]
            for n in (2, 3):
                dve.wait_ge(picked_done[n], 16 * TOP * SIZES[n])
                mix(n, 0, SIZES[n])

        @block.tensor
        def _(pe):
            def transposes(n, source, ready, groups=GROUPS, then=None):
                for q in range(groups + LAG * (then is not None)):
                    if q >= LAG and then is not None:
                        h = q - LAG
                        pe.wait_ge(tp_v[n] if h % 2 == 0 else tp_s[n], h // 2 + 1)
                        then(h)
                    if q >= groups:
                        continue
                    ready(q)
                    if q >= 4:
                        if q % 2 == 0:
                            pe.wait_ge(tp_v[n], (q - 4) // 2 + 1)
                        else:
                            pe.wait_ge(tp_s[n], (q - 5) // 2 + 1)
                    for t in range(Q):
                        last = nc.tensor.transpose(ps[:, 4 + q % 4, t * P:(t + 1) * P], source(q, t),
                                                   ident[:, :])
                    last.then_inc(tp[n], 1)

            def normalised(n):
                def ready(q):
                    pe.wait_ge(nrm_v[n] if q % 2 == 0 else nrm_s[n], q // 2 + 1)
                return ready

            pe.wait_ge(ident_done, 1)
            pe.wait_ge(ld_adj, 16)
            for cm in range(C):
                for cn in range(C):
                    last = nc.tensor.transpose(ps[:, 0, (cm * C + cn) * P:(cm * C + cn + 1) * P],
                                               a_rows[:, cn, cm * P:(cm + 1) * P], ident[:, :])
            last.then_inc(prep_T, 1)
            pe.wait_ge(ld_bn, 32)
            for k in range(4):
                last = nc.tensor.transpose(ps[:, 1, k * P:(k + 1) * P], w_in[:, k, :], ident[:, :])
            last.then_inc(prep_T, 1)
            def gate_logits(q):
                k = q % CG
                mm = nc.tensor.matmul(ps[0:3 * CG, 2, :], gw_wide[:, 3 * (CG - 1 - k):3 * (2 * CG - 1 - k)],
                                      cols[:, BANK * q:BANK * (q + 1)], start=k == 0, stop=k == CG - 1)
                if k == CG - 1:
                    mm.then_inc(gate_acc, 1)

            def turn_gates(c):
                pe.wait_ge(gate_copied, c + 1)
                for t in range(Q):
                    last = nc.tensor.transpose(ps[:, 3, 3 * CG * t:3 * CG * (t + 1)],
                                               gates_T[:, t * P:(t + 1) * P], ident[0:3 * CG, 0:3 * CG])
                last.then_inc(gate_ps, 1)

            def aggregate(q):
                if q >= 4 and q % 2 == 0:
                    pe.wait_ge(mstep, 3 * (q // 2 - 1))
                for cm in range(C):
                    last = nc.tensor.matmul(
                        ps[:, 4 * (q // 2 % 2) + q % 2, :], a_T[:, cm, 0:P],
                        nrm[:, cm * B + Q * q:cm * B + Q * (q + 1), :].rearrange("p a b -> p (a b)"),
                        start=(cm == 0), stop=(cm == C - 1))
                last.then_inc(agg, 1)
            pe.wait_ge(gw_ready, 1)
            transposes(0, lambda q, t: nrm[:, Q * q + t, :], normalised(0), GROUPS // 2, gate_logits)
            turn_gates(0)
            pe.wait_ge(prep_used, 1)
            pe.wait_ge(nrm_v[0], GROUPS // 2)
            pe.wait_ge(nrm_s[0], GROUPS // 2)
            for q in range(4):
                aggregate(q)
            pe.wait_ge(gate_th, 1)
            half = GROUPS // 2
            for q in range(half + 2):
                if q >= 2:
                    pe.wait_ge(cp_c1, q - 1)
                    gate_logits(half + q - 2)
                if q < half:
                    for t in range(Q):
                        last = nc.tensor.transpose(ps[:, 6 + q % 2, t * P:(t + 1) * P],
                                                   nrm[:, B + Q * q + t, :], ident[:, :])
                    last.then_inc(tp_c1, 1)
                if q in (3, 7):
                    aggregate(q + 1 if q == 3 else 6)
                    aggregate(q + 2 if q == 3 else 7)
            turn_gates(1)
            transposes(1, lambda q, t: nrm_1[:, Q * q + t, :], normalised(1), GROUPS // 2)

            def gate_inputs(blk, bank0, k, quarter):
                o = ps[:, bank0 + k, quarter * P:(quarter + 1) * P]
                nc.tensor.matmul(o, bp[:, k * P:(k + 1) * P], ones_bf[:, :], start=(quarter == 0),
                                 stop=True, skip_group_check=True)
                return nc.tensor.matmul(o, Ux[:, k, :], cols[:, bass.ds(blk * BANK + quarter * P, P)],
                                        start=False, stop=True, skip_group_check=True)
            pe.wait_ge(lstm_w, 1)
            pe.wait_ge(ld_bp, 16 * PARTS)
            pe.wait_ge(consts, 5)
            pe.wait_ge(tp_v[1], GROUPS // 4)
            pe.wait_ge(tp_s[1], GROUPS // 4)
            for k in range(GATES):
                for quarter in range(Q):
                    gate_inputs(0, 0, k, quarter)

            def between(t):
                j, cm = (t - AGG_1) // 2, (t - AGG_1) % 2
                if 0 <= j < B:
                    if j and cm == 0:
                        pe.wait_ge(fill_msg, j)
                    mm = nc.tensor.matmul(ps[:, 6, 0:D], a_T[:, cm, P:2 * P], nrm[:, cm * B + j, :],
                                          start=(cm == 0), stop=(cm == 1))
                    if cm:
                        mm.then_inc(fill_agg, 1)
                j = t - NORM_1 - 1
                if 0 <= j < B // 2:
                    pe.wait_ge(fill_nrm, j + 1)
                    if j:
                        pe.wait_ge(fill_cols, j)
                    for a in range(2):
                        mm = nc.tensor.transpose(ps[:, 6, a * P:(a + 1) * P],
                                                 nrm[:, B + 2 * j + a, :], ident[:, :])
                    mm.then_inc(fill_T, 1)
                c = t - ADJ - DEGREES
                if 0 <= c < C:
                    pe.wait_ge(fill_adj, DEGREES)
                    if c:
                        pe.wait_ge(ah_done, c)
                    for cn in range(C):
                        mm = nc.tensor.transpose(ps[:, 6, cn * P:(cn + 1) * P],
                                                 s_rows[:, cn, c * P:(c + 1) * P], ident[:, :])
                    mm.then_inc(fill_adj_T, 1)
                j = t - X2_2
                if 0 <= j < B:
                    if j:
                        pe.wait_ge(late_x, j)
                    nc.tensor.transpose(ps[:, 6, 0:P], hs[:, 1:1 + P, j],
                                        ident[:, :]).then_inc(late_T, 1)

            def steps(i, last_round):
                for s in range(2 * STEPS):
                    bank0 = 3 * (s // STEPS)
                    col = (s % STEPS) * B
                    t = 2 * STEPS * i + s

                    def product(k, h, last=None):
                        for part in range(PARTS):
                            mm = nc.tensor.matmul(ps[:, bank0 + k, col:col + B],
                                                  Vp[:, part, k * P:(k + 1) * P], h[:, :],
                                                  start=False, stop=True, skip_group_check=True)
                        if last is not None:
                            mm.then_inc(last, 1)
                    if t:
                        pe.wait_ge(hi_done, t)
                        for k in range(GATES):
                            product(k, h_hi)
                        pe.wait_ge(lo_done, t)
                    for k in range(GATES):
                        product(k, h_lo if t else h_zero, (None, z_ig, z_o)[k])
                    if t == N // C - STEPS:
                        pe.wait_ge(fill_cols, B // 2)
                    piece = s % STEPS
                    if piece < GATES * Q and not (last_round and s >= STEPS):
                        gate_inputs(2 * i + (s // STEPS + 1), 3 - bank0, piece // Q, piece % Q)
                    between(t)
            steps(0, False)
            for i in range(1, BLOCKS // 2 - 1):
                steps(i, False)
            steps(BLOCKS // 2 - 1, True)

            pe.wait_ge(h_done, N)

            for q in range(GROUPS // 2):
                for t in range(Q):
                    last = nc.tensor.transpose(ps[:, (4 + q) % 8, t * P:(t + 1) * P],
                                               hs[:, 1 + P:1 + 2 * P, Q * q + t], ident[:, :])
                last.then_inc(tp[2], 1)
            pe.wait_ge(late_nrm, B // 2)
            pe.wait_ge(ah_done, C)
            for q in range(GROUPS + 2):
                if q < GROUPS:
                    if q < GROUPS // 2:
                        pe.wait_ge(nrm_s[2], q // 2 + 1)
                    else:
                        pe.wait_ge(nrm_v[2], (q - GROUPS // 2) // 2 + 1)
                    if q >= 4:
                        pe.wait_ge(ga_s, q - 3)
                    for t in range(2):
                        b = 2 * q + t
                        for cm in range(C):
                            last = nc.tensor.matmul(ps[:, 4 + q % 4, t * N:(t + 1) * N],
                                                    nrm[:, cm * B + b, :], ah_T[:, cm, :],
                                                    start=(cm == 0), stop=(cm == C - 1))
                    last.then_inc(ga, 1)
                h = q - 2
                if h >= 0:
                    pe.wait_ge(ga_s, h + 1)
                    if h == 0:
                        pe.wait_ge(x2_done, GROUPS // 2)
                    for k in range(HC):
                        if h >= 2:
                            pe.wait_ge(hp_ev, HC * (h - 2) + k + 1)
                        nc.tensor.matmul(ps[:, 2 * (h % 2) + k, :], w_T[:, k, :],
                                         cols[:, BANK * h:BANK * (h + 1)], start=True, stop=True).then_inc(hp, 1)

            def output_layer(i):
                for u in range(2):
                    if not isinstance(i, int):
                        pe.wait_ge(op_ev, 2 * i + (u - 1))
                    for k in range(HC):
                        pe.wait_ge(relu_done, 4 * i + (2 * u + k + 1))
                        last = nc.tensor.matmul(ps[:, 2 + u, :], w_T[:, 2 + k, :],
                                                h1[:, k, bass.ds(2 * BANK * i + BANK * u, BANK)],
                                                start=(k == 0), stop=(k == HC - 1))
                    last.then_inc(op, 1)
            peeled(pe, GROUPS // 2, output_layer)
            for q in range(GROUPS):
                pe.wait_ge(y_v if q % 2 == 0 else y_s, q // 2 + 1)
                if q >= 4:
                    pe.wait_ge(x3_done, q - 3)
                for t in range(Q):
                    last = nc.tensor.transpose(ps[:, 4 + q % 4, t * P:(t + 1) * P],
                                               cols[:, (Q * q + t) * P:(Q * q + t + 1) * P], ident[:, :])
                last.then_inc(tp[4], 1)
            pe.wait_ge(ld_small, 128)

            def rank_marks(g0, g1, n):
                pe.wait_ge(marked, n)
                w = (g1 - g0) * E
                within, whole = rank_banks(n)
                nc.tensor.matmul(within[:, 0:w], before[:, :], mark[:, g0 * E:g1 * E],
                                 start=True, stop=True)
                nc.tensor.matmul(whole[:, 0:w], all_ones[:, :], mark[:, g0 * E:g1 * E],
                                 start=True, stop=True).then_inc(ranked, 1)
            pe.wait_ge(consts, 10)

            def turn_logits(n):
                pe.wait_ge(lg_copied, n + 1)
                for t in range(Q):
                    last = nc.tensor.transpose(ps[:, 2 + n, t * P:(t + 1) * P], logits_T[:, t * P:(t + 1) * P],
                                               ident[:, :])
                last.then_inc(lg, 1)

            def router_logits(q):
                n = q >= EARLY
                mm = nc.tensor.matmul(ps[:, n, :], wg_wide[:, E * (GROUPS - 1 - q):E * (2 * GROUPS - 1 - q)],
                                      cols[:, BANK * q:BANK * (q + 1)], start=q in (0, EARLY),
                                      stop=q in (EARLY - 1, GROUPS - 1))
                if q in (EARLY - 1, GROUPS - 1):
                    mm.then_inc(lg_T, 1)
                if q == TURN_1:
                    turn_logits(0)
                if q == RANK_1:
                    rank_marks(0, FIRST[1], 1)
            pe.wait_ge(wg_ready, 1)
            for q in range(GROUPS + LAG):
                if q >= LAG:
                    pe.wait_ge(tp_s[3], q - LAG + 1)
                    router_logits(q - LAG)
                if q < GROUPS:
                    if q < GROUPS // 2:
                        pe.wait_ge(nrm_s[3], q + 1)
                    else:
                        pe.wait_ge(nrm_v[3], q - GROUPS // 2 + 1)
                    for t in range(Q):
                        last = nc.tensor.transpose(ps[:, 4 + q % 4, t * P:(t + 1) * P], nrm[:, Q * q + t, :],
                                                   ident[:, :])
                    last.then_inc(tp[3], 1)
            turn_logits(1)
            rank_marks(FIRST[1], TILES, 2)
            pe.wait_ge(ld_moe, 16 * (2 * E + 2))
            pe.wait_ge(experts_known, SB)
            e_regs = [pe.alloc_register(f"pe_e{n}") for n in range(U * PER_LOAD + U - 1)]

            def turn_x(tg, rounds, v, first):
                pe.wait_ge(x_loaded[v], 16 * rounds)
                if not first:
                    pe.wait_ge(x_copied, tg)
                nc.tensor.transpose(ps[:, 7, 0:P], x_in[:, v, :], ident[:, :]).then_inc(x_turned, 1)

            def up(tg, v, e, first):
                pe.wait_ge(x_copied, tg + 1)
                if not first:
                    pe.wait_ge(biased, tg - 2)
                nc.tensor.matmul(ps[:, v, :], x_T[:, v, :], w1e[:, bass.ds(e * F, F)],
                                 start=True, stop=True).then_inc(up_done, 1)

            def turn_h(tg, v, first):
                pe.wait_ge(biased, tg + 1)
                if not first:
                    pe.wait_ge(gelu_done, tg - 2)
                for j in range(J):
                    last = nc.tensor.transpose(ps[:, 3 + v, j * P:(j + 1) * P],
                                               h_pre[:, v, j * P:(j + 1) * P], ident[:, :])
                last.then_inc(turned, 1)

            def down(tg, v, e, first):
                pe.wait_ge(gelu_done, tg + 1)
                if not first:
                    pe.wait_ge(y_done, tg)
                for j in range(J):
                    last = nc.tensor.matmul(ps[:, 6, 0:D], h_T[:, v, j * P:(j + 1) * P],
                                            w2e[:, bass.ds(e * F + j * D, D)],
                                            start=(j == 0), stop=(j == J - 1))
                last.then_inc(down_done, 1)
            base = 0
            for n in range(SB):
                done = sum(ROUNDS[:n])
                turn_x(base, done + 1, 0, n == 0)

                def step(i, es=None):
                    if es is None:
                        es = load_experts(pe, e_regs[0:2 * U - 1], n, i)
                    for u in range(U):
                        t = U * i + u
                        peel = isinstance(i, int)
                        if not (peel and t == SLOTS[n] - 1):
                            turn_x(base + t + 1, i + (done + 1 + (u == U - 1)), (u + 1) % U, False)
                        up(base + t, u, es[u + 2], peel and n == 0 and t < 3)
                        if not (peel and t < 1):
                            turn_h(base + t - 1, (u - 1) % U, peel and n == 0 and t < 4)
                        if not (peel and t < 2):
                            down(base + t - 2, (u - 2) % U, es[u], peel and n == 0 and t < 3)
                step(0)
                step(1)
                with pe.Fori(0, (ROUNDS[n] - 3) // PER_LOAD) as i:
                    es = load_experts(pe, e_regs, n, PER_LOAD * i + 2)
                    for k in range(PER_LOAD):
                        step(PER_LOAD * i + (2 + k), es[U * k:U * k + 2 * U - 1])
                step(ROUNDS[n] - 1)
                es = load_experts(pe, e_regs[0:2 * U - 1], n, ROUNDS[n])
                turn_h(base + SLOTS[n] - 1, (SLOTS[n] - 1) % U, False)
                for t in (SLOTS[n] - 2, SLOTS[n] - 1):
                    down(base + t, t % U, es[t - SLOTS[n] + 2], False)
                base += SLOTS[n]


_ARGS = {"x": "x", "adj": "adj"}
_ARGS |= {k: "L0_gnn_" + k for k in ("bias_in", "bias_out", "gate_w_in", "gate_b_in", "gate_w_out",
                                    "gate_b_out", "loop_gate")}
_ARGS |= {k: "L0_ffn_" + k for k in ("U_i", "V_i", "b_i", "U_c", "V_c", "b_c", "U_o", "V_o", "b_o")}
_ARGS |= {k: "L1_gnn_" + k for k in ("W1", "b1", "g1", "be1", "W2", "b2", "g2", "be2")}
_ARGS |= {"Wg": "L1_ffn_Wg", "bg": "L1_ffn_bg", "mW1": "L1_ffn_W1", "mb1": "L1_ffn_b1",
          "mW2": "L1_ffn_W2", "mb2": "L1_ffn_b2"}


def kernel(**inputs):
    import numpy as np
    import concourse.bacc as bacc
    from concourse.bass_utils import run_bass_kernel_spmd

    nc = bacc.Bacc("TRN2", target_bir_lowering=False, num_devices=1)
    arrays, args = {}, {}
    for arg, name in _ARGS.items():
        a = np.ascontiguousarray(inputs[name])
        arrays[name] = a
        args[arg] = nc.dram_tensor(name, a.shape, mybir.dt.from_np(a.dtype), kind="ExternalInput").ap()
    out = nc.dram_tensor("out", (B, N, D), F32, kind="ExternalOutput").ap()
    build(nc, out=out, **args)
    r = run_bass_kernel_spmd(nc, [arrays], core_ids=[0])
    return r.results[0]["out"]
```
